# Optimizing a Trainium2 kernel written in Bass

```python
import numpy as np
import jax
import jax.numpy as jnp

def _softmax(x, axis=-1):
    return jax.nn.softmax(x, axis=axis)

def _gelu(x):
    return jax.nn.gelu(x, approximate=True)

def _silu(x):
    return jax.nn.silu(x)

def _sigmoid(x):
    return jax.nn.sigmoid(x)

def _layernorm(x, axis=-1, eps=1e-05):
    m = jnp.mean(x, axis=axis, keepdims=True)
    v = jnp.var(x, axis=axis, keepdims=True)
    return (x - m) / jnp.sqrt(v + eps)

def _scatter_add(tgt, idx, src, axis=0):
    return tgt.at[idx].add(src)

def _segment_sum(src, seg, n):
    return jax.ops.segment_sum(src, seg, n)
kernel_name = 'mk_vit_tower_cls_d1_tok_img768_r4_f83ebf'

def setup_inputs(seed: int=0):
    np.random.seed(seed)
    _w = jnp.asarray

    def _rec_inputs():
        import jax
        import jax.numpy as jnp
        _rk = jax.random.key(seed)
        x = -0.000356955 + 1 * jax.random.normal(jax.random.fold_in(_rk, 1), (16, 3, 128, 128), jnp.float32)
        cls_tok = 0.02 * jax.random.normal(jax.random.fold_in(_rk, 5), (1, 1, 192), jnp.float32)
        return (x, cls_tok)
    x, cls_tok = _rec_inputs()

    def _L0_tok_setup():
        import jax, jax.numpy as jnp
        import numpy as np
        IMG = 224
        PATCH = 16
        C_IN = 3
        EMB = 192
        B = 128
        K = PATCH * PATCH * C_IN

        def _patchify(x):
            Bn, C, H, Wd = x.shape
            nH, nW = (H // PATCH, Wd // PATCH)
            x = x.reshape(Bn, C, nH, PATCH, nW, PATCH)
            x = x.transpose(0, 2, 4, 3, 5, 1)
            return x.reshape(Bn, nH * nW, PATCH * PATCH * C)
        key = jax.random.key(seed)
        k1, k2 = jax.random.split(key)
        x = jax.random.normal(k1, (B, C_IN, IMG, IMG), dtype=jnp.float32)
        W = jax.random.normal(k2, (EMB, K), dtype=jnp.float32) * (1.0 / np.sqrt(K))
        b = jnp.zeros((EMB,), dtype=jnp.float32)
        return {'x': x, 'W': W, 'b': b}
    _L0_tok_all = _L0_tok_setup()
    _L0_tok_in = {k: v for k, v in _L0_tok_all.items() if k in ('W', 'b')}
    del _L0_tok_all

    def _L0_attn_setup():
        import jax, jax.numpy as jnp
        import numpy as np
        import math

        def closest_square_factors(N):
            s = int(math.isqrt(N))
            for i in range(s, 0, -1):
                if N % i == 0:
                    return (i, N // i)

        def landmark_pool(t, num_landmarks):
            B, H, N, Dh = t.shape
            w1, w2 = closest_square_factors(N - 1)
            h, w = closest_square_factors(num_landmarks)
            assert w1 % h == 0 and w2 % w == 0
            cls = t[:, :, :1, :]
            rest = t[:, :, 1:, :].reshape(B, H, h, w1 // h, w, w2 // w, Dh)
            pooled = rest.mean(axis=(3, 5)).reshape(B, H, num_landmarks, Dh)
            return jnp.concatenate([cls, pooled], axis=2)

        def moore_penrose_iter_pinv(x, iters=6):
            abs_x = jnp.abs(x)
            col = abs_x.sum(axis=-1)
            row = abs_x.sum(axis=-2)
            z = jnp.swapaxes(x, -1, -2) / (jnp.max(col) * jnp.max(row) + 1e-15)
            I = jnp.eye(x.shape[-1], dtype=x.dtype)
            for _ in range(iters):
                xz = x @ z
                z = 0.25 * z @ (13.0 * I - xz @ (15.0 * I - xz @ (7.0 * I - xz)))
            return z
        key = jax.random.key(seed)
        k0, k1, k2 = jax.random.split(key, 3)
        B, N, C = (32, 1025, 192)
        x = jax.random.normal(k0, (B, N, C), dtype=jnp.float32)
        qkv_w = jax.random.normal(k1, (C, 3 * C), dtype=jnp.float32) * 0.02
        qkv_b = jnp.zeros((3 * C,), dtype=jnp.float32)
        proj_w = jax.random.normal(k2, (C, C), dtype=jnp.float32) * 0.02
        proj_b = jnp.zeros((C,), dtype=jnp.float32)
        return {'x': x, 'qkv_w': qkv_w, 'qkv_b': qkv_b, 'proj_w': proj_w, 'proj_b': proj_b}
    _L0_attn_all = _L0_attn_setup()
    _L0_attn_in = {k: v for k, v in _L0_attn_all.items() if k in ('qkv_w', 'qkv_b', 'proj_w', 'proj_b')}
    del _L0_attn_all

    def _L0_ffn_setup():
        import jax, jax.numpy as jnp
        import numpy as np
        TOP_K = 2

        def _moe(x, Wg, bg, W1, b1, W2, b2):
            B, S, D = x.shape
            E = Wg.shape[1]
            logits = x @ Wg + bg
            top_vals, top_idx = jax.lax.top_k(logits, TOP_K)
            gates_k = jax.nn.softmax(top_vals, axis=-1)
            one_hot = jax.nn.one_hot(top_idx, E, dtype=x.dtype)
            gates = jnp.sum(one_hot * gates_k[..., None], axis=-2)
            flat_x = x.reshape(-1, D)
            flat_g = gates.reshape(-1, E).T

            def body(acc, p):
                W1e, b1e, W2e, b2e, ge = p
                h = jax.nn.relu(flat_x @ W1e + b1e)
                acc = acc + (h @ W2e + b2e) * ge[:, None]
                return (acc, None)
            out, _ = jax.lax.scan(body, jnp.zeros_like(flat_x), (W1, b1, W2, b2, flat_g))
            return out.reshape(B, S, D)
        key = jax.random.key(seed)
        k = jax.random.split(key, 5)
        B, S, D, E, H = (8, 512, 192, 8, 768)
        init = lambda kk, shape: jax.random.normal(kk, shape, jnp.float32) * 0.02
        return {'x': jax.random.normal(k[0], (B, S, D), jnp.float32), 'Wg': init(k[1], (D, E)), 'bg': jnp.zeros((E,), jnp.float32), 'W1': init(k[2], (E, D, H)), 'b1': jnp.zeros((E, H), jnp.float32), 'W2': init(k[3], (E, H, D)), 'b2': jnp.zeros((E, D), jnp.float32)}
    _L0_ffn_all = _L0_ffn_setup()
    _L0_ffn_in = {k: v for k, v in _L0_ffn_all.items() if k in ('Wg', 'bg', 'W1', 'b1', 'W2', 'b2')}
    del _L0_ffn_all
    return {'x': x, 'cls_tok': cls_tok, 'L0_tok_W': _L0_tok_in['W'], 'L0_tok_b': _L0_tok_in['b'], 'L0_attn_qkv_w': _L0_attn_in['qkv_w'], 'L0_attn_qkv_b': _L0_attn_in['qkv_b'], 'L0_attn_proj_w': _L0_attn_in['proj_w'], 'L0_attn_proj_b': _L0_attn_in['proj_b'], 'L0_ffn_Wg': _L0_ffn_in['Wg'], 'L0_ffn_bg': _L0_ffn_in['bg'], 'L0_ffn_W1': _L0_ffn_in['W1'], 'L0_ffn_b1': _L0_ffn_in['b1'], 'L0_ffn_W2': _L0_ffn_in['W2'], 'L0_ffn_b2': _L0_ffn_in['b2']}

def reference(x, cls_tok, L0_tok_W, L0_tok_b, L0_attn_qkv_w, L0_attn_qkv_b, L0_attn_proj_w, L0_attn_proj_b, L0_ffn_Wg, L0_ffn_bg, L0_ffn_W1, L0_ffn_b1, L0_ffn_W2, L0_ffn_b2):
    import jax
    import jax.numpy as jnp

    def _L0_tok_ref(x, W, b):
        import jax, jax.numpy as jnp
        import numpy as np
        IMG = 224
        PATCH = 16
        C_IN = 3
        EMB = 192
        B = 128
        K = PATCH * PATCH * C_IN

        def _patchify(x):
            Bn, C, H, Wd = x.shape
            nH, nW = (H // PATCH, Wd // PATCH)
            x = x.reshape(Bn, C, nH, PATCH, nW, PATCH)
            x = x.transpose(0, 2, 4, 3, 5, 1)
            return x.reshape(Bn, nH * nW, PATCH * PATCH * C)
        patches = _patchify(x)
        return jnp.einsum('bnk,ek->bne', patches, W) + b

    def _L0_attn_ref(x, qkv_w, qkv_b, proj_w, proj_b):
        import jax, jax.numpy as jnp
        import numpy as np
        import math

        def closest_square_factors(N):
            s = int(math.isqrt(N))
            for i in range(s, 0, -1):
                if N % i == 0:
                    return (i, N // i)

        def landmark_pool(t, num_landmarks):
            B, H, N, Dh = t.shape
            w1, w2 = closest_square_factors(N - 1)
            h, w = closest_square_factors(num_landmarks)
            assert w1 % h == 0 and w2 % w == 0
            cls = t[:, :, :1, :]
            rest = t[:, :, 1:, :].reshape(B, H, h, w1 // h, w, w2 // w, Dh)
            pooled = rest.mean(axis=(3, 5)).reshape(B, H, num_landmarks, Dh)
            return jnp.concatenate([cls, pooled], axis=2)

        def moore_penrose_iter_pinv(x, iters=6):
            abs_x = jnp.abs(x)
            col = abs_x.sum(axis=-1)
            row = abs_x.sum(axis=-2)
            z = jnp.swapaxes(x, -1, -2) / (jnp.max(col) * jnp.max(row) + 1e-15)
            I = jnp.eye(x.shape[-1], dtype=x.dtype)
            for _ in range(iters):
                xz = x @ z
                z = 0.25 * z @ (13.0 * I - xz @ (15.0 * I - xz @ (7.0 * I - xz)))
            return z
        num_heads, num_landmarks, pinv_iters = (12, 64, 6)
        B, N, C = x.shape
        Dh = C // num_heads
        scale = Dh ** (-0.5)
        qkv = (x @ qkv_w + qkv_b).reshape(B, N, 3, num_heads, Dh).transpose(2, 0, 3, 1, 4)
        q, k, v = (qkv[0] * scale, qkv[1], qkv[2])
        q_m = landmark_pool(q, num_landmarks)
        k_m = landmark_pool(k, num_landmarks)
        S_A = q @ jnp.swapaxes(k_m, -1, -2)
        S_C = q_m @ jnp.swapaxes(k, -1, -2)
        S_B = q_m @ jnp.swapaxes(k_m, -1, -2)
        maxC = S_C.max(axis=-1, keepdims=True)
        expA = jnp.exp(S_A - S_A.max(axis=-1, keepdims=True))
        expC = jnp.exp(S_C - maxC)
        expB = jnp.exp(jnp.maximum(S_B - maxC, -88.0))
        v_aug = jnp.concatenate([v, jnp.ones_like(v[..., :1])], axis=-1)
        pinv = moore_penrose_iter_pinv(expB, pinv_iters)
        prod = expA @ (pinv @ (expC @ v_aug))
        ctx = prod[..., :-1] / jnp.maximum(prod[..., -1:], 1e-08)
        ctx = ctx.transpose(0, 2, 1, 3).reshape(B, N, C)
        return ctx @ proj_w + proj_b

    def _L0_ffn_ref(x, Wg, bg, W1, b1, W2, b2):
        import jax, jax.numpy as jnp
        import numpy as np
        TOP_K = 2

        def _moe(x, Wg, bg, W1, b1, W2, b2):
            B, S, D = x.shape
            E = Wg.shape[1]
            logits = x @ Wg + bg
            top_vals, top_idx = jax.lax.top_k(logits, TOP_K)
            gates_k = jax.nn.softmax(top_vals, axis=-1)
            one_hot = jax.nn.one_hot(top_idx, E, dtype=x.dtype)
            gates = jnp.sum(one_hot * gates_k[..., None], axis=-2)
            flat_x = x.reshape(-1, D)
            flat_g = gates.reshape(-1, E).T

            def body(acc, p):
                W1e, b1e, W2e, b2e, ge = p
                h = jax.nn.relu(flat_x @ W1e + b1e)
                acc = acc + (h @ W2e + b2e) * ge[:, None]
                return (acc, None)
            out, _ = jax.lax.scan(body, jnp.zeros_like(flat_x), (W1, b1, W2, b2, flat_g))
            return out.reshape(B, S, D)
        return _moe(x, Wg, bg, W1, b1, W2, b2)
    h = _L0_tok_ref(x, L0_tok_W, L0_tok_b)
    h = jnp.concatenate([jnp.broadcast_to(cls_tok, (h.shape[0], 1, h.shape[2])), h], axis=1)
    h = h + _L0_attn_ref(_layernorm(h, axis=-1), L0_attn_qkv_w, L0_attn_qkv_b, L0_attn_proj_w, L0_attn_proj_b)
    h = h + _L0_ffn_ref(_layernorm(h, axis=-1), L0_ffn_Wg, L0_ffn_bg, L0_ffn_W1, L0_ffn_b1, L0_ffn_W2, L0_ffn_b2)
    return h

_drawn_inputs = setup_inputs


def setup_inputs(seed=0):
    import zlib

    import numpy as np

    out = dict(_drawn_inputs(seed))
    spreads = {'L0_tok_b': (0.0, 0.1),
     'L0_attn_qkv_b': (0.0, 0.1),
     'L0_attn_proj_b': (0.0, 0.1),
     'L0_ffn_bg': (0.0, 0.1),
     'L0_ffn_b1': (0.0, 0.297),
     'L0_ffn_b2': (0.0, 0.1)}
    factors = {'cls_tok': 8.0, 'L0_attn_qkv_w': 3.742}
    for name, (base, spread) in spreads.items():
        noise = np.random.default_rng([zlib.crc32(name.encode()), seed]).standard_normal(out[name].shape)
        drawn = base * np.exp(spread * noise) if base else spread * noise
        out[name] = jnp.asarray(drawn.astype(out[name].dtype))
    for name, factor in factors.items():
        out[name] = (out[name] * factor).astype(out[name].dtype)
    return out
```

```python
import concourse.bass as bass
from concourse import mybir
from contextlib import ExitStack

F32 = mybir.dt.float32
U32 = mybir.dt.uint32
ALU = mybir.AluOpType
ACT = mybir.ActivationFunctionType
AX = mybir.AxisListType

B = 16
C_IN, IMG, PATCH = 3, 128, 16
NPATCH = (IMG // PATCH) ** 2
N = NPATCH + 1
D = 192
DH_, DL_ = 128, D - 128
KT = PATCH * PATCH * C_IN // 128
H, DH = 12, 16
HH = H // 2
CH = HH * DH
VA = DH + 1
XW = N + VA
PAIRS = B // 2
ITERS = 6
E, HID = 8, 768
MT = HID // 128
TILES = PAIRS + 1
NTOK = B * N
ROWS = 128
BLK = (384, 384, 2 * 128 + B)
BOFF = (0, 384, 768)
EPS = 1e-5

BETA = 92.0 / 13.0
KAPPA = (1.0 / (256.0 * BETA)) ** (1.0 / 3.0)
CV = 13.0 / (112.0 * KAPPA)


def build(nc, xp, cls_tok, tok_w, tok_b, qkv_w, qk_b, v_b, proj_w, proj_b, wg, bg, w1, b1, w2, b2, out):
    ctx = ExitStack()
    with ctx:
        def sb(name, shape, dt=F32):
            return ctx.enter_context(nc.sbuf_tensor(name, shape, dt))

        def sem(name):
            return ctx.enter_context(nc.semaphore(name))

        tokw = sb("tokw", [128, KT, D])
        tokb = sb("tokb", [128, D])
        wqkv_h = sb("wqkv_h", [DH_, 3 * D])
        wqkv_l = sb("wqkv_l", [DL_, 3 * D])
        qkb = sb("qkb", [CH, 4])
        qbs = sb("qbs", [CH, 2])
        vb = sb("vb", [128, D])
        wp_h = sb("wp_h", [DH_, D])
        wp_l = sb("wp_l", [DL_, D])
        pb = sb("pb", [128, D])
        wg_h = sb("wg_h", [DH_, E])
        wg_l = sb("wg_l", [DL_, E])
        bgb = sb("bgb", [128, E])
        b2t = sb("b2t", [E, D])
        ident = sb("ident", [128, 128])
        ones = sb("ones", [1, N])
        mask = sb("mask", [CH, HH])
        hid = sb("hid", [128, TILES, D])
        mv = sb("mv", [128, TILES, 2])
        rstd = sb("rstd", [128, TILES])
        stat = sb("stat", [128, TILES, 6])
        patch = [sb(f"patch{s}", [128, KT, 128]) for s in range(2)]
        xn = sb("xn", [128, D])
        xncls = sb("xncls", [B, D])
        xT_h = sb("xT_h", [DH_, 2, N])
        xT_l = sb("xT_l", [DL_, 2, N])
        qT = sb("qT", [ROWS, 2, 2, N])
        kT = sb("kT", [CH, 2, 2, N])
        kbd = sb("kbd", [ROWS, 2, 2, HH, N])
        rmax = sb("rmax", [N, 2, H])
        sdiff = [sb(f"sdiff{m}", [N, H, N]) for m in range(2)]
        xexp = [sb(f"xexp{m}", [N, H, N]) for m in range(2)]
        xtv = [sb(f"xtv{m}", [ROWS, H, XW]) for m in range(2)]
        big = sb("big", [128, B * H * N])
        gall = big[0:N, :].rearrange("p (g n) -> p g n", n=N)
        wall = sb("wall", [ROWS, B * H, VA])
        csum = sb("csum", [N, B * H])
        mx2 = sb("mx2", [N, 2])
        grow = sb("grow", [1, 4])
        grow2 = sb("grow2", [1, 2])
        cscale = sb("cscale", [N, 1])
        T = [sb(f"T{c}", [ROWS, HH, N]) for c in range(4)]
        Qs = [sb(f"Qs{c}", [ROWS, HH, N]) for c in range(4)]
        Sm = [sb(f"Sm{c}", [ROWS, HH, N]) for c in range(4)]
        V = [sb(f"V{c}", [N, HH, N]) for c in range(4)]
        Fin = [sb(f"Fin{c}", [ROWS, HH, N]) for c in range(4)]
        den = sb("den", [N, 2, H])
        rden = sb("rden", [N, 2, H])
        ctxv = sb("ctxv", [N, 2, D])
        cT_h = sb("cT_h", [DH_, 2, NPATCH])
        cT_l = sb("cT_l", [DL_, 2, NPATCH])
        cTc_h = sb("cTc_h", [DH_, B])
        cTc_l = sb("cTc_l", [DL_, B])
        mv2 = sb("mv2", [128, TILES, 2])
        rstd2 = sb("rstd2", [128, TILES])
        stat2 = sb("stat2", [128, TILES, 6])
        x2 = [sb(f"x2_{p}", [128, D]) for p in range(2)]
        x2T_h = sb("x2T_h", [DH_, NTOK])
        x2T_l = sb("x2T_l", [DL_, NTOK])
        logit = sb("logit", [128, TILES, E])
        top = sb("top", [128, TILES, 8])
        topi = sb("topi", [128, TILES, 8], U32)
        topf = sb("topf", [128, TILES, 2])
        gk = sb("gk", [128, 4, TILES])
        eidx_i = sb("eidx_i", [128, E], mybir.dt.int32)
        eidx = sb("eidx", [128, E])
        eq = sb("eq", [128, 2, TILES, E])
        gate = sb("gate", [128, TILES, E])
        gateT = sb("gateT", [E, NTOK])
        w1h = [sb(f"w1h{p}", [DH_, HID]) for p in range(2)]
        w1l = [sb(f"w1l{p}", [DL_, HID]) for p in range(2)]
        b1s = [sb(f"b1s{p}", [128, MT]) for p in range(2)]
        w2s = [sb(f"w2s{p}", [128, MT, D]) for p in range(2)]
        hT = [big[:, MT * BLK[0] * p:MT * BLK[0] * (p + 1)].rearrange("p (m n) -> p m n", m=MT) for p in range(2)]

        sx = [ctx.enter_context(nc.psum_tensor(f"sx{m}", [128, 2, 512], F32)) for m in range(2)]
        bank = [ctx.enter_context(nc.psum_tensor(f"bank{b}", [128, 512], F32)) for b in range(4)]
        half_heads = [sx[m][0:N, :, 0:HH * N].rearrange("p b (h n) -> p b h n", n=N) for m in range(2)]
        gram = [sx[m][0:N, :, 0:HH * XW].rearrange("p b (h n) -> p b h n", n=XW) for m in range(2)]
        L1 = [sx[q // 2][:, q % 2, :] for q in range(4)]
        P = [sx[c // 2][0:N, c % 2, 0:HH * N] for c in range(4)]

        def sems(prefix, n):
            return [sem(f"{prefix}{k}") for k in range(n)]

        w_in, consts_in = sem("w_in"), sem("consts_in")
        patch_in, cls_in = sems("patch_in", 2), sem("cls_in")
        ident_zero, ident_ok, mask_one, mask_half, mask_ok, eidx_ok = (
            sem(n) for n in ("ident_zero", "ident_ok", "mask_one", "mask_half", "mask_ok", "eidx_ok"))
        zero_ok, tiles_zero = sem("zero_ok"), sem("tiles_zero")
        ones_ok, vones_ok, mv_init, qbs_ok, logit_zero = (
            sem(n) for n in ("ones_ok", "vones_ok", "mv_init", "qbs_ok", "logit_zero"))
        emb_done, emb_free, hid_ok, stat_ok, mv_ok = (
            sem(n) for n in ("emb_done", "emb_free", "hid_ok", "stat_ok", "mv_ok"))
        eps_ok, sqrt_ok, rstd_ok = (sem(n) for n in ("eps_ok", "sqrt_ok", "rstd_ok"))
        xncls_ok, clsT_done, clsT_ok, xn_ok, xnT_done, xT_ok = (
            sem(n) for n in ("xncls_ok", "clsT_done", "clsT_ok", "xn_ok", "xnT_done", "xT_ok"))
        qk_done, v_done, q_ok, k_ok, kbd_ok, vx_ok = (
            sem(n) for n in ("qk_done", "v_done", "q_ok", "k_ok", "kbd_ok", "vx_ok"))
        score_done, rmax_ok, diff_ok, clamp_ok, exp_ok = (
            sem(n) for n in ("score_done", "rmax_ok", "diff_ok", "clamp_ok", "exp_ok"))
        xt_done, xtv_ok, csum_ok, gram_done, g_ok, w_ok = (
            sem(n) for n in ("xt_done", "xtv_ok", "csum_ok", "gram_done", "g_ok", "w_ok"))
        gmax_ok, gmaxT_done, gmax1_ok, gprod_ok, geps_ok, grec_ok, gscale_ok, gbc_done, cscale_ok = (
            sem(n) for n in ("gmax_ok", "gmaxT_done", "gmax1_ok", "gprod_ok", "geps_ok", "grec_ok", "gscale_ok",
                             "gbc_done", "cscale_ok"))
        t_ok, p1_done, qs_ok, sm_ok, v_ok, p2_done, fin_ok = (
            sems(n, 4) for n in ("t_ok", "p1_done", "qs_ok", "sm_ok", "v_ok", "p2_done", "fin_ok"))
        hb_ok, wv_done, den_ok, rden_ok, ctx_ok, ctxT_done, cT_ok, proj_done, h2_ok, stat2_ok, mv2_ok = (
            sem(n) for n in ("hb_ok", "wv_done", "den_ok", "rden_ok", "ctx_ok", "ctxT_done", "cT_ok", "proj_done",
                             "h2_ok", "stat2_ok", "mv2_ok"))
        eps2_ok, sqrt2_ok, rstd2_ok, x2_ok, x2T_done, x2T_ok = (
            sem(n) for n in ("eps2_ok", "sqrt2_ok", "rstd2_ok", "x2_ok", "x2T_done", "x2T_ok"))
        logit_done, logit_ok, top_ok, topi_ok, topf_ok, gdiff_ok, gexp_ok = (
            sem(n) for n in ("logit_done", "logit_ok", "top_ok", "topi_ok", "topf_ok", "gdiff_ok", "gexp_ok"))
        gden_ok, gate1_ok, gate2_ok, eq_ok, eqg_ok, gate_ok, gateT_done, gateT_ok, b2_done = (
            sem(n) for n in ("gden_ok", "gate1_ok", "gate2_ok", "eq_ok", "eqg_ok", "gate_ok", "gateT_done",
                             "gateT_ok", "b2_done"))
        wexp_in = sems("wexp_in", 2)
        l1_done, h_ok, l2_done, acc_ok, out_done = (
            sem(n) for n in ("l1_done", "h_ok", "l2_done", "acc_ok", "out_done"))

        block = ctx.enter_context(nc.Block())
        CONSTS = 12 * 16

        def settled(eng):
            eng.wait_ge(consts_in, CONSTS)

        def load_expert(eng, e, p):
            eng.dma_start(w1h[p][:, :], w1[e, 0:DH_, :]).then_inc(wexp_in[p], 16)
            eng.dma_start(w1l[p][:, :], w1[e, DH_:D, :]).then_inc(wexp_in[p], 16)
            eng.dma_start(w2s[p][:, :, :], w2[e]).then_inc(wexp_in[p], 16)
            eng.dma_start(b1s[p][:, :], b1[e]).then_inc(wexp_in[p], 16)

        @block.sync
        def _(sp):
            sp.dma_start(tokw[:, :, :], tok_w).then_inc(w_in, 16)
            sp.dma_start(patch[0][:, :, :], xp[0]).then_inc(patch_in[0], 16)
            sp.dma_start(patch[1][:, :, :], xp[1]).then_inc(patch_in[1], 16)
            sp.dma_start(hid[0:B, PAIRS, :], cls_tok[0, 0:1, :].partition_broadcast(B)).then_inc(cls_in, 16)
            with sp.Fori(1, PAIRS // 2) as it:
                for p in range(2):
                    sp.wait_ge(emb_done, 2 * it + p - 1)
                    sp.dma_start(patch[p][:, :, :], xp[2 * it + p]).then_inc(patch_in[p], 16)
            for p in range(2):
                load_expert(sp, p, p)
            with sp.Fori(1, E // 2) as it:
                for p in range(2):
                    sp.wait_ge(l2_done, TILES * (2 * it + p - 1))
                    load_expert(sp, 2 * it + p, p)
            for t in range(TILES):
                sp.wait_ge(acc_ok, TILES * E + t + 1)
                if t < PAIRS:
                    for m in range(2):
                        sp.dma_start(out[2 * t + m, 1:N, :],
                                     hid[m * NPATCH:(m + 1) * NPATCH, t, :]).then_inc(out_done, 16)
                else:
                    sp.dma_start(out[:, 0, :], hid[0:B, t, :]).then_inc(out_done, 16)
            sp.wait_ge(out_done, 16 * (2 * PAIRS + 1))

        @block.gpsimd
        def _(pool):
            pool.memset(ident[:, :], 0.0).then_inc(ident_zero, 1)
            pool.memset(mask[:, :], 1.0).then_inc(mask_one, 1)
            pool.iota(eidx_i[:, :], pattern=[[1, E]], base=0, channel_multiplier=0).then_inc(eidx_ok, 1)
            for tile in T + Qs + Sm + Fin:
                pool.memset(tile[:, :, :], 0.0).then_inc(tiles_zero, 1)
            pool.wait_ge(ident_zero, 1)
            pool.affine_select(out=ident[:, :], in_=ident[:, :], compare_op=ALU.not_equal, fill=1.0, base=0,
                               pattern=[[-1, 128]], channel_multiplier=1).then_inc(ident_ok, 1)
            pool.wait_ge(mask_one, 1)
            pool.affine_select(out=mask[:, :], in_=mask[:, :], compare_op=ALU.is_ge, fill=0.0, base=0,
                               pattern=[[-DH, HH]], channel_multiplier=1).then_inc(mask_half, 1)
            pool.wait_ge(mask_half, 1)
            pool.affine_select(out=mask[:, :], in_=mask[:, :], compare_op=ALU.is_ge, fill=0.0, base=DH - 1,
                               pattern=[[DH, HH]], channel_multiplier=-1).then_inc(mask_ok, 1)
            pool.wait_ge(eidx_ok, 1)
            pool.tensor_copy(eidx[:, :], eidx_i[:, :]).then_inc(eidx_ok, 1)

            def spread_k(i):
                pool.wait_ge(k_ok, 2 * i + 2)
                for f in range(2):
                    pool.tensor_tensor(
                        kbd[0:CH, f], kT[:, f].unsqueeze(2).broadcast_to([CH, 2, HH, N]),
                        mask[:, :].unsqueeze(1).unsqueeze(3).broadcast_to([CH, 2, HH, N]), ALU.mult,
                    ).then_inc(kbd_ok, 1)

            pool.wait_ge(mask_ok, 1)
            with pool.Fori(0, PAIRS) as i:
                spread_k(i)

            pool.wait_ge(xn_ok, PAIRS)
            pool.wait_ge(xncls_ok, 1)
            pool.tensor_tensor(hid[:, 0:PAIRS, :], hid[:, 0:PAIRS, :],
                               pb[:, :].unsqueeze(1).broadcast_to([128, PAIRS, D]), ALU.add).then_inc(hb_ok, 1)
            pool.tensor_tensor(hid[0:B, PAIRS, :], hid[0:B, PAIRS, :], pb[0:B, :], ALU.add).then_inc(hb_ok, 1)

            def combine(g):
                for c in range(4):
                    pool.wait_ge(qs_ok[c], g + 1)
                    pool.wait_ge(sm_ok[c], g + 1)
                    pool.tensor_tensor(V[c][:, :, :], Qs[c][0:N, :, :], Sm[c][0:N, :, :], ALU.add).then_inc(v_ok[c], 1)

            with pool.Fori(0, PAIRS * ITERS) as g:
                combine(g)

        @block.scalar
        def _(act):
            for dst, src in ((tokb[:, :], tok_b.partition_broadcast(128)),
                             (wqkv_h[:, :], qkv_w[0:DH_, :]), (wqkv_l[:, :], qkv_w[DH_:D, :]),
                             (qkb[:, :], qk_b), (vb[:, :], v_b.partition_broadcast(128)),
                             (wp_h[:, :], proj_w[0:DH_, :]), (wp_l[:, :], proj_w[DH_:D, :]),
                             (pb[:, :], proj_b.partition_broadcast(128)),
                             (wg_h[:, :], wg[0:DH_, :]), (wg_l[:, :], wg[DH_:D, :]),
                             (bgb[:, :], bg.partition_broadcast(128)),
                             (b2t[:, :], b2)):
                act.dma_start(dst, src).then_inc(consts_in, 16)
            act.wait_ge(consts_in, CONSTS)
            act.wait_ge(zero_ok, 5)
            act.wait_ge(tiles_zero, 16)

            act.mul(qbs[:, :], qkb[:, 0:2], DH ** -0.5).then_inc(qbs_ok, 1)
            act.wait_ge(eps_ok, 1)
            act.activation(rstd[:, :], rstd[:, :], ACT.Sqrt).then_inc(sqrt_ok, 1)
            act.wait_ge(clsT_done, 1)
            for k, (dst, rows) in enumerate(((xT_h, DH_), (xT_l, DL_))):
                act.copy(dst[:, :, NPATCH], bank[0][0:rows, k * 16:k * 16 + 2]).then_inc(clsT_ok, 1)

            def transposed_x(i):
                act.wait_ge(xnT_done, i + 1)
                if not isinstance(i, int) or i:
                    act.wait_ge(v_done, i)
                for k, (dst, rows) in enumerate(((xT_h, DH_), (xT_l, DL_))):
                    act.copy(dst[:, :, 0:NPATCH],
                             bank[0][0:rows, 128 * k:128 * k + 128].rearrange("p (m n) -> p m n", m=2),
                             ).then_inc(xT_ok, 1)

            def qk_out(i):
                act.wait_ge(qk_done, i + 1)
                if not isinstance(i, int) or i:
                    act.wait_ge(score_done, 2 * i)
                    act.wait_ge(kbd_ok, 2 * i)
                for f in range(2):
                    act.activation(qT[0:CH, f].rearrange("p m n -> p (m n)"), bank[1][0:CH, 130 * f:130 * f + 130],
                                   ACT.Identity, bias=qbs[:, f:f + 1], scale=DH ** -0.5).then_inc(q_ok, 1)
                for f, src in ((0, bank[1][0:CH, 260:390]), (1, bank[0][0:CH, 256:386])):
                    act.activation(kT[:, f].rearrange("p m n -> p (m n)"), src,
                                   ACT.Identity, bias=qkb[:, 2 + f:3 + f], scale=1.0).then_inc(k_ok, 1)

            def attention(i, more):
                if more:
                    transposed_x(i + 1)
                for m in range(2):
                    act.wait_ge(clamp_ok, 2 * i + m + 1)
                    act.activation(xexp[m][:, :, :], sdiff[m][:, :, :], ACT.Exp).then_inc(exp_ok, 1)
                if more:
                    qk_out(i + 1)
                for m in range(2):
                    act.wait_ge(xt_done, 2 * i + m + 1)
                    act.copy(xtv[m][0:N, :, 0:N].rearrange("p (f h) n -> p f h n", f=2),
                             half_heads[m]).then_inc(xtv_ok, 1)
                for m in range(2):
                    act.wait_ge(g_ok, 2 * i + m + 1)
                    settled(act)
                    act.copy(wall[0:N, bass.ds((2 * i + m) * H, H), :].rearrange("p (f h) v -> p f h v", f=2),
                             gram[m][:, :, :, N:XW]).then_inc(w_ok, 1)

            transposed_x(0)
            qk_out(0)
            with act.Fori(0, PAIRS - 2) as i:
                attention(i, True)
            attention(PAIRS - 2, True)
            attention(PAIRS - 1, False)

            def square_out(g):
                for c in range(4):
                    act.wait_ge(p1_done[c], g + 1)
                    act.mul(Qs[c][0:N, :, :].rearrange("p h n -> p (h n)"), P[c], BETA).then_inc(qs_ok[c], 1)

            def context_out(j):
                act.wait_ge(ctxT_done, j + 1)
                for k, (dst, dstc, rows) in enumerate(((cT_h, cTc_h, DH_), (cT_l, cTc_l, DL_))):
                    settled(act)
                    src = bank[1][0:rows, 130 * k:130 * k + 130].rearrange("p (m n) -> p m n", m=2)
                    act.copy(dst[:, :, :], src[:, :, 0:NPATCH]).then_inc(cT_ok, 1)
                    act.copy(dstc[:, bass.ds(2 * j, 2)], src[:, :, NPATCH]).then_inc(cT_ok, 1)

            with act.Fori(0, ITERS) as g:
                square_out(g)
            with act.Fori(1, PAIRS) as j:
                with act.Fori(0, ITERS) as it:
                    square_out(ITERS * j + it)
                context_out(j - 1)
            context_out(PAIRS - 1)

            act.wait_ge(eps2_ok, 1)
            act.activation(rstd2[:, :], rstd2[:, :], ACT.Sqrt).then_inc(sqrt2_ok, 1)
            for t in range(TILES):
                rows = 128 if t < PAIRS else B
                act.wait_ge(x2T_done, t + 1)
                for k, (dst, r) in enumerate(((x2T_h, DH_), (x2T_l, DL_))):
                    act.copy(dst[:, 128 * t:128 * t + rows],
                             bank[t % 2][0:r, 128 * k:128 * k + rows]).then_inc(x2T_ok, 1)
            def hidden(g, e, k):
                for mt in range(MT):
                    act.wait_ge(l1_done, MT * g + mt + 1)
                    if mt == 0 and (not isinstance(g, int) or g > 1):
                        act.wait_ge(l2_done, 3 * (g - 1))
                    q = (MT * gpos[0] + mt) % 4
                    act.activation(hT[gpos[0] % 2][:, mt, 0:BLK[k]], L1[q][:, 0:BLK[k]], ACT.Relu,
                                   bias=b1s[gpos[0] // 3 % 2][:, mt:mt + 1]).then_inc(h_ok, 1)

            gpos = [0]
            hidden(0, 0, 0)
            act.wait_ge(gdiff_ok, 1)
            act.activation(gk[:, 1, :], gk[:, 0, :], ACT.Exp).then_inc(gexp_ok, 1)
            for t in range(TILES):
                rows = 128 if t < PAIRS else B
                act.wait_ge(gateT_done, t + 1)
                act.copy(gateT[:, 128 * t:128 * t + rows], bank[t % 2][0:E, 256:256 + rows]).then_inc(gateT_ok, 1)

            def experts(it, blocks):
                for n in range(1, blocks + 1):
                    gpos[0] = n
                    hidden(6 * it + n, 2 * it + n // 3, n % 3)

            experts(0, 6)
            with act.Fori(1, E // 2 - 1) as it:
                experts(it, 6)
            experts(E // 2 - 1, 5)

        @block.vector
        def _(dve):
            dve.memset(ones[:, :], 1.0).then_inc(ones_ok, 1)
            dve.memset(mv[:, :, :], 1.0).then_inc(mv_init, 1)
            dve.memset(mv2[:, :, :], 1.0).then_inc(mv_init, 1)
            dve.memset(logit[:, :, :], 0.0).then_inc(logit_zero, 1)
            for m in range(2):
                dve.memset(xtv[m][:, :, :], 0.0).then_inc(emb_free, 1)
            dve.memset(qT[CH:ROWS], 0.0).then_inc(zero_ok, 1)
            dve.memset(kbd[CH:ROWS], 0.0).then_inc(zero_ok, 1)
            dve.memset(wall[:, :, :], 0.0).then_inc(zero_ok, 1)
            dve.wait_ge(emb_free, 2)
            for m in range(2):
                dve.memset(xtv[m][0:N, :, XW - 1:XW], 1.0).then_inc(zero_ok, 1)
            dve.wait_ge(consts_in, CONSTS)
            dve.wait_ge(mv_init, 2)
            dve.wait_ge(tiles_zero, 16)
            dve.wait_ge(zero_ok, 5)

            def mean_variance(stats, dst, stats_sem, mv_sem):
                dve.wait_ge(stats_sem, TILES)
                for t in range(TILES):
                    rows = 128 if t < PAIRS else B
                    dve.bn_aggr(dst[0:rows, t, :], stats[0:rows, t, :]).then_inc(mv_sem, 1)
                dve.wait_ge(mv_sem, TILES)

            with dve.Fori(0, PAIRS // 2) as it:
                for p in range(2):
                    t = 2 * it + p
                    dve.wait_ge(emb_done, t + 1)
                    dve.tensor_tensor(hid[:, t, :], bank[p][:, 0:D], tokb[:, :], ALU.add).then_inc(emb_free, 1)
                    dve.wait_ge(emb_free, t + 3)
                    settled(dve)
                    dve.bn_stats(stat[:, t, :], hid[:, t, :]).then_inc(stat_ok, 1)
            dve.wait_ge(cls_in, 16)
            dve.bn_stats(stat[0:B, PAIRS, :], hid[0:B, PAIRS, :]).then_inc(stat_ok, 1)
            mean_variance(stat, mv, stat_ok, mv_ok)
            dve.tensor_scalar(rstd[:, :], mv[:, :, 1], EPS, None, ALU.add).then_inc(eps_ok, 1)
            dve.wait_ge(sqrt_ok, 1)
            dve.reciprocal(rstd[:, :], rstd[:, :]).then_inc(rstd_ok, 1)
            dve.wait_ge(rstd_ok, 1)
            dve.tensor_scalar(xncls[:, :], hid[0:B, PAIRS, :], mv[0:B, PAIRS, 0:1], rstd[0:B, PAIRS:TILES],
                              ALU.subtract, ALU.mult).then_inc(xncls_ok, 1)

            def normalise(i):
                if not isinstance(i, int) or i:
                    dve.wait_ge(xnT_done, i)
                dve.tensor_scalar(xn[:, :], hid[:, i, :], mv[:, i, 0:1], rstd[:, i:i + 1] if isinstance(i, int) else
                                  rstd[:, bass.ds(i, 1)], ALU.subtract, ALU.mult).then_inc(xn_ok, 1)

            normalise(0)
            normalise(1)

            def attention(i, norm):
                def maximum(m):
                    dve.wait_ge(score_done, 2 * i + m + 1)
                    dve.tensor_reduce(rmax[:, m, :].rearrange("p (f h) -> p f h", f=2), half_heads[m],
                                      AX.X, ALU.max).then_inc(rmax_ok, 1)
                    dve.wait_ge(rmax_ok, 2 * i + m + 1)
                    dve.tensor_tensor(
                        sdiff[m][:, :, :].rearrange("p (f h) n -> p f h n", f=2), half_heads[m],
                        rmax[:, m, :].rearrange("p (f h) -> p f h", f=2).unsqueeze(3).broadcast_to([N, 2, HH, N]),
                        ALU.subtract).then_inc(diff_ok, 1)
                    dve.wait_ge(diff_ok, 2 * i + m + 1)
                    dve.tensor_scalar(sdiff[m][:, :, :], sdiff[m][:, :, :], -88.0, None,
                                      ALU.max).then_inc(clamp_ok, 1)

                def values(m):
                    dve.wait_ge(v_done, i + 1)
                    dve.tensor_tensor(
                        xtv[m][0:N, :, N:XW - 1], bank[2][0:N, D * m:D * m + D].rearrange("p (h d) -> p h d", h=H),
                        vb[0:N, :].rearrange("p (h d) -> p h d", h=H), ALU.add).then_inc(vx_ok, 1)

                maximum(0)
                values(0)
                values(1)
                maximum(1)
                if norm:
                    normalise(i + 2)
                for m in range(2):
                    dve.wait_ge(xtv_ok, 2 * i + m + 1)
                    dve.tensor_reduce(csum[:, bass.ds((2 * i + m) * H, H)], xtv[m][0:N, :, 0:N],
                                      AX.X, ALU.add).then_inc(csum_ok, 1)
                for m in range(2):
                    dve.wait_ge(gram_done, 2 * i + m + 1)
                    dve.tensor_copy(gall[:, bass.ds((2 * i + m) * H, H), :].rearrange("p (f h) n -> p f h n", f=2),
                                    gram[m][:, :, :, 0:N]).then_inc(g_ok, 1)

            with dve.Fori(0, PAIRS - 2) as i:
                attention(i, True)
            attention(PAIRS - 2, False)
            attention(PAIRS - 1, False)

            dve.wait_ge(csum_ok, B)
            dve.tensor_reduce(mx2[:, 0:1], csum[:, :], AX.X, ALU.max).then_inc(gmax_ok, 1)
            dve.wait_ge(w_ok, B)
            dve.tensor_reduce(mx2[:, 1:2], wall[0:N, :, VA - 1], AX.X, ALU.max).then_inc(gmax_ok, 1)
            dve.wait_ge(gmaxT_done, 1)
            dve.tensor_reduce(grow[0:1, 0:2], bank[2][0:1, 0:2 * N].rearrange("p (a n) -> p a n", a=2),
                              AX.X, ALU.max).then_inc(gmax1_ok, 1)
            dve.wait_ge(gmax1_ok, 1)
            dve.tensor_tensor(grow[0:1, 2:3], grow[0:1, 0:1], grow[0:1, 1:2], ALU.mult).then_inc(gprod_ok, 1)
            dve.wait_ge(gprod_ok, 1)
            dve.tensor_scalar(grow[0:1, 3:4], grow[0:1, 2:3], 1e-15, None, ALU.add).then_inc(geps_ok, 1)
            dve.wait_ge(geps_ok, 1)
            dve.reciprocal(grow2[0:1, 0:1], grow[0:1, 3:4]).then_inc(grec_ok, 1)
            dve.wait_ge(grec_ok, 1)
            dve.tensor_scalar(grow2[0:1, 1:2], grow2[0:1, 0:1], -4.0 * KAPPA, None, ALU.mult).then_inc(gscale_ok, 1)
            dve.wait_ge(gbc_done, 1)
            dve.tensor_copy(cscale[:, :], bank[2][0:N, 256:257]).then_inc(cscale_ok, 1)
            dve.wait_ge(cscale_ok, 1)
            dve.wait_ge(g_ok, B)

            def start(j, c):
                dve.tensor_scalar(T[c][0:N, :, :], gall[:, bass.ds((4 * j + c) * HH, HH), :], cscale[:, 0:1], None,
                                  ALU.mult).then_inc(t_ok[c], 1)

            def middle(g, c):
                dve.wait_ge(qs_ok[c], g + 1)
                dve.scalar_tensor_tensor(Sm[c][0:N, :, :].rearrange("p h n -> p (h n)"),
                                         T[c][0:N, :, :].rearrange("p h n -> p (h n)"), 28.0 * KAPPA, P[c],
                                         ALU.mult, ALU.add).then_inc(sm_ok[c], 1)

            def close(g, c, dst, done):
                dve.wait_ge(p2_done[c], g + 1)
                dve.wait_ge(v_ok[c], g + 1)
                dve.scalar_tensor_tensor(dst[c][0:N, :, :].rearrange("p h n -> p (h n)"),
                                         V[c][:, :, :].rearrange("p h n -> p (h n)"), CV, P[c],
                                         ALU.mult, ALU.add).then_inc(done[c], 1)

            def context(j):
                dve.wait_ge(wv_done, j + 1)
                prod = bank[0][0:N, 0:2 * H * VA].rearrange("p (g v) -> p g v", v=VA)
                dve.tensor_scalar(den[:, :, :].rearrange("p m h -> p (m h)"), prod[:, :, VA - 1],
                                  -0.25 / KAPPA, 1e-8, ALU.mult, ALU.max).then_inc(den_ok, 1)
                dve.wait_ge(den_ok, j + 1)
                dve.reciprocal(rden[:, :, :], den[:, :, :]).then_inc(rden_ok, 1)
                dve.wait_ge(rden_ok, j + 1)
                dve.scalar_tensor_tensor(
                    ctxv[:, :, :].rearrange("p m (h d) -> p (m h) d", d=DH), prod[:, :, 0:DH], -0.25 / KAPPA,
                    rden[:, :, :].rearrange("p m h -> p (m h)").unsqueeze(2).broadcast_to([N, 2 * H, DH]),
                    ALU.mult, ALU.mult).then_inc(ctx_ok, 1)

            def residual(j, rows):
                dve.wait_ge(proj_done, j + 1)
                dve.tensor_tensor(hid[0:rows, j, :], bank[2][0:rows, 0:D], hid[0:rows, j, :],
                                  ALU.add).then_inc(h2_ok, 1)
                dve.wait_ge(h2_ok, j + 1)
                settled(dve)
                dve.bn_stats(stat2[0:rows, j, :], hid[0:rows, j, :]).then_inc(stat2_ok, 1)

            def pair(j, tail, more):
                g0 = ITERS * j
                for c in range(4):
                    middle(g0, c)
                for c in range(4):
                    close(g0, c, T, t_ok)
                if tail:
                    context(j - 1)
                with dve.Fori(1, ITERS - 1) as it:
                    for c in range(4):
                        middle(g0 + it, c)
                    for c in range(4):
                        close(g0 + it, c, T, t_ok)
                for c in range(4):
                    middle(g0 + ITERS - 1, c)
                for c in range(4):
                    if more:
                        dve.wait_ge(sm_ok[c], g0 + ITERS)
                        start(j + 1, c)
                for c in range(4):
                    close(g0 + ITERS - 1, c, Fin, fin_ok)
                if tail:
                    residual(j - 1, 128)

            dve.wait_ge(hb_ok, 2)
            for c in range(4):
                start(0, c)
            pair(0, False, True)
            with dve.Fori(1, PAIRS - 1) as j:
                pair(j, True, True)
            pair(PAIRS - 1, True, False)
            context(PAIRS - 1)
            residual(PAIRS - 1, 128)
            residual(PAIRS, B)

            mean_variance(stat2, mv2, stat2_ok, mv2_ok)
            dve.tensor_scalar(rstd2[:, :], mv2[:, :, 1], EPS, None, ALU.add).then_inc(eps2_ok, 1)
            dve.wait_ge(sqrt2_ok, 1)
            dve.reciprocal(rstd2[:, :], rstd2[:, :]).then_inc(rstd2_ok, 1)
            dve.wait_ge(rstd2_ok, 1)
            for t in range(TILES):
                rows = 128 if t < PAIRS else B
                if t >= 2:
                    dve.wait_ge(x2T_done, t - 1)
                dve.tensor_scalar(x2[t % 2][0:rows, :], hid[0:rows, t, :], mv2[0:rows, t, 0:1],
                                  rstd2[0:rows, t:t + 1], ALU.subtract, ALU.mult).then_inc(x2_ok, 1)

            dve.wait_ge(logit_done, 1)
            dve.wait_ge(logit_zero, 1)
            lp = bank[3][:, 0:TILES * E].rearrange("p (t e) -> p t e", e=E)
            dve.tensor_tensor(logit[:, 0:PAIRS, :], lp[:, 0:PAIRS, :],
                              bgb[:, :].unsqueeze(1).broadcast_to([128, PAIRS, E]), ALU.add).then_inc(logit_ok, 1)
            dve.tensor_tensor(logit[0:B, PAIRS, :], lp[0:B, PAIRS, :], bgb[0:B, :], ALU.add).then_inc(logit_ok, 1)
            dve.wait_ge(logit_ok, 2)
            for t in range(TILES):
                dve.max(top[:, t, :], logit[:, t, :]).then_inc(top_ok, 1)
            dve.wait_ge(top_ok, TILES)
            for t in range(TILES):
                dve.max_index(topi[:, t, :], top[:, t, :], logit[:, t, :]).then_inc(topi_ok, 1)
            dve.tensor_tensor(gk[:, 0, :], top[:, :, 1], top[:, :, 0], ALU.subtract).then_inc(gdiff_ok, 1)
            dve.wait_ge(topi_ok, TILES)
            dve.tensor_copy(topf[:, :, :], topi[:, :, 0:2]).then_inc(topf_ok, 1)
            dve.wait_ge(topf_ok, 1)
            dve.wait_ge(eidx_ok, 2)
            for r in range(2):
                dve.tensor_tensor(eq[:, r, :, :], eidx[:, :].unsqueeze(1).broadcast_to([128, TILES, E]),
                                  topf[:, :, r].unsqueeze(2).broadcast_to([128, TILES, E]),
                                  ALU.is_equal).then_inc(eq_ok, 1)
            dve.wait_ge(gexp_ok, 1)
            dve.tensor_scalar(gk[:, 0, :], gk[:, 1, :], 1.0, None, ALU.add).then_inc(gden_ok, 1)
            dve.wait_ge(gden_ok, 1)
            dve.reciprocal(gk[:, 2, :], gk[:, 0, :]).then_inc(gate1_ok, 1)
            dve.wait_ge(gate1_ok, 1)
            dve.tensor_tensor(gk[:, 3, :], gk[:, 1, :], gk[:, 2, :], ALU.mult).then_inc(gate2_ok, 1)
            dve.wait_ge(gate2_ok, 1)
            dve.wait_ge(eq_ok, 2)
            for r in range(2):
                dve.tensor_tensor(eq[:, r, :, :], eq[:, r, :, :],
                                  gk[:, 2 + r, :].unsqueeze(2).broadcast_to([128, TILES, E]),
                                  ALU.mult).then_inc(eqg_ok, 1)
            dve.wait_ge(eqg_ok, 2)
            dve.tensor_tensor(gate[:, :, :], eq[:, 0, :, :], eq[:, 1, :, :], ALU.add).then_inc(gate_ok, 1)
            dve.wait_ge(gate_ok, 1)
            for t in range(TILES):
                rows = 128 if t < PAIRS else B
                dve.wait_ge(b2_done, t + 1)
                dve.tensor_tensor(hid[0:rows, t, :], bank[t % 3][0:rows, 0:D], hid[0:rows, t, :],
                                  ALU.add).then_inc(acc_ok, 1)

            def expert(e, y0):
                for t in range(TILES):
                    rows = 128 if t < PAIRS else B
                    y = TILES * e + t
                    dve.wait_ge(l2_done, y + 1)
                    dve.wait_ge(acc_ok, y + 1)
                    dve.scalar_tensor_tensor(hid[0:rows, t, :], bank[(y0 + t) % 3][0:rows, 0:D],
                                             gate[0:rows, t, bass.ds(e, 1)], hid[0:rows, t, :],
                                             ALU.mult, ALU.add).then_inc(acc_ok, 1)

            with dve.Fori(0, E) as e:
                expert(e, 0)

        @block.tensor
        def _(pe):
            def two(dst, st_h, st_l, mv_h, mv_l):
                pe.matmul(dst, st_h, mv_h, start=True, stop=False)
                return pe.matmul(dst, st_l, mv_l, start=False, stop=True)

            pe.wait_ge(w_in, 16)
            with pe.Fori(0, PAIRS // 2) as it:
                for p in range(2):
                    pe.wait_ge(patch_in[p], 16 * it + 16)
                    pe.wait_ge(emb_free, 2 * it + p + 1)
                    for k in range(KT):
                        last = pe.matmul(bank[p][:, 0:D], patch[p][:, k, :], tokw[:, k, :],
                                         start=(k == 0), stop=(k == KT - 1))
                    last.then_inc(emb_done, 1)

            pe.wait_ge(ident_ok, 1)
            pe.wait_ge(consts_in, CONSTS)
            pe.wait_ge(xncls_ok, 1)
            pe.transpose(bank[0][:, 0:B], xncls[:, 0:DH_], ident[0:B, 0:B])
            pe.transpose(bank[0][0:DL_, B:2 * B], xncls[:, DH_:D], ident[0:B, 0:B]).then_inc(clsT_done, 1)
            pe.wait_ge(clsT_ok, 2)

            def transpose_x(i):
                pe.wait_ge(xn_ok, i + 1)
                if not isinstance(i, int) or i:
                    pe.wait_ge(xT_ok, 2 * i)
                    pe.wait_ge(k_ok, 2 * i)
                pe.transpose(bank[0][:, 0:128], xn[:, 0:DH_], ident[:, :])
                pe.transpose(bank[0][0:DL_, 128:256], xn[:, DH_:D], ident[:, :]).then_inc(xnT_done, 1)

            def project(i):
                pe.wait_ge(xT_ok, 2 * i + 2)
                if not isinstance(i, int) or i:
                    pe.wait_ge(q_ok, 2 * i)
                    pe.wait_ge(k_ok, 2 * i)
                xh, xl = (x[:, :, :].rearrange("p m n -> p (m n)") for x in (xT_h, xT_l))
                for f in range(4):
                    dst = bank[1][0:CH, 130 * f:130 * f + 130] if f < 3 else bank[0][0:CH, 256:386]
                    last = two(dst, wqkv_h[:, CH * f:CH * f + CH], wqkv_l[:, CH * f:CH * f + CH], xh, xl)
                last.then_inc(qk_done, 1)
                if not isinstance(i, int) or i:
                    pe.wait_ge(vx_ok, 2 * i)
                for m in range(2):
                    last = two(bank[2][0:N, D * m:D * m + D], xT_h[:, m, :], xT_l[:, m, :],
                               wqkv_h[:, 2 * D:3 * D], wqkv_l[:, 2 * D:3 * D])
                last.then_inc(v_done, 1)

            def attention(i, more):
                if more:
                    transpose_x(i + 1)
                pe.wait_ge(q_ok, 2 * i + 2)
                pe.wait_ge(kbd_ok, 2 * i + 2)
                for m in range(2):
                    if not isinstance(i, int) or i:
                        pe.wait_ge(g_ok, 2 * i)
                        pe.wait_ge(w_ok, 2 * i)
                    for f in range(2):
                        last = pe.matmul(sx[m][0:N, f, 0:HH * N], qT[:, f, m, :],
                                         kbd[:, f, m, :, :].rearrange("p h n -> p (h n)"), start=True, stop=True)
                    last.then_inc(score_done, 1)
                if more:
                    project(i + 1)
                for m in range(2):
                    pe.wait_ge(exp_ok, 2 * i + m + 1)
                    for h in range(H):
                        last = pe.transpose(sx[m][0:N, h // HH, N * (h % HH):N * (h % HH) + N], xexp[m][:, h, :],
                                            ident[0:N, 0:N])
                    last.then_inc(xt_done, 1)
                for m in range(2):
                    pe.wait_ge(xtv_ok, 2 * i + m + 1)
                    pe.wait_ge(vx_ok, 2 * i + m + 1)
                    for h in range(H):
                        last = pe.matmul(sx[m][0:N, h // HH, XW * (h % HH):XW * (h % HH) + XW],
                                         xtv[m][:, h, 0:N], xtv[m][:, h, :], start=True, stop=True)
                    last.then_inc(gram_done, 1)

            transpose_x(0)
            project(0)
            pe.wait_ge(zero_ok, 5)
            attention(0, True)
            with pe.Fori(1, PAIRS - 2) as i:
                attention(i, True)
            attention(PAIRS - 2, True)
            attention(PAIRS - 1, False)

            pe.wait_ge(gmax_ok, 2)
            pe.wait_ge(ones_ok, 1)
            for a in range(2):
                last = pe.transpose(bank[2][0:1, a * N:a * N + N], mx2[:, a:a + 1], ident[0:N, 0:N])
            last.then_inc(gmaxT_done, 1)
            pe.wait_ge(gscale_ok, 1)
            pe.matmul(bank[2][0:N, 256:257], ones[:, :], grow2[0:1, 1:2], start=True, stop=True).then_inc(gbc_done, 1)

            def square(g, c):
                pe.wait_ge(t_ok[c], g + 1)
                for h in range(HH):
                    last = pe.matmul(P[c][:, N * h:N * h + N], T[c][:, h, :], T[c][:, h, :], start=True, stop=True)
                last.then_inc(p1_done[c], 1)

            def product(g, c):
                pe.wait_ge(qs_ok[c], g + 1)
                pe.wait_ge(sm_ok[c], g + 1)
                for h in range(HH):
                    last = pe.matmul(P[c][:, N * h:N * h + N], Qs[c][:, h, :], Sm[c][:, h, :], start=True, stop=True)
                last.then_inc(p2_done[c], 1)

            def apply(j):
                for c in range(4):
                    pe.wait_ge(fin_ok[c], j + 1)
                    for h in range(HH):
                        n = HH * c + h
                        last = pe.matmul(bank[0][0:N, VA * n:VA * n + VA], Fin[c][:, h, :],
                                         wall[:, bass.ds(2 * H * j + n, 1), :].rearrange("p a v -> p (a v)"),
                                         start=True, stop=True)
                last.then_inc(wv_done, 1)

            def transpose_context(j):
                pe.wait_ge(ctx_ok, j + 1)
                for m in range(2):
                    pe.transpose(bank[1][:, N * m:N * m + N], ctxv[:, m, 0:DH_], ident[0:N, 0:N])
                    last = pe.transpose(bank[1][0:DL_, 130 + N * m:130 + N * m + N], ctxv[:, m, DH_:D],
                                        ident[0:N, 0:N])
                last.then_inc(ctxT_done, 1)

            def project_context(j):
                pe.wait_ge(cT_ok, 4 * j + 4)
                two(bank[2][:, 0:D], cT_h[:, :, :].rearrange("p m n -> p (m n)"),
                    cT_l[:, :, :].rearrange("p m n -> p (m n)"), wp_h[:, :], wp_l[:, :]).then_inc(proj_done, 1)

            def pair(j, tail):
                g0 = ITERS * j
                for c in range(4):
                    if tail:
                        pe.wait_ge(fin_ok[c], j)
                    square(g0, c)
                if tail:
                    apply(j - 1)
                for c in range(4):
                    product(g0, c)
                with pe.Fori(1, ITERS - 1) as it:
                    for c in range(4):
                        square(g0 + it, c)
                    for c in range(4):
                        product(g0 + it, c)
                for c in range(4):
                    square(g0 + ITERS - 1, c)
                if tail:
                    transpose_context(j - 1)
                for c in range(4):
                    product(g0 + ITERS - 1, c)
                if tail:
                    project_context(j - 1)

            pair(0, False)
            with pe.Fori(1, PAIRS) as j:
                pair(j, True)
            apply(PAIRS - 1)
            transpose_context(PAIRS - 1)
            project_context(PAIRS - 1)
            pe.wait_ge(h2_ok, PAIRS)
            two(bank[2][0:B, 0:D], cTc_h[:, :], cTc_l[:, :], wp_h[:, :], wp_l[:, :]).then_inc(proj_done, 1)

            for t in range(TILES):
                rows = 128 if t < PAIRS else B
                pe.wait_ge(x2_ok, t + 1)
                if t >= 2:
                    pe.wait_ge(x2T_ok, 2 * (t - 1))
                pe.transpose(bank[t % 2][:, 0:rows], x2[t % 2][0:rows, 0:DH_], ident[0:rows, 0:rows])
                pe.transpose(bank[t % 2][0:DL_, 128:128 + rows], x2[t % 2][0:rows, DH_:D],
                             ident[0:rows, 0:rows]).then_inc(x2T_done, 1)
            for t in range(TILES):
                cols = slice(128 * t, 128 * t + (128 if t < PAIRS else B))
                pe.wait_ge(x2T_ok, 2 * t + 2)
                last = two(bank[3][0:cols.stop - cols.start, E * t:E * t + E], x2T_h[:, cols], x2T_l[:, cols],
                           wg_h[:, :], wg_l[:, :])
            last.then_inc(logit_done, 1)

            def first_layer(g, n, k, p, it):
                if n % 3 == 0:
                    pe.wait_ge(wexp_in[p], 64 * it + 64)
                for mt in range(MT):
                    q = MT * n + mt
                    if n or mt >= 4:
                        pe.wait_ge(h_ok, MT * g + mt - 3)
                    cols = slice(BOFF[k], BOFF[k] + BLK[k])
                    two(L1[q % 4][:, 0:BLK[k]], w1h[p][:, 128 * mt:128 * mt + 128], w1l[p][:, 128 * mt:128 * mt + 128],
                        x2T_h[:, cols], x2T_l[:, cols]).then_inc(l1_done, 1)

            def second_layer(g, n, k, p):
                pe.wait_ge(h_ok, MT * g + MT)
                for u in range(3):
                    t = 3 * k + u
                    rows = 128 if t < PAIRS else B
                    pe.wait_ge(acc_ok, 3 * g + u + TILES - 2)
                    for mt in range(MT):
                        last = pe.matmul(bank[t % 3][0:rows, 0:D], hT[n % 2][:, mt, 128 * u:128 * u + rows],
                                         w2s[p][:, mt, :], start=(mt == 0), stop=(mt == MT - 1))
                    last.then_inc(l2_done, 1)

            first_layer(0, 0, 0, 0, 0)

            pe.wait_ge(gate_ok, 1)
            for t in range(TILES):
                rows = 128 if t < PAIRS else B
                if t >= 2:
                    pe.wait_ge(gateT_ok, t - 1)
                pe.transpose(bank[t % 2][0:E, 256:256 + rows], gate[0:rows, t, :],
                             ident[0:rows, 0:rows]).then_inc(gateT_done, 1)
            for t in range(TILES):
                rows = 128 if t < PAIRS else B
                pe.wait_ge(gateT_ok, TILES)
                if t >= 3:
                    pe.wait_ge(acc_ok, t - 2)
                pe.matmul(bank[t % 3][0:rows, 0:D], gateT[:, 128 * t:128 * t + rows], b2t[:, :],
                          start=True, stop=True).then_inc(b2_done, 1)

            def experts(it, blocks):
                for n in range(6):
                    if n < blocks:
                        first_layer(6 * it + n + 1, n + 1, (n + 1) % 3, ((n + 1) // 3) % 2, it + (n + 1) // 6)
                    second_layer(6 * it + n, n, n % 3, n // 3)

            with pe.Fori(0, E // 2 - 1) as it:
                experts(it, 6)
            experts(E // 2 - 1, 5)


def kernel(x, cls_tok, L0_tok_W, L0_tok_b, L0_attn_qkv_w, L0_attn_qkv_b, L0_attn_proj_w, L0_attn_proj_b,
           L0_ffn_Wg, L0_ffn_bg, L0_ffn_W1, L0_ffn_b1, L0_ffn_W2, L0_ffn_b2):
    import numpy as np
    import concourse.bacc as bacc
    from concourse.bass_utils import run_bass_kernel_spmd

    def lay(a):
        return np.ascontiguousarray(a)

    side = IMG // PATCH
    p = np.asarray(x).reshape(PAIRS, 2, C_IN, side, PATCH, side, PATCH)
    p = p.transpose(0, 4, 6, 2, 1, 3, 5).reshape(PAIRS, KT, 128, 128).transpose(0, 2, 1, 3)
    arrays = {
        "xp": lay(p),
        "cls_tok": lay(cls_tok),
        "tok_w": lay(np.asarray(L0_tok_W).T.reshape(KT, 128, D).transpose(1, 0, 2)),
        "tok_b": lay(L0_tok_b),
        "qkv_w": lay(L0_attn_qkv_w),
        "qk_b": lay(np.asarray(L0_attn_qkv_b)[0:2 * D].reshape(4, CH).T),
        "v_b": lay(np.asarray(L0_attn_qkv_b)[2 * D:3 * D]),
        "proj_w": lay(L0_attn_proj_w),
        "proj_b": lay(L0_attn_proj_b),
        "wg": lay(L0_ffn_Wg),
        "bg": lay(L0_ffn_bg),
        "w1": lay(L0_ffn_W1),
        "b1": lay(np.asarray(L0_ffn_b1).reshape(E, MT, 128).transpose(0, 2, 1)),
        "w2": lay(np.asarray(L0_ffn_W2).reshape(E, MT, 128, D).transpose(0, 2, 1, 3)),
        "b2": lay(L0_ffn_b2),
    }
    nc = bacc.Bacc("TRN2", target_bir_lowering=False, num_devices=1)
    args = [nc.dram_tensor(n, a.shape, mybir.dt.from_np(a.dtype), kind="ExternalInput").ap()
            for n, a in arrays.items()]
    args.append(nc.dram_tensor("out", (B, N, D), F32, kind="ExternalOutput").ap())
    build(nc, *args)
    return run_bass_kernel_spmd(nc, [arrays], core_ids=[0]).results[0]["out"]
```

```python
import concourse.bass as bass
from concourse import mybir
from contextlib import ExitStack

F32 = mybir.dt.float32
U32 = mybir.dt.uint32
I32 = mybir.dt.int32
BF16 = mybir.dt.bfloat16
ALU = mybir.AluOpType
ACT = mybir.ActivationFunctionType
AX = mybir.AxisListType

B = 16
C_IN, IMG, PATCH = 3, 128, 16
NPATCH = (IMG // PATCH) ** 2
N = NPATCH + 1
D = 192
DH_, DL_ = 128, D - 128
KT = PATCH * PATCH * C_IN // 128
H, DH = 12, 16
HH = H // 2
CH = HH * DH
VA = DH + 1
XW = N + VA
PAIRS = B // 2
ITERS = 6
E, HID = 8, 768
MT = HID // 128
TILES = PAIRS + 1
NTOK = B * N
ROWS = 128
TOPK = 2
SLOTS = 128
ST = (TOPK * NTOK + E * (SLOTS - 1)) // SLOTS
G = TOPK * TILES
HH2 = HID // 2
EPS = 1e-5

BETA = 92.0 / 13.0
KAPPA = (1.0 / (256.0 * BETA)) ** (1.0 / 3.0)
CV = 13.0 / (112.0 * KAPPA)


class Area:

    def __init__(self, tensor):
        self.tensor, self.used = tensor, 0

    def take(self, n):
        self.used += n
        return self.tensor[:, self.used - n:self.used]

    def again(self):
        self.used = 0


def build(nc, xp, cls_tok, tok_w, tok_b, qkv_w, qk_b, v_b, proj_w, proj_b, wg, bg, w1, b1, w2, b2, out):
    ctx = ExitStack()
    with ctx:
        def sb(name, shape, dt=F32):
            return ctx.enter_context(nc.sbuf_tensor(name, shape, dt))

        def sem(name):
            return ctx.enter_context(nc.semaphore(name))

        tokw = sb("tokw", [128, KT, D])
        tokb = sb("tokb", [128, D])
        wqkv_h = sb("wqkv_h", [DH_, 3 * D])
        wqkv_l = sb("wqkv_l", [DL_, 3 * D])
        qkb = sb("qkb", [CH, 4])
        qbs = sb("qbs", [CH, 2])
        vb = sb("vb", [128, D])
        wp_h = sb("wp_h", [DH_, D])
        wp_l = sb("wp_l", [DL_, D])
        pb = sb("pb", [128, D])
        wg_h = sb("wg_h", [DH_, E])
        wg_l = sb("wg_l", [DL_, E])
        bgb = sb("bgb", [128, E])
        b2t = sb("b2t", [E, D])
        ident = sb("ident", [128, 128])
        ones = sb("ones", [1, N])
        mask = sb("mask", [CH, HH])
        hid = sb("hid", [128, TILES, D])
        mv = sb("mv", [128, TILES, 2])
        rstd = sb("rstd", [128, TILES])
        stat = sb("stat", [128, TILES, 6])
        front = Area(sb("front", [128, 2 * (KT * 128 + 2 * H * N + H * XW) + 4 * HH * N]))
        patch = [front.take(KT * 128).rearrange("p (k n) -> p k n", k=KT) for s in range(2)]
        xn = sb("xn", [128, D])
        xncls = sb("xncls", [B, D])
        xT_h = sb("xT_h", [DH_, 2, N])
        xT_l = sb("xT_l", [DL_, 2, N])
        qT = sb("qT", [ROWS, 2, 2, N])
        kT = sb("kT", [CH, 2, 2, N])
        kbd = front.take(4 * HH * N).rearrange("p (f m h n) -> p f m h n", f=2, m=2, h=HH)
        rmax = sb("rmax", [N, 2, H])
        sdiff = [front.take(H * N)[0:N].rearrange("p (h n) -> p h n", h=H) for m in range(2)]
        xexp = [front.take(H * N)[0:N].rearrange("p (h n) -> p h n", h=H) for m in range(2)]
        xtv = [front.take(H * XW).rearrange("p (h n) -> p h n", h=H) for m in range(2)]
        big = sb("big", [128, B * H * N])
        gall = big[0:N, :].rearrange("p (g n) -> p g n", n=N)
        wall = sb("wall", [ROWS, B * H, VA])
        csum = sb("csum", [N, B * H])
        mx2 = sb("mx2", [N, 2])
        grow = sb("grow", [1, 4])
        grow2 = sb("grow2", [1, 2])
        cscale = sb("cscale", [N, 1])
        area = Area(sb("area", [ROWS, 16 * HH * N]))
        T = [area.take(HH * N).rearrange("p (h n) -> p h n", n=N) for c in range(4)]
        Qs = [area.take(HH * N).rearrange("p (h n) -> p h n", n=N) for c in range(4)]
        Sm = [area.take(HH * N).rearrange("p (h n) -> p h n", n=N) for c in range(4)]
        V = [sb(f"V{c}", [N, HH, N]) for c in range(4)]
        Fin = [area.take(HH * N).rearrange("p (h n) -> p h n", n=N) for c in range(4)]
        den = sb("den", [N, 2, H])
        rden = sb("rden", [N, 2, H])
        ctxv = sb("ctxv", [N, 2, D])
        cT_h = sb("cT_h", [DH_, 2, NPATCH])
        cT_l = sb("cT_l", [DL_, 2, NPATCH])
        cTc_h = sb("cTc_h", [DH_, B])
        cTc_l = sb("cTc_l", [DL_, B])
        mv2 = sb("mv2", [128, TILES, 2])
        rstd2 = sb("rstd2", [128, TILES])
        stat2 = sb("stat2", [128, TILES, 6])
        area.again()
        front.again()
        x2 = area.take(TILES * D).rearrange("p (t d) -> p t d", d=D)
        hs = area.take(HID)
        hT = area.take(HID).rearrange("p (m n) -> p m n", m=MT)
        xin = [area.take(D) for p in range(2)]
        yout = [area.take(D) for p in range(2)]
        xe_h = area.take(SLOTS)
        xe_l = area.take(SLOTS)[0:DL_ + 1]
        in_p = front.take(G * SLOTS).rearrange("p (g n) -> p g n", g=G)
        x2T_h = front.take(NTOK)
        x2T_l = front.take(NTOK)[0:DL_]
        logit = sb("logit", [128, TILES, E])
        top = sb("top", [128, TILES, 8])
        topi = sb("topi", [128, TILES, 8], U32)
        topf = sb("topf", [128, TILES, TOPK])
        gk = sb("gk", [128, 4, TILES])
        chosen = sb("chosen", [128, TOPK, TILES, E])
        chosen_b = sb("chosen_b", [128, G, E], BF16)
        count_b = sb("count_b", [128, E], BF16)
        geq = front.take(G * E).rearrange("p (r t e) -> p r t e", r=TOPK, t=TILES)
        gate = sb("gate", [128, TILES, E])
        gateT = front.take(NTOK)[0:E]
        over = sb("over", [128, E, TILES])
        ntile = sb("ntile", [128, E])
        upto = sb("upto", [128, E, E])
        tend = sb("tend", [128, E])
        tstart = sb("tstart", [128, E])
        place = front.take(G * E).rearrange("p (g e) -> p g e", g=G)
        slot = sb("slot", [128, G])
        sge = front.take(G * (ST + 1)).rearrange("p (g j) -> p g j", g=G)
        in_j = front.take(G * ST).rearrange("p (g j) -> p g j", g=G)
        slot_j = sb("slot_j", [128, G])
        slot_p = sb("slot_p", [128, G])
        val = front.take(2 * G * ST).rearrange("p (g a j) -> p g a j", g=G, a=2)
        val_g = front.take(G * ST).rearrange("p (g j) -> p g j", g=G)
        row_out = sb("row_out", [128, 2, ST])
        row_add = sb("row_add", [128, ST])
        idx_get = sb("idx_get", [128, ST], U32)
        idx_add = sb("idx_add", [128, ST], U32)
        gslot = sb("gslot", [128, ST])
        tcmp = sb("tcmp", [1, ST, E])
        texp = sb("texp", [1, ST])
        texp_c = sb("texp_c", [1, ST])
        texp_i = sb("texp_i", [1, ST], I32)
        NI = E + TILES + (ST + 1) + ST + SLOTS + TILES + 1
        iota_i = sb("iota_i", [128, NI], I32)
        iota_f = sb("iota_f", [128, NI])
        cuts = [0]
        for n in (E, TILES, ST + 1, ST, SLOTS, TILES, 1):
            cuts.append(cuts[-1] + n)
        (i_exp, i_thr, i_slot, i_tile, i_col, i_row, i_pad), (eidx, thr, thr_slot, tidx, pidx, trow, pad_row) = (
            [t[:, cuts[n]:cuts[n + 1]] for n in range(7)] for t in (iota_i, iota_f))
        npad_row = sb("npad_row", [128, 1])
        tri_e = sb("tri_e", [128, E, E])
        before = sb("before", [128, 128])
        before_b = sb("before_b", [128, 128], BF16)
        ones_b = sb("ones_b", [128, 128], BF16)
        w1h = big[:, 0:E * HID].rearrange("p (e n) -> p e n", e=E)
        w1l = big[0:DL_ + 1, E * HID:2 * E * HID].rearrange("p (e n) -> p e n", e=E)
        w2a = sb("w2a", [128, E, MT * D])
        x2_rows = nc.dram_tensor("x2_rows", (NTOK, D), F32).ap()
        sums = nc.dram_tensor("sums", (NTOK + SLOTS, D), F32).ap()

        sx = [ctx.enter_context(nc.psum_tensor(f"sx{m}", [128, 2, 512], F32)) for m in range(2)]
        bank = [ctx.enter_context(nc.psum_tensor(f"bank{b}", [128, 512], F32)) for b in range(4)]
        half_heads = [sx[m][0:N, :, 0:HH * N].rearrange("p b (h n) -> p b h n", n=N) for m in range(2)]
        gram = [sx[m][0:N, :, 0:HH * XW].rearrange("p b (h n) -> p b h n", n=XW) for m in range(2)]
        HP, HTP = sx
        XP, YP = bank[0], bank[1:3]
        P = [sx[c // 2][0:N, c % 2, 0:HH * N] for c in range(4)]

        def sems(prefix, n):
            return [sem(f"{prefix}{k}") for k in range(n)]

        w_in, consts_in = sem("w_in"), sem("consts_in")
        patch_in, cls_in = sems("patch_in", 2), sem("cls_in")
        ident_zero, ident_ok, mask_one, mask_half, mask_ok, eidx_ok, tri_ok, before_ok = (
            sem(n) for n in ("ident_zero", "ident_ok", "mask_one", "mask_half", "mask_ok", "eidx_ok", "tri_ok",
                             "before_ok"))
        zero_ok, tiles_zero = sem("zero_ok"), sem("tiles_zero")
        ones_ok, mv_init, qbs_ok, logit_zero = (
            sem(n) for n in ("ones_ok", "mv_init", "qbs_ok", "logit_zero"))
        emb_done, emb_free, stat_ok, mv_ok = (
            sem(n) for n in ("emb_done", "emb_free", "stat_ok", "mv_ok"))
        eps_ok, sqrt_ok, rstd_ok = (sem(n) for n in ("eps_ok", "sqrt_ok", "rstd_ok"))
        xncls_ok, clsT_done, clsT_ok, xn_ok, xnT_done, xT_ok = (
            sem(n) for n in ("xncls_ok", "clsT_done", "clsT_ok", "xn_ok", "xnT_done", "xT_ok"))
        qk_done, v_done, q_ok, k_ok, kbd_ok, vx_ok = (
            sem(n) for n in ("qk_done", "v_done", "q_ok", "k_ok", "kbd_ok", "vx_ok"))
        score_done, rmax_ok, diff_ok, clamp_ok, exp_ok = (
            sem(n) for n in ("score_done", "rmax_ok", "diff_ok", "clamp_ok", "exp_ok"))
        xt_done, xtv_ok, csum_ok, gram_done, g_ok, w_ok = (
            sem(n) for n in ("xt_done", "xtv_ok", "csum_ok", "gram_done", "g_ok", "w_ok"))
        gmax_ok, gmaxT_done, gscale_ok, gbc_done, cscale_ok = (
            sem(n) for n in ("gmax_ok", "gmaxT_done", "gscale_ok",
                             "gbc_done", "cscale_ok"))
        t_ok, p1_done, qs_ok, sm_ok, v_ok, p2_done, fin_ok = (
            sems(n, 4) for n in ("t_ok", "p1_done", "qs_ok", "sm_ok", "v_ok", "p2_done", "fin_ok"))
        hb_ok, wv_done, den_ok, rden_ok, ctx_ok, ctxT_done, cT_ok, proj_done, h2_ok, stat2_ok, mv2_ok = (
            sem(n) for n in ("hb_ok", "wv_done", "den_ok", "rden_ok", "ctx_ok", "ctxT_done", "cT_ok", "proj_done",
                             "h2_ok", "stat2_ok", "mv2_ok"))
        eps2_ok, sqrt2_ok, rstd2_ok, x2_ok, x2T_done, x2T_ok = (
            sem(n) for n in ("eps2_ok", "sqrt2_ok", "rstd2_ok", "x2_ok", "x2T_done", "x2T_ok"))
        logit_done, logit_ok, top_ok, topi_ok, topf_ok, gdiff_ok, gexp_ok = (
            sem(n) for n in ("logit_done", "logit_ok", "top_ok", "topi_ok", "topf_ok", "gdiff_ok", "gexp_ok"))
        eqg_ok, gate_ok, gateT_done, gateT_ok, b2_done, acc_ok = (
            sem(n) for n in ("eqg_ok", "gate_ok", "gateT_done",
                             "gateT_ok", "b2_done", "acc_ok"))
        chosen_ok, count_ok, total_done, rank_done = (
            sem(n) for n in ("chosen_ok", "count_ok", "total_done",
                             "rank_done"))
        sge_ok, in_j_ok, slot_p_ok, in_p_ok, val_ok, valg_ok = (
            sem(n) for n in ("sge_ok", "in_j_ok", "slot_p_ok", "in_p_ok", "val_ok",
                             "valg_ok"))
        inv_done, row_out_ok, pad_ok, row_add_ok, idx_ok, invg_done, gslot_ok, tcmp_ok, texp_ok, texpi_ok, xones_ok = (
            sem(n) for n in ("inv_done", "row_out_ok", "pad_ok", "row_add_ok", "idx_ok", "invg_done", "gslot_ok",
                             "tcmp_ok", "texp_ok", "texpi_ok", "xones_ok"))
        w2_in, w1_in, x2_out, sums_init, add_out, out_done = (
            sem(n) for n in ("w2_in", "w1_in", "x2_out", "sums_init", "add_out", "out_done"))
        get_in = sems("get_in", 2)
        scale_step, place_step, gate_step = (sem(n) for n in ("scale_step", "place_step", "gate_step"))
        xe_done, xe_ok, l1_done, h_ok, hT_done, hT_ok, l2_done, y_ok = (
            sem(n) for n in ("xe_done", "xe_ok", "l1_done", "h_ok", "hT_done", "hT_ok", "l2_done", "y_ok"))

        block = ctx.enter_context(nc.Block())
        CONSTS = 12 * 16

        def settled(eng):
            eng.wait_ge(consts_in, CONSTS)

        def by_row(dram, t):
            if t == PAIRS:
                return [(dram[0:NTOK, :].rearrange("(i n) d -> i n d", n=N)[:, 0, :], slice(0, B))]
            return [(dram[(2 * t + m) * N + 1:(2 * t + m + 1) * N, :], slice(m * NPATCH, (m + 1) * NPATCH))
                    for m in range(2)]

        @block.sync
        def _(sp):
            sp.dma_start(tokw[:, :, :], tok_w).then_inc(w_in, 16)
            sp.dma_start(patch[0][:, :, :], xp[0]).then_inc(patch_in[0], 16)
            sp.dma_start(patch[1][:, :, :], xp[1]).then_inc(patch_in[1], 16)
            sp.dma_start(hid[0:B, PAIRS, :], cls_tok[0, 0:1, :].partition_broadcast(B)).then_inc(cls_in, 16)
            with sp.Fori(1, PAIRS // 2) as it:
                for p in range(2):
                    sp.wait_ge(emb_done, 2 * it + p - 1)
                    sp.dma_start(patch[p][:, :, :], xp[2 * it + p]).then_inc(patch_in[p], 16)
            sp.dma_start(w2a[:, :, :], w2).then_inc(w2_in, 16)
            for c in range(4):
                sp.wait_ge(t_ok[c], ITERS * (PAIRS - 1) + 1)
            sp.dma_start(w1h, w1[:, 0:DH_, :].rearrange("e p n -> p e n")).then_inc(w1_in, 16)
            sp.dma_start(w1l[0:DL_], w1[:, DH_:D, :].rearrange("e p n -> p e n")).then_inc(w1_in, 16)
            sp.dma_start(w1l[DL_:DL_ + 1], b1.rearrange("e n -> (e n)").unsqueeze(0).rearrange(
                "a (e n) -> a e n", e=E)).then_inc(w1_in, 16)
            for t in range(TILES):
                sp.wait_ge(x2_ok, t + 1)
                for rows, part in by_row(x2_rows, t):
                    sp.dma_start(rows, x2[part, t, :]).then_inc(x2_out, 16)
            for t in range(TILES):
                sp.wait_ge(acc_ok, t + 1)
                for rows, part in by_row(sums, t):
                    sp.dma_start(rows, hid[part, t, :]).then_inc(sums_init, 16)
            sp.dma_start(sums[NTOK:NTOK + SLOTS, :], hid[:, 0, :]).then_inc(sums_init, 16)
            sp.wait_ge(add_out, 16 * ST)
            sp.dma_start(out.rearrange("b n d -> (b n) d"), sums[0:NTOK, :]).then_inc(out_done, 16)
            sp.wait_ge(out_done, 16)

        @block.gpsimd
        def _(pool):
            pool.memset(ident[:, :], 0.0).then_inc(ident_zero, 1)
            pool.memset(mask[:, :], 1.0).then_inc(mask_one, 1)
            pool.memset(tri_e[:, :, :], 1.0).then_inc(tri_ok, 1)
            pool.memset(before[:, :], 1.0).then_inc(before_ok, 1)
            for t, step, n in ((i_exp, 1, E), (i_thr, SLOTS, TILES), (i_slot, SLOTS, ST + 1), (i_tile, 1, ST),
                               (i_col, 1, SLOTS)):
                pool.iota(t, pattern=[[step, n]], base=0, channel_multiplier=0).then_inc(eidx_ok, 1)
            for m in range(2):
                pool.wait_ge(eidx_ok, 5 + m)
                pool.iota(i_row[m * NPATCH:(m + 1) * NPATCH, 0:PAIRS], pattern=[[2 * N, PAIRS]], base=m * N + 1,
                          channel_multiplier=1).then_inc(eidx_ok, 1)
            pool.wait_ge(eidx_ok, 7)
            pool.iota(i_row[:, PAIRS:TILES], pattern=[[0, 1]], base=0, channel_multiplier=N).then_inc(eidx_ok, 1)
            pool.iota(i_pad, pattern=[[0, 1]], base=NTOK, channel_multiplier=1).then_inc(eidx_ok, 1)
            for tile in T + Qs + Sm + Fin:
                pool.memset(tile[:, :, :], 0.0).then_inc(tiles_zero, 1)
            pool.wait_ge(ident_zero, 1)
            pool.affine_select(out=ident[:, :], in_=ident[:, :], compare_op=ALU.not_equal, fill=1.0, base=0,
                               pattern=[[-1, 128]], channel_multiplier=1).then_inc(ident_ok, 1)
            pool.wait_ge(mask_one, 1)
            pool.affine_select(out=mask[:, :], in_=mask[:, :], compare_op=ALU.is_ge, fill=0.0, base=0,
                               pattern=[[-DH, HH]], channel_multiplier=1).then_inc(mask_half, 1)
            pool.wait_ge(mask_half, 1)
            pool.affine_select(out=mask[:, :], in_=mask[:, :], compare_op=ALU.is_ge, fill=0.0, base=DH - 1,
                               pattern=[[DH, HH]], channel_multiplier=-1).then_inc(mask_ok, 1)
            pool.wait_ge(tri_ok, 1)
            pool.affine_select(out=tri_e[:, :, :], in_=tri_e[:, :, :], compare_op=ALU.is_ge, fill=0.0, base=0,
                               pattern=[[1, E], [-1, E]], channel_multiplier=0).then_inc(tri_ok, 1)
            pool.wait_ge(before_ok, 1)
            pool.affine_select(out=before[:, :], in_=before[:, :], compare_op=ALU.is_ge, fill=0.0, base=-1,
                               pattern=[[1, 128]], channel_multiplier=-1).then_inc(before_ok, 1)
            pool.wait_ge(eidx_ok, 9)
            pool.tensor_copy(iota_f[:, :], iota_i[:, :]).then_inc(eidx_ok, 1)

            def spread_k(i):
                pool.wait_ge(k_ok, 2 * i + 2)
                for f in range(2):
                    pool.tensor_tensor(
                        kbd[0:CH, f], kT[:, f].unsqueeze(2).broadcast_to([CH, 2, HH, N]),
                        mask[:, :].unsqueeze(1).unsqueeze(3).broadcast_to([CH, 2, HH, N]), ALU.mult,
                    ).then_inc(kbd_ok, 1)

            pool.wait_ge(mask_ok, 1)
            with pool.Fori(0, PAIRS) as i:
                spread_k(i)

            pool.wait_ge(xn_ok, PAIRS)
            pool.wait_ge(xncls_ok, 1)
            pool.tensor_tensor(hid[:, 0:PAIRS, :], hid[:, 0:PAIRS, :],
                               pb[:, :].unsqueeze(1).broadcast_to([128, PAIRS, D]), ALU.add).then_inc(hb_ok, 1)
            pool.tensor_tensor(hid[0:B, PAIRS, :], hid[0:B, PAIRS, :], pb[0:B, :], ALU.add).then_inc(hb_ok, 1)

            def combine(g):
                for c in range(4):
                    pool.wait_ge(qs_ok[c], g + 1)
                    pool.wait_ge(sm_ok[c], g + 1)
                    pool.tensor_tensor(V[c][:, :, :], Qs[c][0:N, :, :], Sm[c][0:N, :, :], ALU.add).then_inc(v_ok[c], 1)

            with pool.Fori(0, PAIRS * ITERS) as g:
                combine(g)

            def gather(j):
                if j >= 2:
                    pool.wait_ge(xe_done, j - 1)
                pool.indirect_dma_start(out=xin[j % 2], out_offset=None, in_=x2_rows,
                                        in_offset=bass.IndirectOffsetOnAxis(ap=idx_get[:, j:j + 1], axis=0),
                                        ).then_inc(get_in[j % 2], 16)

            pool.wait_ge(idx_ok, 2)
            pool.wait_ge(x2_out, 16 * (2 * PAIRS + 1))
            gather(0)
            gather(1)
            pool.wait_ge(sums_init, 16 * (2 * PAIRS + 2))
            for j in range(ST):
                if j + 2 < ST:
                    gather(j + 2)
                pool.wait_ge(y_ok, j + 1)
                if j:
                    pool.wait_ge(add_out, 16 * j)
                pool.indirect_dma_start(out=sums, out_offset=bass.IndirectOffsetOnAxis(ap=idx_add[:, j:j + 1], axis=0),
                                        in_=yout[j % 2], in_offset=None, compute_op=ALU.add).then_inc(add_out, 16)

        @block.scalar
        def _(act):
            for dst, src in ((tokb[:, :], tok_b.partition_broadcast(128)),
                             (wqkv_h[:, :], qkv_w[0:DH_, :]), (wqkv_l[:, :], qkv_w[DH_:D, :]),
                             (qkb[:, :], qk_b), (vb[:, :], v_b.partition_broadcast(128)),
                             (wp_h[:, :], proj_w[0:DH_, :]), (wp_l[:, :], proj_w[DH_:D, :]),
                             (pb[:, :], proj_b.partition_broadcast(128)),
                             (wg_h[:, :], wg[0:DH_, :]), (wg_l[:, :], wg[DH_:D, :]),
                             (bgb[:, :], bg.partition_broadcast(128)),
                             (b2t[:, :], b2)):
                act.dma_start(dst, src).then_inc(consts_in, 16)
            act.wait_ge(consts_in, CONSTS)
            act.wait_ge(zero_ok, 5)
            act.wait_ge(tiles_zero, 16)

            act.mul(qbs[:, :], qkb[:, 0:2], DH ** -0.5).then_inc(qbs_ok, 1)
            act.wait_ge(eps_ok, 1)
            act.activation(rstd[:, :], rstd[:, :], ACT.Sqrt).then_inc(sqrt_ok, 1)
            act.wait_ge(clsT_done, 1)
            for k, (dst, rows) in enumerate(((xT_h, DH_), (xT_l, DL_))):
                act.copy(dst[:, :, NPATCH], bank[0][0:rows, k * 16:k * 16 + 2]).then_inc(clsT_ok, 1)

            def transposed_x(i):
                act.wait_ge(xnT_done, i + 1)
                if not isinstance(i, int) or i:
                    act.wait_ge(v_done, i)
                for k, (dst, rows) in enumerate(((xT_h, DH_), (xT_l, DL_))):
                    act.copy(dst[:, :, 0:NPATCH],
                             bank[0][0:rows, 128 * k:128 * k + 128].rearrange("p (m n) -> p m n", m=2),
                             ).then_inc(xT_ok, 1)

            def qk_out(i):
                act.wait_ge(qk_done, i + 1)
                if not isinstance(i, int) or i:
                    act.wait_ge(score_done, 2 * i)
                    act.wait_ge(kbd_ok, 2 * i)
                for f in range(2):
                    act.activation(qT[0:CH, f].rearrange("p m n -> p (m n)"), bank[1][0:CH, 130 * f:130 * f + 130],
                                   ACT.Identity, bias=qbs[:, f:f + 1], scale=DH ** -0.5).then_inc(q_ok, 1)
                for f, src in ((0, bank[1][0:CH, 260:390]), (1, bank[0][0:CH, 256:386])):
                    act.activation(kT[:, f].rearrange("p m n -> p (m n)"), src,
                                   ACT.Identity, bias=qkb[:, 2 + f:3 + f], scale=1.0).then_inc(k_ok, 1)

            def attention(i, more):
                if more:
                    transposed_x(i + 1)
                for m in range(2):
                    act.wait_ge(clamp_ok, 2 * i + m + 1)
                    act.activation(xexp[m][:, :, :], sdiff[m][:, :, :], ACT.Exp).then_inc(exp_ok, 1)
                if more:
                    qk_out(i + 1)
                for m in range(2):
                    act.wait_ge(xt_done, 2 * i + m + 1)
                    act.copy(xtv[m][0:N, :, 0:N].rearrange("p (f h) n -> p f h n", f=2),
                             half_heads[m]).then_inc(xtv_ok, 1)
                for m in range(2):
                    act.wait_ge(g_ok, 2 * i + m + 1)
                    settled(act)
                    act.copy(wall[0:N, bass.ds((2 * i + m) * H, H), :].rearrange("p (f h) v -> p f h v", f=2),
                             gram[m][:, :, :, N:XW]).then_inc(w_ok, 1)

            transposed_x(0)
            qk_out(0)
            with act.Fori(0, PAIRS - 2) as i:
                attention(i, True)
            attention(PAIRS - 2, True)
            attention(PAIRS - 1, False)

            def square_out(g):
                for c in range(4):
                    act.wait_ge(p1_done[c], g + 1)
                    act.mul(Qs[c][0:N, :, :].rearrange("p h n -> p (h n)"), P[c], BETA).then_inc(qs_ok[c], 1)

            def context_out(j):
                act.wait_ge(ctxT_done, j + 1)
                for k, (dst, dstc, rows) in enumerate(((cT_h, cTc_h, DH_), (cT_l, cTc_l, DL_))):
                    settled(act)
                    src = bank[1][0:rows, 130 * k:130 * k + 130].rearrange("p (m n) -> p m n", m=2)
                    act.copy(dst[:, :, :], src[:, :, 0:NPATCH]).then_inc(cT_ok, 1)
                    act.copy(dstc[:, bass.ds(2 * j, 2)], src[:, :, NPATCH]).then_inc(cT_ok, 1)

            with act.Fori(0, ITERS) as g:
                square_out(g)
            with act.Fori(1, PAIRS) as j:
                with act.Fori(0, ITERS) as it:
                    square_out(ITERS * j + it)
                context_out(j - 1)
            context_out(PAIRS - 1)

            act.wait_ge(eps2_ok, 1)
            act.activation(rstd2[:, :], rstd2[:, :], ACT.Sqrt).then_inc(sqrt2_ok, 1)
            for t in range(TILES):
                rows = 128 if t < PAIRS else B
                act.wait_ge(x2T_done, t + 1)
                for k, (dst, r) in enumerate(((x2T_h, DH_), (x2T_l, DL_))):
                    act.copy(dst[:, 128 * t:128 * t + rows],
                             bank[t % 2][0:r, 128 * k:128 * k + rows]).then_inc(x2T_ok, 1)
            act.wait_ge(gdiff_ok, 1)
            act.activation(gk[:, 1, :], gk[:, 0, :], ACT.Exp).then_inc(gexp_ok, 1)

            def tokens_out(j):
                act.wait_ge(xe_done, j + 1)
                if not isinstance(j, int) or j:
                    act.wait_ge(l1_done, j)
                act.copy(xe_h, XP[:, 0:SLOTS]).then_inc(xe_ok, 1)
                act.copy(xe_l[0:DL_], XP[0:DL_, SLOTS:2 * SLOTS]).then_inc(xe_ok, 1)

            def hidden_out(j):
                act.wait_ge(l1_done, j + 1)
                if not isinstance(j, int) or j:
                    act.wait_ge(hT_done, j)
                for f in range(2):
                    act.activation(hs[:, HH2 * f:HH2 * f + HH2], HP[:, f, 0:HH2], ACT.Relu).then_inc(h_ok, 1)

            tokens_out(0)
            hidden_out(0)
            tokens_out(1)
            for t in range(TILES):
                rows = 128 if t < PAIRS else B
                act.wait_ge(gateT_done, t + 1)
                act.copy(gateT[:, 128 * t:128 * t + rows], bank[3][0:E, 128 * (t % 2):128 * (t % 2) + rows],
                         ).then_inc(gateT_ok, 1)

            with act.Fori(0, ST - 2) as j:
                hidden_out(j + 1)
                tokens_out(j + 2)
            hidden_out(ST - 1)

        @block.vector
        def _(dve):
            dve.memset(ones[:, :], 1.0).then_inc(ones_ok, 1)
            dve.memset(mv[:, :, :], 1.0).then_inc(mv_init, 1)
            dve.memset(mv2[:, :, :], 1.0).then_inc(mv_init, 1)
            dve.memset(chosen[:, :, :, :], 0.0).then_inc(mv_init, 1)
            dve.memset(ones_b[:, :], 1.0).then_inc(mv_init, 1)
            dve.wait_ge(before_ok, 2)
            dve.tensor_copy(before_b[:, :], before[:, :]).then_inc(mv_init, 1)
            dve.wait_ge(eidx_ok, 10)
            dve.tensor_scalar(npad_row[:, :], pad_row, -1.0, None, ALU.mult).then_inc(pad_ok, 1)
            dve.memset(logit[:, :, :], 0.0).then_inc(logit_zero, 1)
            for m in range(2):
                dve.memset(xtv[m][:, :, :], 0.0).then_inc(emb_free, 1)
            dve.memset(qT[CH:ROWS], 0.0).then_inc(zero_ok, 1)
            dve.memset(kbd[CH:ROWS], 0.0).then_inc(zero_ok, 1)
            dve.memset(wall[:, :, :], 0.0).then_inc(zero_ok, 1)
            dve.wait_ge(emb_free, 2)
            for m in range(2):
                dve.memset(xtv[m][0:N, :, XW - 1:XW], 1.0).then_inc(zero_ok, 1)
            dve.wait_ge(consts_in, CONSTS)
            dve.wait_ge(mv_init, 5)
            dve.wait_ge(tiles_zero, 16)
            dve.wait_ge(zero_ok, 5)

            def mean_variance(stats, dst, stats_sem, mv_sem):
                dve.wait_ge(stats_sem, TILES)
                for t in range(TILES):
                    rows = 128 if t < PAIRS else B
                    dve.bn_aggr(dst[0:rows, t, :], stats[0:rows, t, :]).then_inc(mv_sem, 1)
                dve.wait_ge(mv_sem, TILES)

            with dve.Fori(0, PAIRS // 2) as it:
                for p in range(2):
                    t = 2 * it + p
                    dve.wait_ge(emb_done, t + 1)
                    dve.tensor_tensor(hid[:, t, :], bank[p][:, 0:D], tokb[:, :], ALU.add).then_inc(emb_free, 1)
                    dve.wait_ge(emb_free, t + 3)
                    settled(dve)
                    dve.bn_stats(stat[:, t, :], hid[:, t, :]).then_inc(stat_ok, 1)
            dve.wait_ge(cls_in, 16)
            dve.bn_stats(stat[0:B, PAIRS, :], hid[0:B, PAIRS, :]).then_inc(stat_ok, 1)
            mean_variance(stat, mv, stat_ok, mv_ok)
            dve.tensor_scalar(rstd[:, :], mv[:, :, 1], EPS, None, ALU.add).then_inc(eps_ok, 1)
            dve.wait_ge(sqrt_ok, 1)
            dve.reciprocal(rstd[:, :], rstd[:, :]).then_inc(rstd_ok, 1)
            dve.wait_ge(rstd_ok, 1)
            dve.tensor_scalar(xncls[:, :], hid[0:B, PAIRS, :], mv[0:B, PAIRS, 0:1], rstd[0:B, PAIRS:TILES],
                              ALU.subtract, ALU.mult).then_inc(xncls_ok, 1)

            def normalise(i):
                if not isinstance(i, int) or i:
                    dve.wait_ge(xnT_done, i)
                dve.tensor_scalar(xn[:, :], hid[:, i, :], mv[:, i, 0:1], rstd[:, i:i + 1] if isinstance(i, int) else
                                  rstd[:, bass.ds(i, 1)], ALU.subtract, ALU.mult).then_inc(xn_ok, 1)

            normalise(0)
            normalise(1)

            def attention(i, norm):
                def maximum(m):
                    dve.wait_ge(score_done, 2 * i + m + 1)
                    dve.tensor_reduce(rmax[:, m, :].rearrange("p (f h) -> p f h", f=2), half_heads[m],
                                      AX.X, ALU.max).then_inc(rmax_ok, 1)
                    dve.wait_ge(rmax_ok, 2 * i + m + 1)
                    dve.tensor_tensor(
                        sdiff[m][:, :, :].rearrange("p (f h) n -> p f h n", f=2), half_heads[m],
                        rmax[:, m, :].rearrange("p (f h) -> p f h", f=2).unsqueeze(3).broadcast_to([N, 2, HH, N]),
                        ALU.subtract).then_inc(diff_ok, 1)
                    dve.wait_ge(diff_ok, 2 * i + m + 1)
                    dve.tensor_scalar(sdiff[m][:, :, :], sdiff[m][:, :, :], -88.0, None,
                                      ALU.max).then_inc(clamp_ok, 1)

                def values(m):
                    dve.wait_ge(v_done, i + 1)
                    dve.tensor_tensor(
                        xtv[m][0:N, :, N:XW - 1], bank[2][0:N, D * m:D * m + D].rearrange("p (h d) -> p h d", h=H),
                        vb[0:N, :].rearrange("p (h d) -> p h d", h=H), ALU.add).then_inc(vx_ok, 1)

                maximum(0)
                values(0)
                values(1)
                maximum(1)
                if norm:
                    normalise(i + 2)
                for m in range(2):
                    dve.wait_ge(xtv_ok, 2 * i + m + 1)
                    dve.tensor_reduce(csum[:, bass.ds((2 * i + m) * H, H)], xtv[m][0:N, :, 0:N],
                                      AX.X, ALU.add).then_inc(csum_ok, 1)
                for m in range(2):
                    dve.wait_ge(gram_done, 2 * i + m + 1)
                    dve.tensor_copy(gall[:, bass.ds((2 * i + m) * H, H), :].rearrange("p (f h) n -> p f h n", f=2),
                                    gram[m][:, :, :, 0:N]).then_inc(g_ok, 1)

            with dve.Fori(0, PAIRS - 2) as i:
                attention(i, True)
            attention(PAIRS - 2, False)
            attention(PAIRS - 1, False)

            dve.wait_ge(csum_ok, B)
            dve.tensor_reduce(mx2[:, 0:1], csum[:, :], AX.X, ALU.max).then_inc(gmax_ok, 1)
            dve.wait_ge(w_ok, B)
            dve.tensor_reduce(mx2[:, 1:2], wall[0:N, :, VA - 1], AX.X, ALU.max).then_inc(gmax_ok, 1)
            dve.wait_ge(gmaxT_done, 1)
            dve.tensor_reduce(grow[0:1, 0:2], bank[2][0:1, 0:2 * N].rearrange("p (a n) -> p a n", a=2),
                              AX.X, ALU.max).then_inc(scale_step, 1)
            dve.wait_ge(scale_step, 1)
            dve.tensor_tensor(grow[0:1, 2:3], grow[0:1, 0:1], grow[0:1, 1:2], ALU.mult).then_inc(scale_step, 1)
            dve.wait_ge(scale_step, 2)
            dve.tensor_scalar(grow[0:1, 3:4], grow[0:1, 2:3], 1e-15, None, ALU.add).then_inc(scale_step, 1)
            dve.wait_ge(scale_step, 3)
            dve.reciprocal(grow2[0:1, 0:1], grow[0:1, 3:4]).then_inc(scale_step, 1)
            dve.wait_ge(scale_step, 4)
            dve.tensor_scalar(grow2[0:1, 1:2], grow2[0:1, 0:1], -4.0 * KAPPA, None, ALU.mult).then_inc(gscale_ok, 1)
            dve.wait_ge(gbc_done, 1)
            dve.tensor_copy(cscale[:, :], bank[2][0:N, 256:257]).then_inc(cscale_ok, 1)
            dve.wait_ge(cscale_ok, 1)
            dve.wait_ge(g_ok, B)

            def start(j, c):
                dve.tensor_scalar(T[c][0:N, :, :], gall[:, bass.ds((4 * j + c) * HH, HH), :], cscale[:, 0:1], None,
                                  ALU.mult).then_inc(t_ok[c], 1)

            def middle(g, c):
                dve.wait_ge(qs_ok[c], g + 1)
                dve.scalar_tensor_tensor(Sm[c][0:N, :, :].rearrange("p h n -> p (h n)"),
                                         T[c][0:N, :, :].rearrange("p h n -> p (h n)"), 28.0 * KAPPA, P[c],
                                         ALU.mult, ALU.add).then_inc(sm_ok[c], 1)

            def close(g, c, dst, done):
                dve.wait_ge(p2_done[c], g + 1)
                dve.wait_ge(v_ok[c], g + 1)
                dve.scalar_tensor_tensor(dst[c][0:N, :, :].rearrange("p h n -> p (h n)"),
                                         V[c][:, :, :].rearrange("p h n -> p (h n)"), CV, P[c],
                                         ALU.mult, ALU.add).then_inc(done[c], 1)

            def context(j):
                dve.wait_ge(wv_done, j + 1)
                prod = bank[0][0:N, 0:2 * H * VA].rearrange("p (g v) -> p g v", v=VA)
                dve.tensor_scalar(den[:, :, :].rearrange("p m h -> p (m h)"), prod[:, :, VA - 1],
                                  -0.25 / KAPPA, 1e-8, ALU.mult, ALU.max).then_inc(den_ok, 1)
                dve.wait_ge(den_ok, j + 1)
                dve.reciprocal(rden[:, :, :], den[:, :, :]).then_inc(rden_ok, 1)
                dve.wait_ge(rden_ok, j + 1)
                dve.scalar_tensor_tensor(
                    ctxv[:, :, :].rearrange("p m (h d) -> p (m h) d", d=DH), prod[:, :, 0:DH], -0.25 / KAPPA,
                    rden[:, :, :].rearrange("p m h -> p (m h)").unsqueeze(2).broadcast_to([N, 2 * H, DH]),
                    ALU.mult, ALU.mult).then_inc(ctx_ok, 1)

            def residual(j, rows):
                dve.wait_ge(proj_done, j + 1)
                dve.tensor_tensor(hid[0:rows, j, :], bank[2][0:rows, 0:D], hid[0:rows, j, :],
                                  ALU.add).then_inc(h2_ok, 1)
                dve.wait_ge(h2_ok, j + 1)
                settled(dve)
                dve.bn_stats(stat2[0:rows, j, :], hid[0:rows, j, :]).then_inc(stat2_ok, 1)

            def pair(j, tail, more):
                g0 = ITERS * j
                for c in range(4):
                    middle(g0, c)
                for c in range(4):
                    close(g0, c, T, t_ok)
                if tail:
                    context(j - 1)
                with dve.Fori(1, ITERS - 1) as it:
                    for c in range(4):
                        middle(g0 + it, c)
                    for c in range(4):
                        close(g0 + it, c, T, t_ok)
                for c in range(4):
                    middle(g0 + ITERS - 1, c)
                for c in range(4):
                    if more:
                        dve.wait_ge(sm_ok[c], g0 + ITERS)
                        start(j + 1, c)
                for c in range(4):
                    close(g0 + ITERS - 1, c, Fin, fin_ok)
                if tail:
                    residual(j - 1, 128)

            dve.wait_ge(hb_ok, 2)
            for c in range(4):
                start(0, c)
            pair(0, False, True)
            with dve.Fori(1, PAIRS - 1) as j:
                pair(j, True, True)
            pair(PAIRS - 1, True, False)
            context(PAIRS - 1)
            residual(PAIRS - 1, 128)
            residual(PAIRS, B)

            mean_variance(stat2, mv2, stat2_ok, mv2_ok)
            dve.tensor_scalar(rstd2[:, :], mv2[:, :, 1], EPS, None, ALU.add).then_inc(eps2_ok, 1)
            dve.wait_ge(sqrt2_ok, 1)
            dve.reciprocal(rstd2[:, :], rstd2[:, :]).then_inc(rstd2_ok, 1)
            dve.wait_ge(rstd2_ok, 1)
            for t in range(TILES):
                rows = 128 if t < PAIRS else B
                dve.tensor_scalar(x2[0:rows, t, :], hid[0:rows, t, :], mv2[0:rows, t, 0:1],
                                  rstd2[0:rows, t:t + 1], ALU.subtract, ALU.mult).then_inc(x2_ok, 1)

            dve.wait_ge(logit_done, 1)
            dve.wait_ge(logit_zero, 1)
            lp = bank[3][:, 0:TILES * E].rearrange("p (t e) -> p t e", e=E)
            dve.tensor_tensor(logit[:, 0:PAIRS, :], lp[:, 0:PAIRS, :],
                              bgb[:, :].unsqueeze(1).broadcast_to([128, PAIRS, E]), ALU.add).then_inc(logit_ok, 1)
            dve.tensor_tensor(logit[0:B, PAIRS, :], lp[0:B, PAIRS, :], bgb[0:B, :], ALU.add).then_inc(logit_ok, 1)
            dve.wait_ge(logit_ok, 2)
            for t in range(TILES):
                dve.max(top[:, t, :], logit[:, t, :]).then_inc(top_ok, 1)
            dve.wait_ge(top_ok, TILES)
            for t in range(TILES):
                dve.max_index(topi[:, t, :], top[:, t, :], logit[:, t, :]).then_inc(topi_ok, 1)
            dve.tensor_tensor(gk[:, 0, :], top[:, :, 1], top[:, :, 0], ALU.subtract).then_inc(gdiff_ok, 1)
            dve.memset(xe_l[DL_:DL_ + 1], 1.0).then_inc(xones_ok, 1)
            dve.wait_ge(topi_ok, TILES)
            dve.tensor_copy(topf[:, :, :], topi[:, :, 0:TOPK]).then_inc(topf_ok, 1)
            dve.wait_ge(topf_ok, 1)
            for r in range(TOPK):
                for rows, ts in ((128, slice(0, PAIRS)), (B, slice(PAIRS, TILES))):
                    n = ts.stop - ts.start
                    dve.tensor_tensor(chosen[0:rows, r, ts, :], eidx[0:rows].unsqueeze(1).broadcast_to([rows, n, E]),
                                      topf[0:rows, ts, r].unsqueeze(2).broadcast_to([rows, n, E]),
                                      ALU.is_equal).then_inc(chosen_ok, 1)
            dve.wait_ge(chosen_ok, 2 * TOPK)
            chosen_g = chosen[:, :, :, :].rearrange("p r t e -> p (r t) e")
            with nc.allow_low_precision("a count of at most 18 is exact in bfloat16"):
                dve.tensor_reduce(count_b[:, :], chosen_g.rearrange("p g e -> p e g"), AX.X, ALU.add,
                                  ).then_inc(count_ok, 1)
            dve.tensor_copy(chosen_b[:, :, :], chosen_g).then_inc(chosen_ok, 1)
            dve.wait_ge(total_done, 1)
            dve.tensor_tensor(over[:, :, :], bank[2][:, 0:E].unsqueeze(2).broadcast_to([128, E, TILES]),
                              thr.unsqueeze(1).broadcast_to([128, E, TILES]), ALU.is_gt).then_inc(place_step, 1)
            dve.wait_ge(place_step, 1)
            dve.tensor_reduce(ntile[:, :], over[:, :, :], AX.X, ALU.add).then_inc(place_step, 1)
            dve.wait_ge(place_step, 2)
            dve.tensor_tensor(upto[:, :, :], ntile[:, :].unsqueeze(1).broadcast_to([128, E, E]), tri_e[:, :, :],
                              ALU.mult).then_inc(place_step, 1)
            dve.wait_ge(place_step, 3)
            dve.tensor_reduce(tend[:, :], upto[:, :, :], AX.X, ALU.add).then_inc(place_step, 1)
            dve.wait_ge(place_step, 4)
            dve.tensor_tensor(tstart[:, :], tend[:, :], ntile[:, :], ALU.subtract).then_inc(place_step, 1)
            dve.tensor_tensor(tcmp[:, :, :], tidx[0:1].unsqueeze(2).broadcast_to([1, ST, E]),
                              tend[0:1, :].unsqueeze(1).broadcast_to([1, ST, E]), ALU.is_ge).then_inc(tcmp_ok, 1)
            dve.wait_ge(place_step, 5)
            dve.wait_ge(rank_done, 1)
            dve.scalar_tensor_tensor(place[:, :, :], tstart[:, :].unsqueeze(1).broadcast_to([128, G, E]), float(SLOTS),
                                     bank[1][:, 0:G * E].rearrange("p (g e) -> p g e", e=E), ALU.mult,
                                     ALU.add).then_inc(place_step, 1)
            dve.wait_ge(place_step, 6)
            dve.tensor_tensor(place[:, :, :], place[:, :, :], chosen_g, ALU.mult).then_inc(place_step, 1)
            dve.wait_ge(place_step, 7)
            dve.tensor_reduce(slot[:, :], place[:, :, :], AX.X, ALU.add).then_inc(place_step, 1)
            dve.wait_ge(place_step, 8)
            dve.tensor_tensor(sge[:, :, :], slot[:, :].unsqueeze(2).broadcast_to([128, G, ST + 1]),
                              thr_slot.unsqueeze(1).broadcast_to([128, G, ST + 1]), ALU.is_ge).then_inc(sge_ok, 1)
            dve.wait_ge(sge_ok, 1)
            dve.tensor_reduce(slot_j[:, :], sge[:, :, 1:ST + 1], AX.X, ALU.add).then_inc(sge_ok, 1)
            dve.tensor_tensor(in_j[:, :, :], sge[:, :, 0:ST], sge[:, :, 1:ST + 1], ALU.subtract).then_inc(in_j_ok, 1)
            dve.wait_ge(sge_ok, 2)
            dve.scalar_tensor_tensor(slot_p[:, :], slot_j[:, :], -float(SLOTS), slot[:, :], ALU.mult,
                                     ALU.add).then_inc(slot_p_ok, 1)
            dve.wait_ge(in_j_ok, 1)
            for r in range(TOPK):
                dve.tensor_tensor(val[:, TILES * r:TILES * (r + 1), 0, :], in_j[:, TILES * r:TILES * (r + 1), :],
                                  trow.unsqueeze(2).broadcast_to([128, TILES, ST]), ALU.mult).then_inc(val_ok, 1)
            dve.tensor_copy(val[:, :, 1, :], in_j[:, :, :]).then_inc(val_ok, 1)
            dve.wait_ge(slot_p_ok, 1)
            for q in range(3):
                gs = slice(6 * q, 6 * q + 6)
                dve.tensor_tensor(in_p[:, gs, :], slot_p[:, gs].unsqueeze(2).broadcast_to([128, 6, SLOTS]),
                                  pidx.unsqueeze(1).broadcast_to([128, 6, SLOTS]), ALU.is_equal).then_inc(in_p_ok, 1)
            dve.wait_ge(tcmp_ok, 1)
            dve.tensor_reduce(texp[:, :], tcmp[:, :, :], AX.X, ALU.add).then_inc(texp_ok, 1)
            dve.wait_ge(texp_ok, 1)
            dve.tensor_scalar(texp_c[:, :], texp[:, :], float(E - 1), None, ALU.min).then_inc(texp_ok, 1)
            dve.wait_ge(texp_ok, 2)
            dve.tensor_copy(texp_i[:, :], texp_c[:, :]).then_inc(texpi_ok, 1)
            dve.wait_ge(inv_done, 1)
            dve.tensor_copy(row_out[:, :, :], bank[2][:, 64:64 + 2 * ST].rearrange("p (a j) -> p a j", a=2),
                            ).then_inc(row_out_ok, 1)
            dve.wait_ge(row_out_ok, 1)
            dve.tensor_copy(idx_get[:, :], row_out[:, 0, :]).then_inc(idx_ok, 1)
            dve.wait_ge(pad_ok, 1)
            dve.tensor_scalar(row_add[:, :], row_out[:, 1, :], npad_row[:, 0:1], pad_row, ALU.mult,
                              ALU.add).then_inc(pad_ok, 1)
            dve.wait_ge(pad_ok, 2)
            dve.tensor_tensor(row_out[:, 1, :], row_add[:, :], row_out[:, 0, :], ALU.add).then_inc(row_add_ok, 1)
            dve.wait_ge(row_add_ok, 1)
            dve.tensor_copy(idx_add[:, :], row_out[:, 1, :]).then_inc(idx_ok, 1)
            dve.wait_ge(gexp_ok, 1)
            dve.tensor_scalar(gk[:, 0, :], gk[:, 1, :], 1.0, None, ALU.add).then_inc(gate_step, 1)
            dve.wait_ge(gate_step, 1)
            dve.reciprocal(gk[:, 2, :], gk[:, 0, :]).then_inc(gate_step, 1)
            dve.wait_ge(gate_step, 2)
            dve.tensor_tensor(gk[:, 3, :], gk[:, 1, :], gk[:, 2, :], ALU.mult).then_inc(gate_step, 1)
            dve.wait_ge(gate_step, 3)
            for r in range(TOPK):
                dve.tensor_tensor(geq[:, r, :, :], chosen[:, r, :, :],
                                  gk[:, 2 + r, :].unsqueeze(2).broadcast_to([128, TILES, E]),
                                  ALU.mult).then_inc(eqg_ok, 1)
            dve.tensor_tensor(val_g[:, :, :], in_j[:, :, :],
                              gk[:, 2:4, :].rearrange("p r t -> p (r t)").unsqueeze(2).broadcast_to([128, G, ST]),
                              ALU.mult).then_inc(valg_ok, 1)
            dve.wait_ge(eqg_ok, 2)
            dve.tensor_tensor(gate[:, :, :], geq[:, 0, :, :], geq[:, 1, :, :], ALU.add).then_inc(gate_ok, 1)
            dve.wait_ge(invg_done, 1)
            dve.tensor_copy(gslot[:, :], bank[2][:, 128:128 + ST]).then_inc(gslot_ok, 1)
            dve.wait_ge(gslot_ok, 1)
            for t in range(TILES):
                rows = 128 if t < PAIRS else B
                dve.wait_ge(b2_done, t + 1)
                dve.tensor_tensor(hid[0:rows, t, :], bank[1 + t % 2][0:rows, 0:D], hid[0:rows, t, :],
                                  ALU.add).then_inc(acc_ok, 1)

            def tile(j, p):
                dve.wait_ge(hT_done, j + 1)
                for f in range(2):
                    dve.tensor_copy(hT[:, 3 * f:3 * f + 3, :].rearrange("p m n -> p (m n)"),
                                    HTP[:, f, 0:3 * SLOTS]).then_inc(hT_ok, 1)
                dve.wait_ge(l2_done, j + 1)
                if not isinstance(j, int) or j >= 2:
                    dve.wait_ge(add_out, 16 * (j - 1))
                dve.tensor_scalar(yout[p], YP[p][:, 0:D], gslot[:, bass.ds(j, 1)], None, ALU.mult).then_inc(y_ok, 1)

            tile(0, 0)
            tile(1, 1)
            with dve.Fori(1, ST // 2) as jj:
                for p in range(2):
                    tile(2 * jj + p, p)

        @block.tensor
        def _(pe):
            def two(dst, st_h, st_l, mv_h, mv_l):
                pe.matmul(dst, st_h, mv_h, start=True, stop=False)
                return pe.matmul(dst, st_l, mv_l, start=False, stop=True)

            pe.wait_ge(w_in, 16)
            with pe.Fori(0, PAIRS // 2) as it:
                for p in range(2):
                    pe.wait_ge(patch_in[p], 16 * it + 16)
                    pe.wait_ge(emb_free, 2 * it + p + 1)
                    for k in range(KT):
                        last = pe.matmul(bank[p][:, 0:D], patch[p][:, k, :], tokw[:, k, :],
                                         start=(k == 0), stop=(k == KT - 1))
                    last.then_inc(emb_done, 1)

            pe.wait_ge(ident_ok, 1)
            pe.wait_ge(consts_in, CONSTS)
            pe.wait_ge(xncls_ok, 1)
            pe.transpose(bank[0][:, 0:B], xncls[:, 0:DH_], ident[0:B, 0:B])
            pe.transpose(bank[0][0:DL_, B:2 * B], xncls[:, DH_:D], ident[0:B, 0:B]).then_inc(clsT_done, 1)
            pe.wait_ge(clsT_ok, 2)

            def transpose_x(i):
                pe.wait_ge(xn_ok, i + 1)
                if not isinstance(i, int) or i:
                    pe.wait_ge(xT_ok, 2 * i)
                    pe.wait_ge(k_ok, 2 * i)
                pe.transpose(bank[0][:, 0:128], xn[:, 0:DH_], ident[:, :])
                pe.transpose(bank[0][0:DL_, 128:256], xn[:, DH_:D], ident[:, :]).then_inc(xnT_done, 1)

            def project(i):
                pe.wait_ge(xT_ok, 2 * i + 2)
                if not isinstance(i, int) or i:
                    pe.wait_ge(q_ok, 2 * i)
                    pe.wait_ge(k_ok, 2 * i)
                xh, xl = (x[:, :, :].rearrange("p m n -> p (m n)") for x in (xT_h, xT_l))
                for f in range(4):
                    dst = bank[1][0:CH, 130 * f:130 * f + 130] if f < 3 else bank[0][0:CH, 256:386]
                    last = two(dst, wqkv_h[:, CH * f:CH * f + CH], wqkv_l[:, CH * f:CH * f + CH], xh, xl)
                last.then_inc(qk_done, 1)
                if not isinstance(i, int) or i:
                    pe.wait_ge(vx_ok, 2 * i)
                for m in range(2):
                    last = two(bank[2][0:N, D * m:D * m + D], xT_h[:, m, :], xT_l[:, m, :],
                               wqkv_h[:, 2 * D:3 * D], wqkv_l[:, 2 * D:3 * D])
                last.then_inc(v_done, 1)

            def attention(i, more):
                if more:
                    transpose_x(i + 1)
                pe.wait_ge(q_ok, 2 * i + 2)
                pe.wait_ge(kbd_ok, 2 * i + 2)
                for m in range(2):
                    if not isinstance(i, int) or i:
                        pe.wait_ge(g_ok, 2 * i)
                        pe.wait_ge(w_ok, 2 * i)
                    for f in range(2):
                        last = pe.matmul(sx[m][0:N, f, 0:HH * N], qT[:, f, m, :],
                                         kbd[:, f, m, :, :].rearrange("p h n -> p (h n)"), start=True, stop=True)
                    last.then_inc(score_done, 1)
                if more:
                    project(i + 1)
                for m in range(2):
                    pe.wait_ge(exp_ok, 2 * i + m + 1)
                    for h in range(H):
                        last = pe.transpose(sx[m][0:N, h // HH, N * (h % HH):N * (h % HH) + N], xexp[m][:, h, :],
                                            ident[0:N, 0:N])
                    last.then_inc(xt_done, 1)
                for m in range(2):
                    pe.wait_ge(xtv_ok, 2 * i + m + 1)
                    pe.wait_ge(vx_ok, 2 * i + m + 1)
                    for h in range(H):
                        last = pe.matmul(sx[m][0:N, h // HH, XW * (h % HH):XW * (h % HH) + XW],
                                         xtv[m][:, h, 0:N], xtv[m][:, h, :], start=True, stop=True)
                    last.then_inc(gram_done, 1)

            transpose_x(0)
            project(0)
            pe.wait_ge(zero_ok, 5)
            attention(0, True)
            with pe.Fori(1, PAIRS - 2) as i:
                attention(i, True)
            attention(PAIRS - 2, True)
            attention(PAIRS - 1, False)

            pe.wait_ge(gmax_ok, 2)
            pe.wait_ge(ones_ok, 1)
            for a in range(2):
                last = pe.transpose(bank[2][0:1, a * N:a * N + N], mx2[:, a:a + 1], ident[0:N, 0:N])
            last.then_inc(gmaxT_done, 1)
            pe.wait_ge(gscale_ok, 1)
            pe.matmul(bank[2][0:N, 256:257], ones[:, :], grow2[0:1, 1:2], start=True, stop=True).then_inc(gbc_done, 1)

            def square(g, c):
                pe.wait_ge(t_ok[c], g + 1)
                for h in range(HH):
                    last = pe.matmul(P[c][:, N * h:N * h + N], T[c][:, h, :], T[c][:, h, :], start=True, stop=True)
                last.then_inc(p1_done[c], 1)

            def product(g, c):
                pe.wait_ge(qs_ok[c], g + 1)
                pe.wait_ge(sm_ok[c], g + 1)
                for h in range(HH):
                    last = pe.matmul(P[c][:, N * h:N * h + N], Qs[c][:, h, :], Sm[c][:, h, :], start=True, stop=True)
                last.then_inc(p2_done[c], 1)

            def apply(j):
                for c in range(4):
                    pe.wait_ge(fin_ok[c], j + 1)
                    for h in range(HH):
                        n = HH * c + h
                        last = pe.matmul(bank[0][0:N, VA * n:VA * n + VA], Fin[c][:, h, :],
                                         wall[:, bass.ds(2 * H * j + n, 1), :].rearrange("p a v -> p (a v)"),
                                         start=True, stop=True)
                last.then_inc(wv_done, 1)

            def transpose_context(j):
                pe.wait_ge(ctx_ok, j + 1)
                for m in range(2):
                    pe.transpose(bank[1][:, N * m:N * m + N], ctxv[:, m, 0:DH_], ident[0:N, 0:N])
                    last = pe.transpose(bank[1][0:DL_, 130 + N * m:130 + N * m + N], ctxv[:, m, DH_:D],
                                        ident[0:N, 0:N])
                last.then_inc(ctxT_done, 1)

            def project_context(j):
                pe.wait_ge(cT_ok, 4 * j + 4)
                two(bank[2][:, 0:D], cT_h[:, :, :].rearrange("p m n -> p (m n)"),
                    cT_l[:, :, :].rearrange("p m n -> p (m n)"), wp_h[:, :], wp_l[:, :]).then_inc(proj_done, 1)

            def pair(j, tail):
                g0 = ITERS * j
                for c in range(4):
                    if tail:
                        pe.wait_ge(fin_ok[c], j)
                    square(g0, c)
                if tail:
                    apply(j - 1)
                for c in range(4):
                    product(g0, c)
                with pe.Fori(1, ITERS - 1) as it:
                    for c in range(4):
                        square(g0 + it, c)
                    for c in range(4):
                        product(g0 + it, c)
                for c in range(4):
                    square(g0 + ITERS - 1, c)
                if tail:
                    transpose_context(j - 1)
                for c in range(4):
                    product(g0 + ITERS - 1, c)
                if tail:
                    project_context(j - 1)

            pair(0, False)
            with pe.Fori(1, PAIRS) as j:
                pair(j, True)
            apply(PAIRS - 1)
            transpose_context(PAIRS - 1)
            project_context(PAIRS - 1)
            pe.wait_ge(h2_ok, PAIRS)
            two(bank[2][0:B, 0:D], cTc_h[:, :], cTc_l[:, :], wp_h[:, :], wp_l[:, :]).then_inc(proj_done, 1)

            for t in range(TILES):
                rows = 128 if t < PAIRS else B
                pe.wait_ge(x2_ok, t + 1)
                if t >= 2:
                    pe.wait_ge(x2T_ok, 2 * (t - 1))
                pe.transpose(bank[t % 2][:, 0:rows], x2[0:rows, t, 0:DH_], ident[0:rows, 0:rows])
                pe.transpose(bank[t % 2][0:DL_, 128:128 + rows], x2[0:rows, t, DH_:D],
                             ident[0:rows, 0:rows]).then_inc(x2T_done, 1)
            for t in range(TILES):
                cols = slice(128 * t, 128 * t + (128 if t < PAIRS else B))
                pe.wait_ge(x2T_ok, 2 * t + 2)
                last = two(bank[3][0:cols.stop - cols.start, E * t:E * t + E], x2T_h[:, cols], x2T_l[:, cols],
                           wg_h[:, :], wg_l[:, :])
            last.then_inc(logit_done, 1)

            pe.wait_ge(count_ok, 1)
            pe.matmul(bank[2][:, 0:E], ones_b[:, :], count_b[:, :], start=True, stop=True).then_inc(total_done, 1)
            pe.wait_ge(chosen_ok, 2 * TOPK + 1)
            rank = bank[1][:, 0:G * E].rearrange("p (g e) -> p g e", e=E)
            pe.matmul(rank, before_b[:, :], chosen_b[:, :, :], start=True, stop=False)
            for g in range(G - 1):
                last = pe.matmul(rank[:, g + 1:G, :], ones_b[:, :],
                                 chosen_b[:, g:g + 1, :].broadcast_to([128, G - 1 - g, E]),
                                 start=False, stop=(g == G - 2))
            last.then_inc(rank_done, 1)

            def by_slot(dst, values):
                for g in range(G):
                    rows = 128 if g % TILES < PAIRS else B
                    last = pe.matmul(dst, in_p[0:rows, g, :], values[0:rows, g], start=(g == 0), stop=(g == G - 1))
                return last

            pe.wait_ge(in_p_ok, 3)
            pe.wait_ge(val_ok, TOPK + 1)
            by_slot(bank[2][:, 64:64 + 2 * ST], val[:, :, :, :].rearrange("p g a j -> p g (a j)")).then_inc(inv_done, 1)
            pe.wait_ge(valg_ok, 1)
            by_slot(bank[2][:, 128:128 + ST], val_g).then_inc(invg_done, 1)

            def expert_of(j):
                return pe.value_load(texp_i[0:1, bass.ds(j, 1)], min_val=0, max_val=E - 1)

            def transpose_tokens(j, p, nth):
                pe.wait_ge(get_in[p], 16 * (nth + 1))
                if not isinstance(j, int) or j:
                    pe.wait_ge(xe_ok, 2 * j)
                pe.transpose(XP[:, 0:SLOTS], xin[p][:, 0:DH_], ident[:, :])
                pe.transpose(XP[0:DL_, SLOTS:2 * SLOTS], xin[p][:, DH_:D], ident[:, :]).then_inc(xe_done, 1)

            def first_layer(j, e):
                pe.wait_ge(xe_ok, 2 * j + 2)
                for f in range(2):
                    units = slice(HH2 * f, HH2 * f + HH2)
                    last = two(HP[:, f, 0:HH2], xe_h, xe_l, w1h[:, bass.ds(e, 1), units].rearrange("p a n -> p (a n)"),
                               w1l[:, bass.ds(e, 1), units].rearrange("p a n -> p (a n)"))
                last.then_inc(l1_done, 1)

            def transpose_hidden(j):
                pe.wait_ge(h_ok, 2 * j + 2)
                for mt in range(MT):
                    last = pe.transpose(HTP[:, mt // 3, SLOTS * (mt % 3):SLOTS * (mt % 3) + SLOTS],
                                        hs[:, SLOTS * mt:SLOTS * mt + SLOTS], ident[:, :])
                last.then_inc(hT_done, 1)

            def second_layer(j, p, e):
                pe.wait_ge(hT_ok, 2 * j + 2)
                if not isinstance(j, int) or j >= 2:
                    pe.wait_ge(y_ok, j - 1)
                for mt in range(MT):
                    last = pe.matmul(YP[p][:, 0:D], hT[:, mt, :],
                                     w2a[:, bass.ds(e, 1), D * mt:D * mt + D].rearrange("p a n -> p (a n)"),
                                     start=(mt == 0), stop=(mt == MT - 1))
                last.then_inc(l2_done, 1)

            pe.wait_ge(texpi_ok, 1)
            pe.wait_ge(xones_ok, 1)
            pe.wait_ge(w1_in, 48)
            pe.wait_ge(w2_in, 16)
            transpose_tokens(0, 0, 0)
            first_layer(0, expert_of(0))
            transpose_tokens(1, 1, 0)

            pe.wait_ge(gate_ok, 1)
            for t in range(TILES):
                rows = 128 if t < PAIRS else B
                if t >= 1:
                    pe.wait_ge(gateT_ok, t)
                pe.transpose(bank[3][0:E, 128 * (t % 2):128 * (t % 2) + rows], gate[0:rows, t, :],
                             ident[0:rows, 0:rows]).then_inc(gateT_done, 1)
            pe.wait_ge(gslot_ok, 1)
            for t in range(TILES):
                rows = 128 if t < PAIRS else B
                pe.wait_ge(gateT_ok, t + 1)
                if t >= 2:
                    pe.wait_ge(acc_ok, t - 1)
                pe.matmul(bank[1 + t % 2][0:rows, 0:D], gateT[:, 128 * t:128 * t + rows], b2t[:, :],
                          start=True, stop=True).then_inc(b2_done, 1)
            pe.wait_ge(acc_ok, TILES)

            def tiles(jj):
                e = expert_of(2 * jj)
                for p in range(2):
                    j = 2 * jj + p
                    transpose_hidden(j)
                    following = None
                    if not isinstance(j, int) or j + 1 < ST:
                        following = expert_of(j + 1)
                        first_layer(j + 1, following)
                    if not isinstance(j, int) or j + 2 < ST:
                        transpose_tokens(j + 2, p, jj + 1)
                    second_layer(j, p, e)
                    e = following

            tiles(0)
            with pe.Fori(1, ST // 2 - 1) as jj:
                tiles(jj)
            tiles(ST // 2 - 1)


def kernel(x, cls_tok, L0_tok_W, L0_tok_b, L0_attn_qkv_w, L0_attn_qkv_b, L0_attn_proj_w, L0_attn_proj_b,
           L0_ffn_Wg, L0_ffn_bg, L0_ffn_W1, L0_ffn_b1, L0_ffn_W2, L0_ffn_b2):
    import numpy as np
    import concourse.bacc as bacc
    from concourse.bass_utils import run_bass_kernel_spmd

    def lay(a):
        return np.ascontiguousarray(a)

    side = IMG // PATCH
    p = np.asarray(x).reshape(PAIRS, 2, C_IN, side, PATCH, side, PATCH)
    p = p.transpose(0, 4, 6, 2, 1, 3, 5).reshape(PAIRS, KT, 128, 128).transpose(0, 2, 1, 3)
    arrays = {
        "xp": lay(p),
        "cls_tok": lay(cls_tok),
        "tok_w": lay(np.asarray(L0_tok_W).T.reshape(KT, 128, D).transpose(1, 0, 2)),
        "tok_b": lay(L0_tok_b),
        "qkv_w": lay(L0_attn_qkv_w),
        "qk_b": lay(np.asarray(L0_attn_qkv_b)[0:2 * D].reshape(4, CH).T),
        "v_b": lay(np.asarray(L0_attn_qkv_b)[2 * D:3 * D]),
        "proj_w": lay(L0_attn_proj_w),
        "proj_b": lay(L0_attn_proj_b),
        "wg": lay(L0_ffn_Wg),
        "bg": lay(L0_ffn_bg),
        "w1": lay(L0_ffn_W1),
        "b1": lay(L0_ffn_b1),
        "w2": lay(np.asarray(L0_ffn_W2).reshape(E, MT, 128, D).transpose(2, 0, 1, 3).reshape(128, E, MT * D)),
        "b2": lay(L0_ffn_b2),
    }
    nc = bacc.Bacc("TRN2", target_bir_lowering=False, num_devices=1)
    args = [nc.dram_tensor(n, a.shape, mybir.dt.from_np(a.dtype), kind="ExternalInput").ap()
            for n, a in arrays.items()]
    args.append(nc.dram_tensor("out", (B, N, D), F32, kind="ExternalOutput").ap())
    build(nc, *args)
    return run_bass_kernel_spmd(nc, [arrays], core_ids=[0]).results[0]["out"]
```

```python
import concourse.bass as bass
from concourse import mybir
from contextlib import ExitStack

F32 = mybir.dt.float32
U32 = mybir.dt.uint32
I32 = mybir.dt.int32
BF16 = mybir.dt.bfloat16
ALU = mybir.AluOpType
ACT = mybir.ActivationFunctionType
AX = mybir.AxisListType

B = 16
C_IN, IMG, PATCH = 3, 128, 16
NPATCH = (IMG // PATCH) ** 2
N = NPATCH + 1
D = 192
DH_, DL_ = 128, D - 128
KT = PATCH * PATCH * C_IN // 128
H, DH = 12, 16
HH = H // 2
CH = HH * DH
VA = DH + 1
XW = N + VA
PAIRS = B // 2
ITERS = 6
E, HID = 8, 768
MT = HID // 128
TILES = PAIRS + 1
NTOK = B * N
ROWS = 128
TOPK = 2
SLOTS = 128
ST = (TOPK * NTOK + E * (SLOTS - 1)) // SLOTS
G = TOPK * TILES
HH2 = HID // 2
FIRST = 2
XINS = 4
VALS = 6
TOK = 3
EPS = 1e-5

BETA = 92.0 / 13.0
KAPPA = (1.0 / (256.0 * BETA)) ** (1.0 / 3.0)
CV = 13.0 / (112.0 * KAPPA)


class Area:

    def __init__(self, tensor):
        self.tensor, self.used = tensor, 0

    def take(self, n):
        self.used += n
        return self.tensor[:, self.used - n:self.used]

    def again(self):
        self.used = 0


def build(nc, xp, cls_tok, tok_w, tok_b, qkv_w, qk_b, v_b, proj_w, proj_b, wg, bg, w1, b1, w2, b2, out):
    ctx = ExitStack()
    with ctx:
        def sb(name, shape, dt=F32):
            return ctx.enter_context(nc.sbuf_tensor(name, shape, dt))

        def sem(name):
            return ctx.enter_context(nc.semaphore(name))

        tokw = sb("tokw", [128, KT, D])
        tokb = sb("tokb", [128, D])
        wqkv_h = sb("wqkv_h", [DH_, 3 * D])
        wqkv_l = sb("wqkv_l", [DL_, 3 * D])
        qkb = sb("qkb", [CH, 4])
        qbs = sb("qbs", [CH, 2])
        vb = sb("vb", [128, D])
        wp_h = sb("wp_h", [DH_, D])
        wp_l = sb("wp_l", [DL_, D])
        pb = sb("pb", [128, D])
        wg_h = sb("wg_h", [DH_, E])
        wg_l = sb("wg_l", [DL_, E])
        bgb = sb("bgb", [128, E])
        ident = sb("ident", [128, 128])
        kappa4 = sb("kappa4", [1, N])
        mask = sb("mask", [CH, HH])
        hid = sb("hid", [128, TILES, D])
        mv = sb("mv", [128, TILES, 2])
        rstd = sb("rstd", [128, TILES])
        stat = sb("stat", [128, TILES, 6])
        front = Area(sb("front", [128, 2 * (2 * H * N + H * XW) + 4 * HH * N + 16 * N]))
        xn = sb("xn", [128, D])
        xncls = sb("xncls", [B, D])
        xT_h = sb("xT_h", [DH_, 2, N])
        xT_l = sb("xT_l", [DL_, 2, N])
        qT = [front.take(4 * N).rearrange("p (f m n) -> p f m n", f=2, m=2) for s in range(2)]
        kT = [front.take(4 * N)[0:CH].rearrange("p (f m n) -> p f m n", f=2, m=2) for s in range(2)]
        spare = sb("spare", [128, 4 * HH * N])
        kbd = [t.rearrange("p (f m h n) -> p f m h n", f=2, m=2, h=HH) for t in (front.take(4 * HH * N), spare[:, :])]
        rmax = sb("rmax", [N, 2, H])
        sdiff = [front.take(H * N)[0:N].rearrange("p (h n) -> p h n", h=H) for m in range(2)]
        xexp = [front.take(H * N)[0:N].rearrange("p (h n) -> p h n", h=H) for m in range(2)]
        xtv = [front.take(H * XW).rearrange("p (h n) -> p h n", h=H) for m in range(2)]
        big = sb("big", [128, B * H * N])
        gall = big[0:N, :].rearrange("p (g n) -> p g n", n=N)
        wall = sb("wall", [ROWS, B * H, VA])
        csum = sb("csum", [N, B * H])
        mx2 = sb("mx2", [N, 2])
        grow = sb("grow", [1, 4])
        cscale = sb("cscale", [N, 1])
        area = Area(sb("area", [ROWS, 16 * HH * N]))
        patch = [area.take(KT * 128).rearrange("p (k n) -> p k n", k=KT) for t in range(PAIRS)]
        area.again()
        T = [area.take(HH * N).rearrange("p (h n) -> p h n", n=N) for c in range(4)]
        Qs = [area.take(HH * N).rearrange("p (h n) -> p h n", n=N) for c in range(4)]
        Sm = [area.take(HH * N).rearrange("p (h n) -> p h n", n=N) for c in range(4)]
        V = [spare[0:N, HH * N * c:HH * N * (c + 1)].rearrange("p (h n) -> p h n", n=N) for c in range(4)]
        Fin = [area.take(HH * N).rearrange("p (h n) -> p h n", n=N) for c in range(4)]
        den = sb("den", [N, 2, H])
        rden = sb("rden", [N, 2, H])
        ctxv = sb("ctxv", [N, 2, D])
        cT_h = sb("cT_h", [DH_, 2, NPATCH])
        cT_l = sb("cT_l", [DL_, 2, NPATCH])
        cTc_h = sb("cTc_h", [DH_, B])
        cTc_l = sb("cTc_l", [DL_, B])
        stat2 = sb("stat2", [128, 2, 6])
        mv2 = sb("mv2", [128, 2, 2])
        std2 = sb("std2", [128, 2])
        rstd2 = sb("rstd2", [128, 2])
        area.again()
        front.again()
        hs = area.take(HID)
        hT = area.take(HID).rearrange("p (m n) -> p m n", m=MT)
        xin = [area.take(D) for p in range(XINS)]
        ysum = area.take(D)
        yout = [area.take(D) for p in range(2)]
        xe_h = area.take(SLOTS)
        xe_l = area.take(SLOTS)[0:DL_ + 1]
        b2t = front.take(E * D).rearrange("p (e d) -> p e d", e=E)
        x2 = [front.take(D) for k in range(2)]
        x2T_h = [front.take(128) for k in range(2)]
        x2T_l = [front.take(128)[0:DL_] for k in range(2)]
        logit = sb("logit", [128, TILES, E])
        top = sb("top", [128, TILES, 8])
        key = front.take(TILES * E).rearrange("p (t e) -> p t e", t=TILES)
        above = sb("above", [128, TILES, E])
        key_top = sb("key_top", [128, TILES, 8])
        rev_e = sb("rev_e", [128, E])
        gk = sb("gk", [128, 4, TILES])
        chosen = sb("chosen", [128, TOPK, TILES, E])
        chosen_b = sb("chosen_b", [128, G, E], BF16)
        count_b = sb("count_b", [128, E], BF16)
        gate_b = sb("gate_b", [128, 3, G], BF16)
        gleft = sb("gleft", [128, 2, G])
        over = front.take(E * TILES).rearrange("p (e t) -> p e t", e=E)
        ntile = sb("ntile", [128, E])
        upto = sb("upto", [128, E, E])
        tend = sb("tend", [128, E])
        tstart = sb("tstart", [128, E])
        place = front.take(G * E).rearrange("p (g e) -> p g e", g=G)
        slot = sb("slot", [128, G])
        slot_j = sb("slot_j", [128, G])
        slot_p = sb("slot_p", [128, G])
        in_p = front.take(G * SLOTS // 2).bitcast(BF16).rearrange("p (g n) -> p g n", g=G)
        in_j = sb("in_j", [128, G, ST], BF16)
        val = front.take(G * VALS * ST // 2).bitcast(BF16).rearrange("p (g a j) -> p g a j", g=G, a=VALS)
        found = sb("found", [128, VALS, ST])
        row_add = sb("row_add", [128, ST])
        idx_get = sb("idx_get", [128, ST], U32)
        idx_add = sb("idx_add", [128, ST], U32)
        gsum = sb("gsum", [128, ST])
        gslot = sb("gslot", [128, ST])
        tcmp = front.take(ST * E)[0:1].rearrange("p (j e) -> p j e", j=ST)
        texp = sb("texp", [1, ST])
        texp_c = sb("texp_c", [1, ST])
        texp_i = sb("texp_i", [1, ST], I32)
        CUTS = (E, TILES, ST, SLOTS, TILES, 1, 1)
        NI = sum(CUTS)
        iota_i = sb("iota_i", [128, NI], I32)
        iota_f = sb("iota_f", [128, NI])
        cuts = [sum(CUTS[0:n]) for n in range(len(CUTS) + 1)]
        (i_exp, i_thr, i_tile, i_col, i_img, i_tok, i_pad), (
            eidx, thr, tidx, pidx, timg, ttok, pad_row) = (
            [t[:, cuts[n]:cuts[n + 1]] for n in range(len(CUTS))] for t in (iota_i, iota_f))
        token_of = sb("token_of", [128, 2, TOPK, TILES], BF16)
        pidx_b = sb("pidx_b", [128, SLOTS], BF16)
        npad_row = sb("npad_row", [128, 1])
        tri_e = sb("tri_e", [128, E, E])
        before = sb("before", [128, 128])
        before_b = sb("before_b", [128, 128], BF16)
        ones_b = sb("ones_b", [128, 128], BF16)
        w1h = big[:, 0:E * HID].rearrange("p (e n) -> p e n", e=E)
        w1l = big[0:DL_ + 1, E * HID:2 * E * HID].rearrange("p (e n) -> p e n", e=E)
        w2a = sb("w2a", [128, E, MT * D])
        x2_rows = nc.dram_tensor("x2_rows", (NTOK, D), F32).ap()

        sx = [ctx.enter_context(nc.psum_tensor(f"sx{m}", [128, 2, 512], F32)) for m in range(2)]
        bank = [ctx.enter_context(nc.psum_tensor(f"bank{b}", [128, 512], F32)) for b in range(4)]
        half_heads = [sx[m][0:N, :, 0:HH * N].rearrange("p b (h n) -> p b h n", n=N) for m in range(2)]
        gram = [sx[m][0:N, :, 0:HH * XW].rearrange("p b (h n) -> p b h n", n=XW) for m in range(2)]
        HP, HTP = sx
        XP, YP = bank[0], bank[1:3]
        P = [sx[c // 2][0:N, c % 2, 0:HH * N] for c in range(4)]

        EMB = [sx[1][:, b, 0:D] for b in range(2)]
        RB = bank[3], bank[1]
        JB = bank[2], bank[0]

        def sems(prefix, n):
            return [sem(f"{prefix}{k}") for k in range(n)]

        w_in, consts_in = sem("w_in"), sem("consts_in")
        patch_in, cls_in = sems("patch_in", PAIRS), sem("cls_in")
        ident_zero, ident_ok, mask_one, mask_half, mask_ok, eidx_ok, tri_ok, before_ok = (
            sem(n) for n in ("ident_zero", "ident_ok", "mask_one", "mask_half", "mask_ok", "eidx_ok", "tri_ok",
                             "before_ok"))
        xtv_zero, zero_ok, rows_zero, tiles_zero = (
            sem(n) for n in ("xtv_zero", "zero_ok", "rows_zero", "tiles_zero"))
        kappa4_ok, mv_init, qbs_ok = (
            sem(n) for n in ("kappa4_ok", "mv_init", "qbs_ok"))
        emb_done, emb_free, stat_ok, mv_ok = (
            sem(n) for n in ("emb_done", "emb_free", "stat_ok", "mv_ok"))
        eps_ok, sqrt_ok, rstd_ok = (sem(n) for n in ("eps_ok", "sqrt_ok", "rstd_ok"))
        xncls_ok, clsT_done, clsT_ok, xn_ok, xnT_done, xT_ok = (
            sem(n) for n in ("xncls_ok", "clsT_done", "clsT_ok", "xn_ok", "xnT_done", "xT_ok"))
        qk_done, v_done, q_ok, k_ok, kbd_ok, vx_ok = (
            sem(n) for n in ("qk_done", "v_done", "q_ok", "k_ok", "kbd_ok", "vx_ok"))
        score_done, rmax_ok, diff_ok, clamp_ok, exp_ok = (
            sem(n) for n in ("score_done", "rmax_ok", "diff_ok", "clamp_ok", "exp_ok"))
        xt_done, xtv_ok, csum_ok, gram_done, g_ok, w_ok = (
            sem(n) for n in ("xt_done", "xtv_ok", "csum_ok", "gram_done", "g_ok", "w_ok"))
        gmax_ok, gmaxT_done, gscale_ok, gbc_done, cscale_ok = (
            sem(n) for n in ("gmax_ok", "gmaxT_done", "gscale_ok",
                             "gbc_done", "cscale_ok"))
        t_ok, p1_done, qs_ok, sm_ok, v_ok, p2_done, fin_ok = (
            sems(n, 4) for n in ("t_ok", "p1_done", "qs_ok", "sm_ok", "v_ok", "p2_done", "fin_ok"))
        hb_ok, wv_done, den_ok, rden_ok, ctx_ok, ctxT_done, cT_ok, proj_done, h2_ok, stat2_ok, mv2_ok = (
            sem(n) for n in ("hb_ok", "wv_done", "den_ok", "rden_ok", "ctx_ok", "ctxT_done", "cT_ok", "proj_done",
                             "h2_ok", "stat2_ok", "mv2_ok"))
        eps2_ok, sqrt2_ok, rstd2_ok, x2_ok, x2T_done, x2T_ok = (
            sem(n) for n in ("eps2_ok", "sqrt2_ok", "rstd2_ok", "x2_ok", "x2T_done", "x2T_ok"))
        logit_done, logit_ok, top_ok, key_part, key_ok, key_top_ok, gdiff_ok, gexp_ok = (
            sem(n) for n in ("logit_done", "logit_ok", "top_ok", "key_part", "key_ok", "key_top_ok", "gdiff_ok",
                             "gexp_ok"))
        token_ok, b2_in, ysum_ok, gsplit_ok, found_ok = (
            sem(n) for n in ("token_ok", "b2_in", "ysum_ok", "gsplit_ok", "found_ok"))
        tval_ok, rev_ok = sem("tval_ok"), sem("rev_ok")
        chosen_ok, count_ok, total_done, rank_done = (
            sem(n) for n in ("chosen_ok", "count_ok", "total_done",
                             "rank_done"))
        slot_j_ok, in_j_ok, slot_p_ok, in_p_ok, ival_ok, oval_ok = (
            sem(n) for n in ("slot_j_ok", "in_j_ok", "slot_p_ok", "in_p_ok", "ival_ok", "oval_ok"))
        inv_done, pad_ok, idx_ok, gslot_ok, texp_ok, texpi_ok, xones_ok = (
            sem(n) for n in ("inv_done", "pad_ok", "idx_ok", "gslot_ok", "texp_ok", "texpi_ok", "xones_ok"))
        w2_in, w1_in, rows_out, add_out = (
            sem(n) for n in ("w2_in", "w1_in", "rows_out", "add_out"))
        get_in = sems("get_in", XINS)
        scale_step, place_step, gate_step = (sem(n) for n in ("scale_step", "place_step", "gate_step"))
        xe_done, xe_ok, l1_done, h_ok, hT_done, hT_ok, l2_done, y_ok = (
            sem(n) for n in ("xe_done", "xe_ok", "l1_done", "h_ok", "hT_done", "hT_ok", "l2_done", "y_ok"))

        CHOICES = 3
        block = ctx.enter_context(nc.Block())
        CONSTS = 10 * 16

        def settled(eng):
            eng.wait_ge(w_in, 32)

        def rows_before(t):
            return 16 + 64 * t

        def by_row(dram, t):
            if t == PAIRS:
                return [(dram[0:NTOK, :].rearrange("(i n) d -> i n d", n=N)[:, 0, :], slice(0, B))]
            return [(dram[(2 * t + m) * N + 1:(2 * t + m + 1) * N, :], slice(m * NPATCH, (m + 1) * NPATCH))
                    for m in range(2)]

        @block.sync
        def _(sp):
            sp.dma_start(tokw[:, :, :], tok_w).then_inc(w_in, 16)
            for t in range(PAIRS):
                sp.dma_start(patch[t][:, :, :], xp[t]).then_inc(patch_in[t], 16)
                if t == 0:
                    sp.dma_start(tokb[:, :], tok_b.partition_broadcast(128)).then_inc(w_in, 16)
                    sp.dma_start(hid[0:B, PAIRS, :], cls_tok[0, 0:1, :].partition_broadcast(B)).then_inc(cls_in, 16)
            sp.wait_ge(emb_done, PAIRS)
            sp.dma_start(w2a[:, :, :], w2).then_inc(w2_in, 16)
            sp.wait_ge(w_in, 32)
            sp.dma_start(out[NTOK:NTOK + SLOTS, :], tokb[:, :]).then_inc(rows_out, 16)
            for c in range(4):
                sp.wait_ge(t_ok[c], 1)
            sp.dma_start(b2t, b2.rearrange("e d -> (e d)").partition_broadcast(128).rearrange(
                "p (e d) -> p e d", e=E)).then_inc(b2_in, 16)

            def token_rows(t):
                sp.wait_ge(x2_ok, t + 1)
                for rows, part in by_row(x2_rows, t):
                    sp.dma_start(rows, x2[t // PAIRS][part, :]).then_inc(rows_out, 16)
                for rows, part in by_row(out, t):
                    sp.dma_start(rows, hid[part, t, :]).then_inc(rows_out, 16)

            for t in range(PAIRS - 1):
                token_rows(t)
                if t == PAIRS - 3:
                    for c in range(4):
                        sp.wait_ge(t_ok[c], ITERS * (PAIRS - 1) + 1)
                    sp.dma_start(w1h, w1[:, 0:DH_, :].rearrange("e p n -> p e n")).then_inc(w1_in, 16)
                    sp.dma_start(w1l[0:DL_], w1[:, DH_:D, :].rearrange("e p n -> p e n")).then_inc(w1_in, 16)
                    sp.dma_start(w1l[DL_:DL_ + 1], b1.rearrange("e n -> (e n)").unsqueeze(0).rearrange(
                        "a (e n) -> a e n", e=E)).then_inc(w1_in, 16)
            for t in (PAIRS - 1, PAIRS):
                token_rows(t)
            sp.wait_ge(add_out, 16 * ST)

        @block.gpsimd
        def _(pool):
            pool.memset(ident[:, :], 0.0).then_inc(ident_zero, 1)
            pool.wait_ge(ident_zero, 1)
            pool.affine_select(out=ident[:, :], in_=ident[:, :], compare_op=ALU.not_equal, fill=1.0, base=0,
                               pattern=[[-1, 128]], channel_multiplier=1).then_inc(ident_ok, 1)
            pool.wait_ge(ident_ok, 1)
            pool.memset(mask[:, :], 1.0).then_inc(mask_one, 1)
            pool.memset(tri_e[:, :, :], 1.0).then_inc(tri_ok, 1)
            pool.memset(before[:, :], 1.0).then_inc(before_ok, 1)
            for t, step, n in ((i_exp, 1, E), (i_thr, SLOTS, TILES), (i_tile, 1, ST), (i_col, 1, SLOTS)):
                pool.iota(t, pattern=[[step, n]], base=0, channel_multiplier=0).then_inc(eidx_ok, 1)
            for m in range(2):
                pool.wait_ge(eidx_ok, 4 + m)
                pool.iota(i_img[m * NPATCH:(m + 1) * NPATCH, 0:PAIRS], pattern=[[2, PAIRS]], base=m,
                          channel_multiplier=0).then_inc(eidx_ok, 1)
            pool.wait_ge(eidx_ok, 6)
            pool.iota(i_img[:, PAIRS:TILES], pattern=[[0, 1]], base=0, channel_multiplier=1).then_inc(eidx_ok, 1)
            for m in range(2):
                pool.wait_ge(eidx_ok, 7 + m)
                pool.iota(i_tok[m * NPATCH:(m + 1) * NPATCH], pattern=[[0, 1]], base=1,
                          channel_multiplier=1).then_inc(eidx_ok, 1)
            pool.wait_ge(eidx_ok, 9)
            pool.iota(i_pad, pattern=[[0, 1]], base=NTOK, channel_multiplier=1).then_inc(eidx_ok, 1)
            pool.wait_ge(mask_one, 1)
            pool.affine_select(out=mask[:, :], in_=mask[:, :], compare_op=ALU.is_ge, fill=0.0, base=0,
                               pattern=[[-DH, HH]], channel_multiplier=1).then_inc(mask_half, 1)
            pool.wait_ge(mask_half, 1)
            pool.affine_select(out=mask[:, :], in_=mask[:, :], compare_op=ALU.is_ge, fill=0.0, base=DH - 1,
                               pattern=[[DH, HH]], channel_multiplier=-1).then_inc(mask_ok, 1)
            pool.wait_ge(tri_ok, 1)
            pool.affine_select(out=tri_e[:, :, :], in_=tri_e[:, :, :], compare_op=ALU.is_ge, fill=0.0, base=0,
                               pattern=[[1, E], [-1, E]], channel_multiplier=0).then_inc(tri_ok, 1)
            pool.wait_ge(before_ok, 1)
            pool.affine_select(out=before[:, :], in_=before[:, :], compare_op=ALU.is_ge, fill=0.0, base=-1,
                               pattern=[[1, 128]], channel_multiplier=-1).then_inc(before_ok, 1)
            pool.wait_ge(eidx_ok, 10)
            pool.tensor_copy(iota_f[:, :], iota_i[:, :]).then_inc(eidx_ok, 1)
            pool.wait_ge(eidx_ok, 11)
            for s in range(2):
                pool.memset(qT[s][CH:ROWS], 0.0).then_inc(rows_zero, 1)
                pool.memset(kbd[s][CH:ROWS], 0.0).then_inc(rows_zero, 1)
            pool.wait_ge(rows_zero, 4)
            pool.memset(wall[:, :, :], 0.0).then_inc(rows_zero, 1)

            def spread_k(i, s):
                pool.wait_ge(k_ok, 2 * i + 2)
                for f in range(2):
                    pool.tensor_tensor(
                        kbd[s][0:CH, f], kT[s][:, f].unsqueeze(2).broadcast_to([CH, 2, HH, N]),
                        mask[:, :].unsqueeze(1).unsqueeze(3).broadcast_to([CH, 2, HH, N]), ALU.mult,
                    ).then_inc(kbd_ok, 1)

            pool.wait_ge(mask_ok, 1)
            spread_k(0, 0)
            pool.wait_ge(emb_done, PAIRS)
            for tile in T + Qs + Sm + Fin:
                pool.memset(tile[:, :, :], 0.0).then_inc(tiles_zero, 1)
            spread_k(1, 1)
            with pool.Fori(1, PAIRS // 2) as ii:
                for s in range(2):
                    spread_k(2 * ii + s, s)

            pool.wait_ge(xn_ok, PAIRS)
            pool.wait_ge(xncls_ok, 1)
            pool.tensor_tensor(hid[:, 0:PAIRS, :], hid[:, 0:PAIRS, :],
                               pb[:, :].unsqueeze(1).broadcast_to([128, PAIRS, D]), ALU.add).then_inc(hb_ok, 1)
            pool.tensor_tensor(hid[0:B, PAIRS, :], hid[0:B, PAIRS, :], pb[0:B, :], ALU.add).then_inc(hb_ok, 1)

            def combine(g):
                for c in range(4):
                    pool.wait_ge(qs_ok[c], g + 1)
                    pool.wait_ge(sm_ok[c], g + 1)
                    pool.tensor_tensor(V[c][:, :, :], Qs[c][0:N, :, :], Sm[c][0:N, :, :], ALU.add).then_inc(v_ok[c], 1)

            with pool.Fori(0, PAIRS * ITERS) as g:
                combine(g)

            pool.wait_ge(token_ok, 4)
            pool.wait_ge(in_j_ok, 1)
            pool.tensor_tensor(val[:, :, 1, :], in_j[:, :, :],
                               token_of[:, 1].rearrange("p r t -> p (r t)").unsqueeze(2).broadcast_to([128, G, ST]),
                               ALU.mult).then_inc(tval_ok, 1)
            pool.wait_ge(gsplit_ok, 5)
            for a in range(3):
                pool.tensor_tensor(val[:, :, TOK + a, :], in_j[:, :, :],
                                   gate_b[:, a, :].unsqueeze(2).broadcast_to([128, G, ST]), ALU.mult,
                                   ).then_inc(tval_ok, 1)

            def gather(j):
                if j >= XINS:
                    pool.wait_ge(xe_done, j - XINS + 1)
                pool.indirect_dma_start(out=xin[j % XINS], out_offset=None, in_=x2_rows,
                                        in_offset=bass.IndirectOffsetOnAxis(ap=idx_get[:, j:j + 1], axis=0),
                                        ).then_inc(get_in[j % XINS], 16)

            pool.wait_ge(idx_ok, 1)
            pool.wait_ge(rows_out, rows_before(PAIRS) + 32)
            for j in range(XINS):
                gather(j)
            pool.wait_ge(idx_ok, 2)
            for j in range(ST):
                pool.wait_ge(y_ok, j + 1)
                if j:
                    pool.wait_ge(add_out, 16 * j)
                pool.indirect_dma_start(out=out, out_offset=bass.IndirectOffsetOnAxis(ap=idx_add[:, j:j + 1], axis=0),
                                        in_=yout[j % 2], in_offset=None, compute_op=ALU.add).then_inc(add_out, 16)
                if j + XINS < ST:
                    gather(j + XINS)

        @block.scalar
        def _(act):
            for dst, src in ((wqkv_h[:, :], qkv_w[0:DH_, :]), (wqkv_l[:, :], qkv_w[DH_:D, :]),
                             (qkb[:, :], qk_b), (vb[:, :], v_b.partition_broadcast(128)),
                             (wp_h[:, :], proj_w[0:DH_, :]), (wp_l[:, :], proj_w[DH_:D, :]),
                             (pb[:, :], proj_b.partition_broadcast(128)),
                             (wg_h[:, :], wg[0:DH_, :]), (wg_l[:, :], wg[DH_:D, :]),
                             (bgb[:, :], bg.partition_broadcast(128))):
                act.dma_start(dst, src).then_inc(consts_in, 16)

            def deviation1(n, cols):
                act.wait_ge(eps_ok, n + 1)
                act.activation(rstd[:, cols], rstd[:, cols], ACT.Sqrt).then_inc(sqrt_ok, 1)

            deviation1(0, slice(PAIRS, TILES))
            deviation1(1, slice(0, FIRST))
            act.wait_ge(consts_in, CONSTS)
            act.mul(qbs[:, :], qkb[:, 0:2], DH ** -0.5).then_inc(qbs_ok, 1)
            act.wait_ge(clsT_done, 1)
            for k, (dst, rows) in enumerate(((xT_h, DH_), (xT_l, DL_))):
                act.copy(dst[:, :, NPATCH], bank[0][0:rows, k * 16:k * 16 + 2]).then_inc(clsT_ok, 1)

            def transposed_x(i):
                act.wait_ge(xnT_done, i + 1)
                if not isinstance(i, int) or i:
                    act.wait_ge(v_done, 2 * i)
                for k, (dst, rows) in enumerate(((xT_h, DH_), (xT_l, DL_))):
                    act.copy(dst[:, :, 0:NPATCH],
                             bank[0][0:rows, 128 * k:128 * k + 128].rearrange("p (m n) -> p m n", m=2),
                             ).then_inc(xT_ok, 1)

            def qk_out(i, s):
                act.wait_ge(qk_done, i + 1)
                if not isinstance(i, int) or i > 1:
                    act.wait_ge(score_done, 2 * i - 2)
                    act.wait_ge(kbd_ok, 2 * i - 2)
                for f in range(2):
                    act.activation(qT[s][0:CH, f].rearrange("p m n -> p (m n)"), bank[1][0:CH, 130 * f:130 * f + 130],
                                   ACT.Identity, bias=qbs[:, f:f + 1], scale=DH ** -0.5).then_inc(q_ok, 1)
                for f, src in ((0, bank[1][0:CH, 260:390]), (1, bank[0][0:CH, 256:386])):
                    act.activation(kT[s][:, f].rearrange("p m n -> p (m n)"), src,
                                   ACT.Identity, bias=qkb[:, 2 + f:3 + f], scale=1.0).then_inc(k_ok, 1)

            def exponential(i, m):
                act.wait_ge(clamp_ok, 2 * i + m + 1)
                act.activation(xexp[m][:, :, :], sdiff[m][:, :, :], ACT.Exp).then_inc(exp_ok, 1)

            def transpose_out(i, m):
                act.wait_ge(xt_done, 2 * i + m + 1)
                act.copy(xtv[m][0:N, :, 0:N].rearrange("p (f h) n -> p f h n", f=2), half_heads[m]).then_inc(xtv_ok, 1)

            def gram_out(i, m):
                act.wait_ge(gram_done, 2 * i + m + 1)
                settled(act)
                act.copy(gall[:, bass.ds((2 * i + m) * H, H), :].rearrange("p (f h) n -> p f h n", f=2),
                         gram[m][:, :, :, 0:N]).then_inc(g_ok, 1)
                act.copy(wall[0:N, bass.ds((2 * i + m) * H, H), :].rearrange("p (f h) v -> p f h v", f=2),
                         gram[m][:, :, :, N:XW]).then_inc(w_ok, 1)

            def attention(i, s, first, more):
                if more:
                    transposed_x(i + 1)
                if not first:
                    transpose_out(i - 1, 1)
                exponential(i, 0)
                if more:
                    qk_out(i + 1, 1 - s)
                if not first:
                    gram_out(i - 1, 1)
                transpose_out(i, 0)
                gram_out(i, 0)
                exponential(i, 1)

            transposed_x(0)
            qk_out(0, 0)
            deviation1(2, slice(FIRST, PAIRS))
            act.wait_ge(rows_zero, 5)
            act.wait_ge(zero_ok, 2)
            attention(0, 0, True, True)
            with act.Fori(0, PAIRS // 2 - 1) as ii:
                attention(2 * ii + 1, 1, False, True)
                attention(2 * ii + 2, 0, False, True)
            attention(PAIRS - 1, 1, False, False)
            transpose_out(PAIRS - 1, 1)
            gram_out(PAIRS - 1, 1)

            def square_out(g):
                for c in range(4):
                    act.wait_ge(p1_done[c], g + 1)
                    act.mul(Qs[c][0:N, :, :].rearrange("p h n -> p (h n)"), P[c], BETA).then_inc(qs_ok[c], 1)

            def context_out(j):
                act.wait_ge(ctxT_done, j + 1)
                for k, (dst, dstc, rows) in enumerate(((cT_h, cTc_h, DH_), (cT_l, cTc_l, DL_))):
                    settled(act)
                    src = bank[1][0:rows, 130 * k:130 * k + 130].rearrange("p (m n) -> p m n", m=2)
                    act.copy(dst[:, :, :], src[:, :, 0:NPATCH]).then_inc(cT_ok, 1)
                    act.copy(dstc[:, bass.ds(2 * j, 2)], src[:, :, NPATCH]).then_inc(cT_ok, 1)

            act.wait_ge(tiles_zero, 16)
            with act.Fori(0, ITERS) as g:
                square_out(g)

            def deviation(t, k):
                act.wait_ge(eps2_ok, t + 1)
                settled(act)
                act.activation(std2[:, k:k + 1], std2[:, k:k + 1], ACT.Sqrt).then_inc(sqrt2_ok, 1)

            def transposed_x2(t, k, rows):
                act.wait_ge(x2T_done, t + 1)
                for n, (dst, r) in enumerate(((x2T_h[k], DH_), (x2T_l[k], DL_))):
                    act.copy(dst[:, 0:rows], RB[k][0:r, 128 * n:128 * n + rows]).then_inc(x2T_ok, 1)

            with act.Fori(1, PAIRS) as j:
                for it in range(ITERS):
                    square_out(ITERS * j + it)
                    if it == 1:
                        context_out(j - 1)
                    if it == 4:
                        deviation(j - 1, 0)
                    if it == 5:
                        transposed_x2(j - 1, 0, 128)
            context_out(PAIRS - 1)
            deviation(PAIRS - 1, 0)
            deviation(PAIRS, 1)
            transposed_x2(PAIRS - 1, 0, 128)
            transposed_x2(PAIRS, 1, B)
            act.wait_ge(gdiff_ok, 2)
            act.activation(gk[:, 1, :], gk[:, 0, :], ACT.Exp).then_inc(gexp_ok, 1)
            act.wait_ge(in_j_ok, 1)
            act.copy(val[:, :, 2, :], in_j[:, :, :]).then_inc(oval_ok, 1)

            def tokens_out(j):
                act.wait_ge(xe_done, j + 1)
                if not isinstance(j, int) or j:
                    act.wait_ge(l1_done, j)
                act.copy(xe_h, XP[:, 0:SLOTS]).then_inc(xe_ok, 1)
                act.copy(xe_l[0:DL_], XP[0:DL_, SLOTS:2 * SLOTS]).then_inc(xe_ok, 1)

            def hidden_out(j):
                act.wait_ge(l1_done, j + 1)
                if not isinstance(j, int) or j:
                    act.wait_ge(hT_done, j)
                for f in range(2):
                    act.activation(hs[:, HH2 * f:HH2 * f + HH2], HP[:, f, 0:HH2], ACT.Relu).then_inc(h_ok, 1)

            tokens_out(0)
            hidden_out(0)
            tokens_out(1)
            with act.Fori(0, ST - 2) as j:
                hidden_out(j + 1)
                tokens_out(j + 2)
            hidden_out(ST - 1)

        @block.vector
        def _(dve):
            dve.memset(kappa4[:, :], -4.0 * KAPPA).then_inc(kappa4_ok, 1)
            dve.memset(mv[:, :, :], 1.0).then_inc(mv_init, 1)
            dve.memset(std2[:, :], 1.0).then_inc(mv_init, 1)
            dve.memset(chosen[:, :, :, :], 0.0).then_inc(mv_init, 1)
            dve.memset(ones_b[:, :], 1.0).then_inc(mv_init, 1)
            dve.memset(logit[:, :, :], 0.0).then_inc(mv_init, 1)
            for m in range(2):
                dve.memset(xtv[m][:, :, :], 0.0).then_inc(xtv_zero, 1)
            dve.wait_ge(xtv_zero, 2)
            for m in range(2):
                dve.memset(xtv[m][0:N, :, XW - 1:XW], 1.0).then_inc(zero_ok, 1)
            dve.wait_ge(w_in, 32)
            dve.wait_ge(mv_init, 5)

            def statistics1(n, t, rows):
                dve.bn_stats(stat[0:rows, t, :], hid[0:rows, t, :]).then_inc(stat_ok, 1)
                dve.wait_ge(stat_ok, n + 1)
                dve.bn_aggr(mv[0:rows, t, :], stat[0:rows, t, :]).then_inc(mv_ok, 1)

            def embedded(t):
                dve.wait_ge(emb_done, t + 1)
                dve.tensor_tensor(hid[:, t, :], EMB[t % 2], tokb[:, :], ALU.add).then_inc(emb_free, 1)
                dve.wait_ge(emb_free, t + 1)
                statistics1(t + 1, t, 128)

            def add_eps(n, tiles_done, cols):
                dve.wait_ge(mv_ok, tiles_done)
                dve.tensor_scalar(rstd[:, cols], mv[:, cols, 1], EPS, None, ALU.add).then_inc(eps_ok, 1)

            def invert1(n, cols):
                dve.wait_ge(sqrt_ok, n + 1)
                dve.reciprocal(rstd[:, cols], rstd[:, cols]).then_inc(rstd_ok, 1)
                dve.wait_ge(rstd_ok, n + 1)

            dve.wait_ge(cls_in, 16)
            statistics1(0, PAIRS, B)
            add_eps(0, 1, slice(PAIRS, TILES))
            for t in range(FIRST):
                embedded(t)
            add_eps(1, FIRST + 1, slice(0, FIRST))
            invert1(0, slice(PAIRS, TILES))
            dve.tensor_scalar(xncls[:, :], hid[0:B, PAIRS, :], mv[0:B, PAIRS, 0:1], rstd[0:B, PAIRS:TILES],
                              ALU.subtract, ALU.mult).then_inc(xncls_ok, 1)
            invert1(1, slice(0, FIRST))

            def normalise(i):
                if not isinstance(i, int) or i:
                    dve.wait_ge(xnT_done, i)
                dve.tensor_scalar(xn[:, :], hid[:, i, :], mv[:, i, 0:1], rstd[:, i:i + 1] if isinstance(i, int) else
                                  rstd[:, bass.ds(i, 1)], ALU.subtract, ALU.mult).then_inc(xn_ok, 1)

            def maximum(i, m):
                dve.wait_ge(score_done, 2 * i + m + 1)
                dve.tensor_reduce(rmax[:, m, :].rearrange("p (f h) -> p f h", f=2), half_heads[m],
                                  AX.X, ALU.max).then_inc(rmax_ok, 1)
                dve.wait_ge(rmax_ok, 2 * i + m + 1)
                dve.tensor_tensor(
                    sdiff[m][:, :, :].rearrange("p (f h) n -> p f h n", f=2), half_heads[m],
                    rmax[:, m, :].rearrange("p (f h) -> p f h", f=2).unsqueeze(3).broadcast_to([N, 2, HH, N]),
                    ALU.subtract).then_inc(diff_ok, 1)
                dve.wait_ge(diff_ok, 2 * i + m + 1)
                dve.tensor_scalar(sdiff[m][:, :, :], sdiff[m][:, :, :], -88.0, None,
                                  ALU.max).then_inc(clamp_ok, 1)

            normalise(0)
            normalise(1)
            for t in range(FIRST, PAIRS - 2):
                embedded(t)
            maximum(0, 0)
            for t in range(PAIRS - 2, PAIRS):
                embedded(t)
            add_eps(2, TILES, slice(FIRST, PAIRS))
            invert1(2, slice(FIRST, PAIRS))
            dve.wait_ge(consts_in, CONSTS)
            dve.wait_ge(before_ok, 2)
            dve.tensor_copy(before_b[:, :], before[:, :]).then_inc(before_ok, 1)
            dve.wait_ge(eidx_ok, 11)
            for r in range(TOPK):
                dve.tensor_copy(token_of[:, 0, r, :], timg).then_inc(token_ok, 1)
            dve.memset(token_of[:, 1, :, PAIRS:TILES], 0.0).then_inc(token_ok, 1)
            dve.tensor_copy(token_of[:, 1, :, 0:PAIRS], ttok.unsqueeze(2).broadcast_to([128, TOPK, PAIRS]),
                            ).then_inc(token_ok, 1)
            dve.wait_ge(token_ok, 4)
            dve.tensor_scalar(rev_e[:, :], eidx, -0.5 / E, 0.5, ALU.mult, ALU.add).then_inc(rev_ok, 1)
            dve.tensor_copy(pidx_b[:, :], pidx).then_inc(token_ok, 1)
            dve.tensor_scalar(npad_row[:, :], pad_row, -1.0, None, ALU.mult).then_inc(pad_ok, 1)


            def values(i, m):
                dve.wait_ge(v_done, 2 * i + m + 1)
                dve.tensor_tensor(
                    xtv[m][0:N, :, N:XW - 1], bank[2 + m][0:N, 0:D].rearrange("p (h d) -> p h d", h=H),
                    vb[0:N, :].rearrange("p (h d) -> p h d", h=H), ALU.add).then_inc(vx_ok, 1)

            def column_sums(i, m):
                dve.wait_ge(xtv_ok, 2 * i + m + 1)
                settled(dve)
                dve.tensor_reduce(csum[:, bass.ds((2 * i + m) * H, H)], xtv[m][0:N, :, 0:N],
                                  AX.X, ALU.add).then_inc(csum_ok, 1)

            def attention(i, first, norm):
                if not first:
                    maximum(i, 0)
                values(i, 0)
                if not first:
                    column_sums(i - 1, 1)
                    dve.wait_ge(gram_done, 2 * i)
                values(i, 1)
                if norm:
                    normalise(i + 2)
                maximum(i, 1)
                column_sums(i, 0)

            dve.wait_ge(zero_ok, 2)
            attention(0, True, True)
            with dve.Fori(1, PAIRS - 2) as i:
                attention(i, False, True)
            attention(PAIRS - 2, False, False)
            attention(PAIRS - 1, False, False)
            column_sums(PAIRS - 1, 1)

            dve.wait_ge(csum_ok, B)
            dve.tensor_reduce(mx2[:, 0:1], csum[:, :], AX.X, ALU.max).then_inc(gmax_ok, 1)
            dve.wait_ge(w_ok, B)
            dve.tensor_reduce(mx2[:, 1:2], wall[0:N, :, VA - 1], AX.X, ALU.max).then_inc(gmax_ok, 1)
            dve.wait_ge(gmaxT_done, 1)
            dve.tensor_reduce(grow[0:1, 0:2], bank[2][0:1, 0:2 * N].rearrange("p (a n) -> p a n", a=2),
                              AX.X, ALU.max).then_inc(scale_step, 1)
            dve.wait_ge(scale_step, 1)
            dve.tensor_scalar(grow[0:1, 2:3], grow[0:1, 0:1], grow[0:1, 1:2], 1e-15, ALU.mult,
                              ALU.add).then_inc(scale_step, 1)
            dve.wait_ge(scale_step, 2)
            dve.reciprocal(grow[0:1, 3:4], grow[0:1, 2:3]).then_inc(gscale_ok, 1)
            dve.wait_ge(gbc_done, 1)
            dve.tensor_copy(cscale[:, :], bank[2][0:N, 256:257]).then_inc(cscale_ok, 1)
            dve.wait_ge(cscale_ok, 1)
            dve.wait_ge(g_ok, B)

            def start(j, c):
                dve.tensor_scalar(T[c][0:N, :, :], gall[:, bass.ds((4 * j + c) * HH, HH), :], cscale[:, 0:1], None,
                                  ALU.mult).then_inc(t_ok[c], 1)

            def middle(g, c):
                dve.wait_ge(qs_ok[c], g + 1)
                dve.scalar_tensor_tensor(Sm[c][0:N, :, :].rearrange("p h n -> p (h n)"),
                                         T[c][0:N, :, :].rearrange("p h n -> p (h n)"), 28.0 * KAPPA, P[c],
                                         ALU.mult, ALU.add).then_inc(sm_ok[c], 1)

            def close(g, c, dst, done):
                dve.wait_ge(p2_done[c], g + 1)
                dve.wait_ge(v_ok[c], g + 1)
                dve.scalar_tensor_tensor(dst[c][0:N, :, :].rearrange("p h n -> p (h n)"),
                                         V[c][:, :, :].rearrange("p h n -> p (h n)"), CV, P[c],
                                         ALU.mult, ALU.add).then_inc(done[c], 1)

            def context(j):
                dve.wait_ge(wv_done, j + 1)
                prod = bank[0][0:N, 0:2 * H * VA].rearrange("p (g v) -> p g v", v=VA)
                dve.tensor_scalar(den[:, :, :].rearrange("p m h -> p (m h)"), prod[:, :, VA - 1],
                                  -0.25 / KAPPA, 1e-8, ALU.mult, ALU.max).then_inc(den_ok, 1)
                dve.wait_ge(den_ok, j + 1)
                dve.reciprocal(rden[:, :, :], den[:, :, :]).then_inc(rden_ok, 1)
                dve.wait_ge(rden_ok, j + 1)
                dve.scalar_tensor_tensor(
                    ctxv[:, :, :].rearrange("p m (h d) -> p (m h) d", d=DH), prod[:, :, 0:DH], -0.25 / KAPPA,
                    rden[:, :, :].rearrange("p m h -> p (m h)").unsqueeze(2).broadcast_to([N, 2 * H, DH]),
                    ALU.mult, ALU.mult).then_inc(ctx_ok, 1)

            def residual(t, k, rows):
                dve.wait_ge(proj_done, t + 1)
                dve.tensor_tensor(hid[0:rows, t, :], JB[k][0:rows, 0:D], hid[0:rows, t, :],
                                  ALU.add).then_inc(h2_ok, 1)

            def residual_written(t):
                dve.wait_ge(h2_ok, t + 1)

            def statistics(t, k, rows):
                dve.bn_stats(stat2[0:rows, k, :], hid[0:rows, t, :]).then_inc(stat2_ok, 1)

            def statistics_written(t):
                dve.wait_ge(stat2_ok, t + 1)

            def variance(t, k, rows):
                dve.bn_aggr(mv2[0:rows, k, :], stat2[0:rows, k, :]).then_inc(mv2_ok, 1)
                dve.wait_ge(mv2_ok, t + 1)
                dve.tensor_scalar(std2[0:rows, k:k + 1], mv2[0:rows, k, 1:2], EPS, None, ALU.add).then_inc(eps2_ok, 1)

            def layer_norm(t, k, rows):
                dve.wait_ge(sqrt2_ok, t + 1)
                dve.reciprocal(rstd2[0:rows, k:k + 1], std2[0:rows, k:k + 1]).then_inc(rstd2_ok, 1)
                dve.wait_ge(rstd2_ok, t + 1)
                if k == 0:
                    dve.wait_ge(rows_out, rows_before(t))
                dve.tensor_scalar(x2[k][0:rows, :], hid[0:rows, t, :], mv2[0:rows, k, 0:1], rstd2[0:rows, k:k + 1],
                                  ALU.subtract, ALU.mult).then_inc(x2_ok, 1)

            def logits(t, k, rows):
                dve.wait_ge(logit_done, t + 1)
                dve.tensor_tensor(logit[0:rows, t, :], RB[k][0:rows, 256:256 + E], bgb[0:rows, :],
                                  ALU.add).then_inc(logit_ok, 1)

            def pair(j, tail, more):
                g0 = ITERS * j

                def middles(g):
                    for c in range(4):
                        middle(g, c)

                def closes(g, dst, done):
                    for c in range(4):
                        close(g, c, dst, done)

                if not tail:
                    with dve.Fori(0, ITERS - 1) as it:
                        middles(g0 + it)
                        closes(g0 + it, T, t_ok)
                else:
                    for it in range(ITERS - 1):
                        if it == 3:
                            residual_written(j - 1)
                        middles(g0 + it)
                        if it == 3:
                            statistics(j - 1, 0, 128)
                            statistics_written(j - 1)
                        closes(g0 + it, T, t_ok)
                        if it == 0:
                            context(j - 1)
                        if it == 2:
                            residual(j - 1, 0, 128)
                        if it == 3:
                            variance(j - 1, 0, 128)
                        if it == 4:
                            layer_norm(j - 1, 0, 128)
                middles(g0 + ITERS - 1)
                if more:
                    for c in range(4):
                        dve.wait_ge(sm_ok[c], g0 + ITERS)
                        start(j + 1, c)
                closes(g0 + ITERS - 1, Fin, fin_ok)
                if tail:
                    logits(j - 1, 0, 128)

            dve.wait_ge(hb_ok, 2)
            dve.wait_ge(tiles_zero, 16)
            for c in range(4):
                start(0, c)
            pair(0, False, True)
            with dve.Fori(1, PAIRS - 1) as j:
                pair(j, True, True)
            pair(PAIRS - 1, True, False)
            context(PAIRS - 1)

            def greatest(tiles, call):
                ts, n = slice(tiles[0], tiles[-1] + 1), len(tiles)
                for t in tiles:
                    dve.max(top[:, t, :], logit[:, t, :]).then_inc(top_ok, 1)
                dve.wait_ge(top_ok, tiles[-1] + 1)
                dve.tensor_tensor(key[:, ts, :], logit[:, ts, :], top[:, ts, 0:1].broadcast_to([128, n, E]),
                                  ALU.is_equal).then_inc(key_part, 1)
                dve.tensor_tensor(above[:, ts, :], logit[:, ts, :], top[:, ts, 1:2].broadcast_to([128, n, E]),
                                  ALU.is_ge).then_inc(key_part, 1)
                dve.wait_ge(key_part, 3 * call + 1)
                dve.tensor_tensor(key[:, ts, :], key[:, ts, :], rev_e[:, :].unsqueeze(1).broadcast_to([128, n, E]),
                                  ALU.add).then_inc(key_part, 1)
                dve.tensor_tensor(gk[:, 0, ts], top[:, ts, 1], top[:, ts, 0], ALU.subtract).then_inc(gdiff_ok, 1)
                dve.wait_ge(key_part, 3 * call + 3)
                dve.tensor_tensor(key[:, ts, :], key[:, ts, :], above[:, ts, :], ALU.mult).then_inc(key_ok, 1)
                dve.wait_ge(key_ok, call + 1)
                for t in tiles:
                    dve.max(key_top[:, t, :], key[:, t, :]).then_inc(key_top_ok, 1)
                dve.wait_ge(key_top_ok, tiles[-1] + 1)
                for rows, part in ((128, slice(ts.start, min(ts.stop, PAIRS))), (B, slice(PAIRS, ts.stop))):
                    m = part.stop - part.start
                    if m > 0:
                        dve.tensor_tensor(chosen[0:rows, :, part, :],
                                          key[0:rows, part, :].unsqueeze(1).broadcast_to([rows, TOPK, m, E]),
                                          key_top[0:rows, part, 0:TOPK].rearrange("p t r -> p r t").unsqueeze(3)
                                          .broadcast_to([rows, TOPK, m, E]), ALU.is_equal).then_inc(chosen_ok, 1)

            dve.wait_ge(logit_ok, PAIRS - 1)
            dve.wait_ge(rev_ok, 1)
            greatest(range(PAIRS - 1), 0)
            dve.memset(xe_l[DL_:DL_ + 1], 1.0).then_inc(xones_ok, 1)
            residual(PAIRS - 1, 0, 128)
            residual_written(PAIRS - 1)
            statistics(PAIRS - 1, 0, 128)
            statistics_written(PAIRS - 1)
            variance(PAIRS - 1, 0, 128)
            residual(PAIRS, 1, B)
            residual_written(PAIRS)
            statistics(PAIRS, 1, B)
            layer_norm(PAIRS - 1, 0, 128)
            statistics_written(PAIRS)
            variance(PAIRS, 1, B)
            layer_norm(PAIRS, 1, B)
            logits(PAIRS - 1, 0, 128)
            logits(PAIRS, 1, B)
            dve.wait_ge(logit_ok, TILES)
            greatest(range(PAIRS - 1, TILES), 1)
            dve.wait_ge(chosen_ok, CHOICES)
            chosen_g = chosen[:, :, :, :].rearrange("p r t e -> p (r t) e")
            with nc.allow_low_precision("a count of at most 18 is exact in bfloat16"):
                dve.tensor_reduce(count_b[:, :], chosen_g.rearrange("p g e -> p e g"), AX.X, ALU.add,
                                  ).then_inc(count_ok, 1)
            dve.tensor_copy(chosen_b[:, :, :], chosen_g).then_inc(chosen_ok, 1)
            dve.wait_ge(gexp_ok, 1)
            dve.tensor_scalar(gk[:, 0, :], gk[:, 1, :], 1.0, None, ALU.add).then_inc(gate_step, 1)
            dve.wait_ge(total_done, 1)
            dve.tensor_tensor(over[:, :, :], bank[2][:, 0:E].unsqueeze(2).broadcast_to([128, E, TILES]),
                              thr.unsqueeze(1).broadcast_to([128, E, TILES]), ALU.is_gt).then_inc(place_step, 1)
            dve.wait_ge(gate_step, 1)
            dve.reciprocal(gk[:, 2, :], gk[:, 0, :]).then_inc(gate_step, 1)
            dve.wait_ge(place_step, 1)
            dve.tensor_reduce(ntile[:, :], over[:, :, :], AX.X, ALU.add).then_inc(place_step, 1)
            dve.wait_ge(gate_step, 2)
            dve.tensor_tensor(gk[:, 3, :], gk[:, 1, :], gk[:, 2, :], ALU.mult).then_inc(gate_step, 1)
            dve.wait_ge(place_step, 2)
            dve.tensor_tensor(upto[:, :, :], ntile[:, :].unsqueeze(1).broadcast_to([128, E, E]), tri_e[:, :, :],
                              ALU.mult).then_inc(place_step, 1)
            dve.wait_ge(gate_step, 3)
            gates = gk[:, 2:4, :].rearrange("p r t -> p (r t)")
            dve.tensor_copy(gate_b[:, 0, :], gates).then_inc(gsplit_ok, 1)
            dve.wait_ge(place_step, 3)
            dve.tensor_reduce(tend[:, :], upto[:, :, :], AX.X, ALU.add).then_inc(place_step, 1)
            dve.wait_ge(gsplit_ok, 1)
            dve.tensor_tensor(gleft[:, 0, :], gates, gate_b[:, 0, :], ALU.subtract).then_inc(gsplit_ok, 1)
            dve.wait_ge(place_step, 4)
            dve.tensor_tensor(tstart[:, :], tend[:, :], ntile[:, :], ALU.subtract).then_inc(place_step, 1)
            dve.wait_ge(gsplit_ok, 2)
            dve.tensor_copy(gate_b[:, 1, :], gleft[:, 0, :]).then_inc(gsplit_ok, 1)
            dve.wait_ge(place_step, 5)
            dve.wait_ge(rank_done, 1)
            dve.scalar_tensor_tensor(place[:, :, :], tstart[:, :].unsqueeze(1).broadcast_to([128, G, E]), float(SLOTS),
                                     bank[1][:, 0:G * E].rearrange("p (g e) -> p g e", e=E), ALU.mult,
                                     ALU.add).then_inc(place_step, 1)
            dve.wait_ge(gsplit_ok, 3)
            dve.tensor_tensor(gleft[:, 1, :], gleft[:, 0, :], gate_b[:, 1, :], ALU.subtract).then_inc(gsplit_ok, 1)
            dve.wait_ge(place_step, 6)
            dve.tensor_tensor(place[:, :, :], place[:, :, :], chosen_g, ALU.mult).then_inc(place_step, 1)
            dve.wait_ge(gsplit_ok, 4)
            dve.tensor_copy(gate_b[:, 2, :], gleft[:, 1, :]).then_inc(gsplit_ok, 1)
            dve.wait_ge(place_step, 7)
            dve.tensor_reduce(slot[:, :], place[:, :, :], AX.X, ALU.add).then_inc(place_step, 1)
            dve.wait_ge(place_step, 8)
            dve.tensor_scalar(slot_j[:, :], slot[:, :], 1.0 / SLOTS, 63.5 / SLOTS, ALU.mult,
                              ALU.subtract).then_inc(slot_j_ok, 1)
            dve.wait_ge(slot_j_ok, 1)
            dve.tensor_scalar(slot_j[:, :], slot_j[:, :], 1.5 * 2.0 ** 23, None, ALU.add).then_inc(slot_j_ok, 1)
            dve.wait_ge(slot_j_ok, 2)
            dve.tensor_scalar(slot_j[:, :], slot_j[:, :], 1.5 * 2.0 ** 23, None, ALU.subtract).then_inc(slot_j_ok, 1)
            dve.wait_ge(slot_j_ok, 3)
            dve.tensor_tensor(in_j[:, :, :], slot_j[:, :].unsqueeze(2).broadcast_to([128, G, ST]),
                              tidx.unsqueeze(1).broadcast_to([128, G, ST]), ALU.is_equal).then_inc(in_j_ok, 1)
            dve.scalar_tensor_tensor(slot_p[:, :], slot_j[:, :], -float(SLOTS), slot[:, :], ALU.mult,
                                     ALU.add).then_inc(slot_p_ok, 1)
            dve.wait_ge(in_j_ok, 1)
            dve.tensor_tensor(val[:, :, 0, :], in_j[:, :, :],
                              token_of[:, 0].rearrange("p r t -> p (r t)").unsqueeze(2).broadcast_to([128, G, ST]),
                              ALU.mult).then_inc(ival_ok, 1)
            dve.wait_ge(slot_p_ok, 1)
            dve.wait_ge(token_ok, 5)
            for g in range(G):
                dve.tensor_scalar(in_p[:, g, :], pidx_b[:, :], slot_p[:, g:g + 1], None, ALU.is_equal,
                                  ).then_inc(in_p_ok, 1)
            dve.wait_ge(inv_done, 1)
            img = bank[2][:, 64:64 + ST]
            dve.tensor_copy(found[:, 1:TOK, :].rearrange("p a j -> p (a j)"), bank[2][:, 64 + ST:64 + TOK * ST],
                            ).then_inc(found_ok, 1)
            dve.wait_ge(found_ok, 1)
            dve.scalar_tensor_tensor(idx_get[:, :], img, float(N), found[:, 1, :], ALU.mult,
                                     ALU.add).then_inc(idx_ok, 1)
            dve.tensor_tensor(tcmp[:, :, :], tidx[0:1].unsqueeze(2).broadcast_to([1, ST, E]),
                              tend[0:1, :].unsqueeze(1).broadcast_to([1, ST, E]), ALU.is_ge).then_inc(texp_ok, 1)
            dve.wait_ge(texp_ok, 1)
            dve.tensor_reduce(texp[:, :], tcmp[:, :, :], AX.X, ALU.add).then_inc(texp_ok, 1)
            dve.wait_ge(texp_ok, 2)
            dve.tensor_scalar(texp_c[:, :], texp[:, :], float(E - 1), None, ALU.min).then_inc(texp_ok, 1)
            dve.wait_ge(texp_ok, 3)
            dve.tensor_copy(texp_i[:, :], texp_c[:, :]).then_inc(texpi_ok, 1)
            dve.wait_ge(pad_ok, 1)
            dve.tensor_scalar(row_add[:, :], found[:, 2, :], npad_row[:, 0:1], pad_row, ALU.mult,
                              ALU.add).then_inc(pad_ok, 1)
            dve.wait_ge(pad_ok, 2)
            dve.wait_ge(idx_ok, 1)
            dve.tensor_tensor(idx_add[:, :], row_add[:, :], idx_get[:, :], ALU.add).then_inc(idx_ok, 1)
            dve.wait_ge(inv_done, 2)
            dve.tensor_copy(found[:, TOK:VALS, :].rearrange("p a j -> p (a j)"), bank[1][:, 0:(VALS - TOK) * ST],
                            ).then_inc(found_ok, 1)
            dve.wait_ge(found_ok, 2)
            dve.tensor_tensor(gsum[:, :], found[:, 3, :], found[:, 4, :], ALU.add).then_inc(gslot_ok, 1)
            dve.wait_ge(gslot_ok, 1)
            dve.tensor_tensor(gslot[:, :], gsum[:, :], found[:, 5, :], ALU.add).then_inc(gslot_ok, 1)
            dve.wait_ge(gslot_ok, 2)
            dve.wait_ge(b2_in, 16)
            dve.wait_ge(texpi_ok, 1)

            def hidden_transposed(j):
                dve.wait_ge(hT_done, j + 1)
                for f in range(2):
                    dve.tensor_copy(hT[:, 3 * f:3 * f + 3, :].rearrange("p m n -> p (m n)"),
                                    HTP[:, f, 0:3 * SLOTS]).then_inc(hT_ok, 1)

            def outputs(j, p):
                dve.wait_ge(l2_done, j + 1)
                if not isinstance(j, int) or j:
                    dve.wait_ge(y_ok, j)
                e = dve.value_load(texp_i[0:1, bass.ds(j, 1)], min_val=0, max_val=E - 1)
                dve.tensor_tensor(ysum, YP[p][:, 0:D], b2t[:, bass.ds(e, 1), :].rearrange("p a d -> p (a d)"),
                                  ALU.add).then_inc(ysum_ok, 1)
                dve.wait_ge(ysum_ok, j + 1)
                if not isinstance(j, int) or j >= 2:
                    dve.wait_ge(add_out, 16 * (j - 1))
                dve.tensor_scalar(yout[p], ysum, gslot[:, bass.ds(j, 1)], None, ALU.mult).then_inc(y_ok, 1)

            hidden_transposed(0)
            hidden_transposed(1)
            outputs(0, 0)
            hidden_transposed(2)
            outputs(1, 1)
            with dve.Fori(1, ST // 2 - 1) as jj:
                for p in range(2):
                    hidden_transposed(2 * jj + p + 1)
                    outputs(2 * jj + p, p)
            hidden_transposed(ST - 1)
            outputs(ST - 2, 0)
            outputs(ST - 1, 1)

        @block.tensor
        def _(pe):
            def two(dst, st_h, st_l, mv_h, mv_l):
                pe.matmul(dst, st_h, mv_h, start=True, stop=False)
                return pe.matmul(dst, st_l, mv_l, start=False, stop=True)

            def keep_warm(n):
                for _ in range(n):
                    pe.matmul(bank[3][:, 384:512], ident[:, :], ident[:, :], start=True, stop=True)

            def embed(t):
                pe.wait_ge(patch_in[t], 16)
                if t >= 2:
                    pe.wait_ge(emb_free, t - 1)
                for k in range(KT):
                    last = pe.matmul(EMB[t % 2], patch[t][:, k, :], tokw[:, k, :], start=(k == 0), stop=(k == KT - 1))
                last.then_inc(emb_done, 1)

            pe.wait_ge(ident_ok, 1)
            keep_warm(10)
            pe.wait_ge(w_in, 16)
            for t in range(4):
                embed(t)
            pe.wait_ge(consts_in, CONSTS)
            pe.wait_ge(xncls_ok, 1)
            pe.transpose(bank[0][:, 0:B], xncls[:, 0:DH_], ident[0:B, 0:B])
            pe.transpose(bank[0][0:DL_, B:2 * B], xncls[:, DH_:D], ident[0:B, 0:B]).then_inc(clsT_done, 1)
            pe.wait_ge(clsT_ok, 2)

            def transpose_x(i):
                pe.wait_ge(xn_ok, i + 1)
                if not isinstance(i, int) or i:
                    pe.wait_ge(xT_ok, 2 * i)
                    pe.wait_ge(k_ok, 2 * i)
                pe.transpose(bank[0][:, 0:128], xn[:, 0:DH_], ident[:, :])
                pe.transpose(bank[0][0:DL_, 128:256], xn[:, DH_:D], ident[:, :]).then_inc(xnT_done, 1)

            def project_qk(i):
                pe.wait_ge(xT_ok, 2 * i + 2)
                if not isinstance(i, int) or i:
                    pe.wait_ge(q_ok, 2 * i)
                    pe.wait_ge(k_ok, 2 * i)
                xh, xl = (x[:, :, :].rearrange("p m n -> p (m n)") for x in (xT_h, xT_l))
                for f in range(4):
                    dst = bank[1][0:CH, 130 * f:130 * f + 130] if f < 3 else bank[0][0:CH, 256:386]
                    last = two(dst, wqkv_h[:, CH * f:CH * f + CH], wqkv_l[:, CH * f:CH * f + CH], xh, xl)
                last.then_inc(qk_done, 1)

            def project_v(i, m):
                if not isinstance(i, int) or i:
                    pe.wait_ge(vx_ok, 2 * i + m - 1)
                two(bank[2 + m][0:N, 0:D], xT_h[:, m, :], xT_l[:, m, :],
                    wqkv_h[:, 2 * D:3 * D], wqkv_l[:, 2 * D:3 * D]).then_inc(v_done, 1)

            def scores(i, s, m):
                if m == 0:
                    pe.wait_ge(q_ok, 2 * i + 2)
                    pe.wait_ge(kbd_ok, 2 * i + 2)
                if isinstance(i, int) and i == 0 and m == 1:
                    pe.wait_ge(emb_free, PAIRS)
                if not isinstance(i, int) or i:
                    pe.wait_ge(g_ok, 2 * i + m - 1)
                    pe.wait_ge(w_ok, 2 * i + m - 1)
                for f in range(2):
                    last = pe.matmul(sx[m][0:N, f, 0:HH * N], qT[s][:, f, m, :],
                                     kbd[s][:, f, m, :, :].rearrange("p h n -> p (h n)"), start=True, stop=True)
                last.then_inc(score_done, 1)

            def transposes(i, m):
                pe.wait_ge(exp_ok, 2 * i + m + 1)
                for h in range(H):
                    last = pe.transpose(sx[m][0:N, h // HH, N * (h % HH):N * (h % HH) + N], xexp[m][:, h, :],
                                        ident[0:N, 0:N])
                last.then_inc(xt_done, 1)

            def products(i, m):
                pe.wait_ge(xtv_ok, 2 * i + m + 1)
                pe.wait_ge(vx_ok, 2 * i + m + 1)
                for h in range(H):
                    last = pe.matmul(sx[m][0:N, h // HH, XW * (h % HH):XW * (h % HH) + XW],
                                     xtv[m][:, h, 0:N], xtv[m][:, h, :], start=True, stop=True)
                last.then_inc(gram_done, 1)

            def attention(i, s, first, more, more2):
                if not first:
                    scores(i, s, 0)
                    transposes(i - 1, 1)
                if more:
                    project_qk(i + 1)
                if not first:
                    products(i - 1, 1)
                transposes(i, 0)
                if more:
                    project_v(i + 1, 0)
                scores(i, s, 1)
                products(i, 0)
                if more:
                    project_v(i + 1, 1)
                if more2:
                    transpose_x(i + 2)

            transpose_x(0)
            project_qk(0)
            project_v(0, 0)
            project_v(0, 1)
            transpose_x(1)
            for t in range(4, PAIRS - 2):
                embed(t)
            pe.wait_ge(rows_zero, 5)
            pe.wait_ge(zero_ok, 2)
            scores(0, 0, 0)
            for t in range(PAIRS - 2, PAIRS):
                embed(t)
            attention(0, 0, True, True, True)
            with pe.Fori(0, PAIRS // 2 - 2) as ii:
                attention(2 * ii + 1, 1, False, True, True)
                attention(2 * ii + 2, 0, False, True, True)
            attention(PAIRS - 3, 1, False, True, True)
            attention(PAIRS - 2, 0, False, True, False)
            attention(PAIRS - 1, 1, False, False, False)
            transposes(PAIRS - 1, 1)
            products(PAIRS - 1, 1)

            keep_warm(7)
            pe.wait_ge(gmax_ok, 2)
            pe.wait_ge(kappa4_ok, 1)
            for a in range(2):
                last = pe.transpose(bank[2][0:1, a * N:a * N + N], mx2[:, a:a + 1], ident[0:N, 0:N])
            last.then_inc(gmaxT_done, 1)
            keep_warm(3)
            pe.wait_ge(gscale_ok, 1)
            pe.matmul(bank[2][0:N, 256:257], kappa4[:, :], grow[0:1, 3:4], start=True, stop=True).then_inc(gbc_done, 1)

            def square(g, c):
                pe.wait_ge(t_ok[c], g + 1)
                for h in range(HH):
                    last = pe.matmul(P[c][:, N * h:N * h + N], T[c][:, h, :], T[c][:, h, :], start=True, stop=True)
                last.then_inc(p1_done[c], 1)

            def product(g, c):
                pe.wait_ge(qs_ok[c], g + 1)
                pe.wait_ge(sm_ok[c], g + 1)
                for h in range(HH):
                    last = pe.matmul(P[c][:, N * h:N * h + N], Qs[c][:, h, :], Sm[c][:, h, :], start=True, stop=True)
                last.then_inc(p2_done[c], 1)

            def apply(j):
                for c in range(4):
                    pe.wait_ge(fin_ok[c], j + 1)
                    for h in range(HH):
                        n = HH * c + h
                        last = pe.matmul(bank[0][0:N, VA * n:VA * n + VA], Fin[c][:, h, :],
                                         wall[:, bass.ds(2 * H * j + n, 1), :].rearrange("p a v -> p (a v)"),
                                         start=True, stop=True)
                last.then_inc(wv_done, 1)

            def transpose_context(j):
                pe.wait_ge(ctx_ok, j + 1)
                for m in range(2):
                    pe.transpose(bank[1][:, N * m:N * m + N], ctxv[:, m, 0:DH_], ident[0:N, 0:N])
                    last = pe.transpose(bank[1][0:DL_, 130 + N * m:130 + N * m + N], ctxv[:, m, DH_:D],
                                        ident[0:N, 0:N])
                last.then_inc(ctxT_done, 1)

            def project_context(j):
                pe.wait_ge(cT_ok, 4 * j + 4)
                two(bank[2][:, 0:D], cT_h[:, :, :].rearrange("p m n -> p (m n)"),
                    cT_l[:, :, :].rearrange("p m n -> p (m n)"), wp_h[:, :], wp_l[:, :]).then_inc(proj_done, 1)

            def transpose_x2(t, k, rows):
                pe.wait_ge(x2_ok, t + 1)
                pe.transpose(RB[k][:, 0:rows], x2[k][0:rows, 0:DH_], ident[0:rows, 0:rows])
                pe.transpose(RB[k][0:DL_, 128:128 + rows], x2[k][0:rows, DH_:D],
                             ident[0:rows, 0:rows]).then_inc(x2T_done, 1)

            def router(t, k, rows):
                pe.wait_ge(x2T_ok, 2 * t + 2)
                two(RB[k][0:rows, 256:256 + E], x2T_h[k][:, 0:rows], x2T_l[k][:, 0:rows],
                    wg_h[:, :], wg_l[:, :]).then_inc(logit_done, 1)

            keep_warm(2)
            pe.wait_ge(tiles_zero, 16)
            with pe.Fori(0, ITERS) as g:
                for c in range(4):
                    square(g, c)
                for c in range(4):
                    product(g, c)
            with pe.Fori(1, PAIRS) as j:
                for it in range(ITERS):
                    for c in range(4):
                        if it == 0:
                            pe.wait_ge(fin_ok[c], j)
                        square(ITERS * j + it, c)
                    if it == 0:
                        apply(j - 1)
                    if it == 1:
                        transpose_context(j - 1)
                    if it == 2:
                        project_context(j - 1)
                    if it == 5:
                        transpose_x2(j - 1, 0, 128)
                    for c in range(4):
                        product(ITERS * j + it, c)
                router(j - 1, 0, 128)
            apply(PAIRS - 1)
            transpose_context(PAIRS - 1)
            project_context(PAIRS - 1)
            two(JB[1][0:B, 0:D], cTc_h[:, :], cTc_l[:, :], wp_h[:, :], wp_l[:, :]).then_inc(proj_done, 1)
            transpose_x2(PAIRS - 1, 0, 128)
            transpose_x2(PAIRS, 1, B)
            router(PAIRS - 1, 0, 128)
            router(PAIRS, 1, B)

            pe.wait_ge(count_ok, 1)
            pe.matmul(bank[2][:, 0:E], ones_b[:, :], count_b[:, :], start=True, stop=True).then_inc(total_done, 1)
            pe.wait_ge(chosen_ok, CHOICES + 1)
            rank = bank[1][:, 0:G * E].rearrange("p (g e) -> p g e", e=E)
            pe.matmul(rank, before_b[:, :], chosen_b[:, :, :], start=True, stop=False)
            for g in range(G - 1):
                last = pe.matmul(rank[:, g + 1:G, :], ones_b[:, :],
                                 chosen_b[:, g:g + 1, :].broadcast_to([128, G - 1 - g, E]),
                                 start=False, stop=(g == G - 2))
            last.then_inc(rank_done, 1)

            def by_slot(out_, parts):
                for g in range(G):
                    rows = 128 if g % TILES < PAIRS else B
                    pe.wait_ge(in_p_ok, g + 1)
                    last = pe.matmul(out_, in_p[0:rows, g, :],
                                     val[0:rows, g, parts, :].rearrange("p a j -> p (a j)"),
                                     start=(g == 0), stop=(g == G - 1))
                last.then_inc(inv_done, 1)

            pe.wait_ge(ival_ok, 1)
            pe.wait_ge(oval_ok, 1)
            pe.wait_ge(tval_ok, 1)
            by_slot(bank[2][:, 64:64 + TOK * ST], slice(0, TOK))
            pe.wait_ge(tval_ok, 4)
            by_slot(bank[1][:, 0:(VALS - TOK) * ST], slice(TOK, VALS))

            def expert_of(j):
                return pe.value_load(texp_i[0:1, bass.ds(j, 1)], min_val=0, max_val=E - 1)

            def transpose_tokens(j, p, nth):
                pe.wait_ge(get_in[p], 16 * (nth + 1))
                if not isinstance(j, int) or j:
                    pe.wait_ge(xe_ok, 2 * j)
                pe.transpose(XP[:, 0:SLOTS], xin[p][:, 0:DH_], ident[:, :])
                pe.transpose(XP[0:DL_, SLOTS:2 * SLOTS], xin[p][:, DH_:D], ident[:, :]).then_inc(xe_done, 1)

            def first_layer(j, e):
                pe.wait_ge(xe_ok, 2 * j + 2)
                for f in range(2):
                    units = slice(HH2 * f, HH2 * f + HH2)
                    last = two(HP[:, f, 0:HH2], xe_h, xe_l, w1h[:, bass.ds(e, 1), units].rearrange("p a n -> p (a n)"),
                               w1l[:, bass.ds(e, 1), units].rearrange("p a n -> p (a n)"))
                last.then_inc(l1_done, 1)

            def transpose_hidden(j):
                pe.wait_ge(h_ok, 2 * j + 2)
                for mt in range(MT):
                    last = pe.transpose(HTP[:, mt // 3, SLOTS * (mt % 3):SLOTS * (mt % 3) + SLOTS],
                                        hs[:, SLOTS * mt:SLOTS * mt + SLOTS], ident[:, :])
                last.then_inc(hT_done, 1)

            def second_layer(j, p, e):
                if not isinstance(j, int) or j >= 2:
                    pe.wait_ge(y_ok, j - 1)
                for mt in range(MT):
                    if mt % 3 == 0:
                        pe.wait_ge(hT_ok, 2 * j + 1 + mt // 3)
                    last = pe.matmul(YP[p][:, 0:D], hT[:, mt, :],
                                     w2a[:, bass.ds(e, 1), D * mt:D * mt + D].rearrange("p a n -> p (a n)"),
                                     start=(mt == 0), stop=(mt == MT - 1))
                last.then_inc(l2_done, 1)

            keep_warm(5)
            pe.wait_ge(texpi_ok, 1)
            pe.wait_ge(xones_ok, 1)
            pe.wait_ge(w1_in, 48)
            pe.wait_ge(w2_in, 16)
            e = expert_of(0)
            transpose_tokens(0, 0, 0)
            first_layer(0, e)
            transpose_tokens(1, 1, 0)

            pe.wait_ge(found_ok, 2)

            def tiles(jj):
                e = expert_of(XINS * jj)
                for p in range(XINS):
                    j = XINS * jj + p
                    transpose_hidden(j)
                    following = None
                    if not isinstance(j, int) or j + 1 < ST:
                        following = expert_of(j + 1)
                        first_layer(j + 1, following)
                    if not isinstance(j, int) or j + 2 < ST:
                        transpose_tokens(j + 2, (p + 2) % XINS, jj + (p + 2) // XINS)
                    second_layer(j, p % 2, e)
                    e = following

            tiles(0)
            with pe.Fori(1, ST // XINS - 1) as jj:
                tiles(jj)
            tiles(ST // XINS - 1)


def kernel(x, cls_tok, L0_tok_W, L0_tok_b, L0_attn_qkv_w, L0_attn_qkv_b, L0_attn_proj_w, L0_attn_proj_b,
           L0_ffn_Wg, L0_ffn_bg, L0_ffn_W1, L0_ffn_b1, L0_ffn_W2, L0_ffn_b2):
    import numpy as np
    import concourse.bacc as bacc
    from concourse.bass_utils import run_bass_kernel_spmd

    def lay(a):
        return np.ascontiguousarray(a)

    side = IMG // PATCH
    p = np.asarray(x).reshape(PAIRS, 2, C_IN, side, PATCH, side, PATCH)
    p = p.transpose(0, 4, 6, 2, 1, 3, 5).reshape(PAIRS, KT, 128, 128).transpose(0, 2, 1, 3)
    arrays = {
        "xp": lay(p),
        "cls_tok": lay(cls_tok),
        "tok_w": lay(np.asarray(L0_tok_W).T.reshape(KT, 128, D).transpose(1, 0, 2)),
        "tok_b": lay(L0_tok_b),
        "qkv_w": lay(L0_attn_qkv_w),
        "qk_b": lay(np.asarray(L0_attn_qkv_b)[0:2 * D].reshape(4, CH).T),
        "v_b": lay(np.asarray(L0_attn_qkv_b)[2 * D:3 * D]),
        "proj_w": lay(L0_attn_proj_w),
        "proj_b": lay(L0_attn_proj_b),
        "wg": lay(L0_ffn_Wg),
        "bg": lay(L0_ffn_bg),
        "w1": lay(L0_ffn_W1),
        "b1": lay(L0_ffn_b1),
        "w2": lay(np.asarray(L0_ffn_W2).reshape(E, MT, 128, D).transpose(2, 0, 1, 3).reshape(128, E, MT * D)),
        "b2": lay(L0_ffn_b2),
    }
    nc = bacc.Bacc("TRN2", target_bir_lowering=False, num_devices=1)
    args = [nc.dram_tensor(n, a.shape, mybir.dt.from_np(a.dtype), kind="ExternalInput").ap()
            for n, a in arrays.items()]
    args.append(nc.dram_tensor("out", (NTOK + SLOTS, D), F32, kind="ExternalOutput").ap())
    build(nc, *args)
    return run_bass_kernel_spmd(nc, [arrays], core_ids=[0]).results[0]["out"][0:NTOK].reshape(B, N, D)
```
